# Optimizing a Trainium2 kernel written in Bass

```python
import numpy as np
import jax
import jax.numpy as jnp

def _softmax(x, axis=-1):
    return jax.nn.softmax(x, axis=axis)

def _gelu(x):
    return jax.nn.gelu(x, approximate=True)

def _silu(x):
    return jax.nn.silu(x)

def _sigmoid(x):
    return jax.nn.sigmoid(x)

def _layernorm(x, axis=-1, eps=1e-05):
    m = jnp.mean(x, axis=axis, keepdims=True)
    v = jnp.var(x, axis=axis, keepdims=True)
    return (x - m) / jnp.sqrt(v + eps)

def _scatter_add(tgt, idx, src, axis=0):
    return tgt.at[idx].add(src)

def _segment_sum(src, seg, n):
    return jax.ops.segment_sum(src, seg, n)
kernel_name = 'mk_gnn_resnorm_d4_gnn_r64_e8f8da'

def setup_inputs(seed: int=0):
    np.random.seed(seed)
    _w = jnp.asarray

    def _rec_inputs():
        import jax
        import jax.numpy as jnp
        _gk = jax.random.key(seed)
        x = -0.0001006 + 1 * jax.random.normal(jax.random.fold_in(_gk, 1), (100000, 96), jnp.float32)
        src = jax.random.randint(jax.random.fold_in(_gk, 2), (25000,), 0, 100000, jnp.int32)
        dst = jnp.minimum((100000 * jax.random.uniform(jax.random.fold_in(_gk, 3), (25000,)) ** 2.0).astype(jnp.int32), 99999)
        _o = jnp.argsort(dst, stable=True)
        src = src[_o]
        dst = dst[_o]
        edge_attr_4 = 0.000714719 + 1.00021 * jax.random.normal(jax.random.fold_in(_gk, 12), (25000, 4), jnp.float32)
        return (x, src, dst, edge_attr_4)
    x, src, dst, edge_attr_4 = _rec_inputs()

    def _L0_gnn_setup():
        import jax, jax.numpy as jnp
        import numpy as np
        N_NODES = 50000
        N_EDGES = 12500
        D_IN = 96
        D_HID = 96
        D_OUT = 96

        def gcn_conv(x, W, b, src, dst, num_nodes):
            deg = jax.ops.segment_sum(jnp.ones_like(dst, dtype=x.dtype), dst, num_segments=num_nodes)
            dinv = jnp.where(deg > 0, jax.lax.rsqrt(deg), 0.0)
            norm = dinv[src] * dinv[dst]
            h = x @ W
            msg = h[src] * norm[:, None]
            out = jax.ops.segment_sum(msg, dst, num_segments=num_nodes)
            return out + b
        key = jax.random.key(seed)
        ks = jax.random.split(key, 8)
        x = jax.random.normal(ks[0], (N_NODES, D_IN), dtype=jnp.float32)
        edge_index = jax.random.randint(ks[1], (2, N_EDGES), 0, N_NODES, dtype=jnp.int64)
        s_in = 1.0 / np.sqrt(D_IN)
        s_h = 1.0 / np.sqrt(D_HID)
        W1 = jax.random.normal(ks[2], (D_IN, D_HID), dtype=jnp.float32) * s_in
        b1 = jnp.zeros((D_HID,), dtype=jnp.float32)
        W2 = jax.random.normal(ks[3], (D_HID, D_HID), dtype=jnp.float32) * s_h
        b2 = jnp.zeros((D_HID,), dtype=jnp.float32)
        W3 = jax.random.normal(ks[4], (D_HID, D_OUT), dtype=jnp.float32) * s_h
        b3 = jnp.zeros((D_OUT,), dtype=jnp.float32)
        return {'x': x, 'edge_index': edge_index, 'W1': W1, 'b1': b1, 'W2': W2, 'b2': b2, 'W3': W3, 'b3': b3}
    _L0_gnn_all = _L0_gnn_setup()
    _L0_gnn_in = {k: v for k, v in _L0_gnn_all.items() if k in ('W1', 'b1', 'W2', 'b2', 'W3', 'b3')}
    del _L0_gnn_all

    def _L1_gnn_setup():
        import jax, jax.numpy as jnp
        import numpy as np
        N_NODES = 50000
        N_EDGES = 12500
        D_IN = 96
        D_OUT = 96
        NEG_SLOPE = 0.2
        key = jax.random.key(seed)
        k1, k2, k3, k4, k5 = jax.random.split(key, 5)
        x = jax.random.normal(k1, (N_NODES, D_IN), dtype=jnp.float32)
        W = jax.random.normal(k2, (D_IN, D_OUT), dtype=jnp.float32) * (1.0 / np.sqrt(D_IN))
        att_src = jax.random.normal(k3, (D_OUT,), dtype=jnp.float32) * 0.1
        att_dst = jax.random.normal(k4, (D_OUT,), dtype=jnp.float32) * 0.1
        bias = jnp.zeros((D_OUT,), dtype=jnp.float32)
        edge_index = jax.random.randint(k5, (2, N_EDGES), 0, N_NODES, dtype=jnp.int64)
        return {'x': x, 'W': W, 'att_src': att_src, 'att_dst': att_dst, 'bias': bias, 'edge_index': edge_index}
    _L1_gnn_all = _L1_gnn_setup()
    _L1_gnn_in = {k: v for k, v in _L1_gnn_all.items() if k in ('W', 'att_src', 'att_dst', 'bias')}
    del _L1_gnn_all

    def _L2_gnn_setup():
        import jax, jax.numpy as jnp
        import numpy as np
        EPS = 1e-05

        def _mlp(h, W, b, gamma, beta):
            h = jax.nn.relu(h @ W + b)
            mu = jnp.mean(h, axis=0)
            var = jnp.mean(jnp.square(h - mu), axis=0)
            return gamma * (h - mu) * jax.lax.rsqrt(var + EPS) + beta
        key = jax.random.key(seed)
        ks = jax.random.split(key, 10)
        N, E, C_in, C_out, E_dim = (50000, 12500, 96, 96, 4)
        x = jax.random.normal(ks[0], (N, C_in), dtype=jnp.float32)
        edge_index = jax.random.randint(ks[1], (2, E), 0, N, dtype=jnp.int64)
        edge_attr = jax.random.normal(ks[2], (E, E_dim), dtype=jnp.float32)
        s = lambda fan_in: 1.0 / np.sqrt(fan_in)
        W_node = jax.random.uniform(ks[3], (C_in, C_out), jnp.float32, -s(C_in), s(C_in))
        b_node = jnp.zeros((C_out,), jnp.float32)
        g_node = jnp.ones((C_out,), jnp.float32)
        beta_node = jnp.zeros((C_out,), jnp.float32)
        W_edge = jax.random.uniform(ks[4], (E_dim, C_out), jnp.float32, -s(E_dim), s(E_dim))
        b_edge = jnp.zeros((C_out,), jnp.float32)
        g_edge = jnp.ones((C_out,), jnp.float32)
        beta_edge = jnp.zeros((C_out,), jnp.float32)
        M_in = 2 * C_in + C_out
        W_msg = jax.random.uniform(ks[5], (M_in, C_out), jnp.float32, -s(M_in), s(M_in))
        b_msg = jnp.zeros((C_out,), jnp.float32)
        g_msg = jnp.ones((C_out,), jnp.float32)
        beta_msg = jnp.zeros((C_out,), jnp.float32)
        return dict(x=x, edge_index=edge_index, edge_attr=edge_attr, W_node=W_node, b_node=b_node, g_node=g_node, beta_node=beta_node, W_edge=W_edge, b_edge=b_edge, g_edge=g_edge, beta_edge=beta_edge, W_msg=W_msg, b_msg=b_msg, g_msg=g_msg, beta_msg=beta_msg)
    _L2_gnn_all = _L2_gnn_setup()
    _L2_gnn_in = {k: v for k, v in _L2_gnn_all.items() if k in ('W_node', 'b_node', 'g_node', 'beta_node', 'W_edge', 'b_edge', 'g_edge', 'beta_edge', 'W_msg', 'b_msg', 'g_msg', 'beta_msg')}
    del _L2_gnn_all

    def _L3_gnn_setup():
        import jax, jax.numpy as jnp
        import numpy as np
        N_NODES = 50000
        N_EDGES = 12500
        D_FEAT = 96
        L = 0.5
        key = jax.random.key(seed)
        k1, k2, k3 = jax.random.split(key, 3)
        h = jax.random.normal(k1, (N_NODES, D_FEAT), dtype=jnp.float32)
        src = jax.random.randint(k2, (N_EDGES,), 0, N_NODES, dtype=jnp.int64)
        dst = jax.random.randint(k3, (N_EDGES,), 0, N_NODES, dtype=jnp.int64)
        return {'h': h, 'src': src, 'dst': dst}
    _L3_gnn_all = _L3_gnn_setup()
    _L3_gnn_in = {k: v for k, v in _L3_gnn_all.items() if k in ()}
    del _L3_gnn_all
    return {'x': x, 'src': src, 'dst': dst, 'edge_attr_4': edge_attr_4, 'L0_gnn_W1': _L0_gnn_in['W1'], 'L0_gnn_b1': _L0_gnn_in['b1'], 'L0_gnn_W2': _L0_gnn_in['W2'], 'L0_gnn_b2': _L0_gnn_in['b2'], 'L0_gnn_W3': _L0_gnn_in['W3'], 'L0_gnn_b3': _L0_gnn_in['b3'], 'L1_gnn_W': _L1_gnn_in['W'], 'L1_gnn_att_src': _L1_gnn_in['att_src'], 'L1_gnn_att_dst': _L1_gnn_in['att_dst'], 'L1_gnn_bias': _L1_gnn_in['bias'], 'L2_gnn_W_node': _L2_gnn_in['W_node'], 'L2_gnn_b_node': _L2_gnn_in['b_node'], 'L2_gnn_g_node': _L2_gnn_in['g_node'], 'L2_gnn_beta_node': _L2_gnn_in['beta_node'], 'L2_gnn_W_edge': _L2_gnn_in['W_edge'], 'L2_gnn_b_edge': _L2_gnn_in['b_edge'], 'L2_gnn_g_edge': _L2_gnn_in['g_edge'], 'L2_gnn_beta_edge': _L2_gnn_in['beta_edge'], 'L2_gnn_W_msg': _L2_gnn_in['W_msg'], 'L2_gnn_b_msg': _L2_gnn_in['b_msg'], 'L2_gnn_g_msg': _L2_gnn_in['g_msg'], 'L2_gnn_beta_msg': _L2_gnn_in['beta_msg']}

def reference(x, src, dst, edge_attr_4, L0_gnn_W1, L0_gnn_b1, L0_gnn_W2, L0_gnn_b2, L0_gnn_W3, L0_gnn_b3, L1_gnn_W, L1_gnn_att_src, L1_gnn_att_dst, L1_gnn_bias, L2_gnn_W_node, L2_gnn_b_node, L2_gnn_g_node, L2_gnn_beta_node, L2_gnn_W_edge, L2_gnn_b_edge, L2_gnn_g_edge, L2_gnn_beta_edge, L2_gnn_W_msg, L2_gnn_b_msg, L2_gnn_g_msg, L2_gnn_beta_msg):
    import jax
    import jax.numpy as jnp

    def _L0_gnn_ref(x, edge_index, W1, b1, W2, b2, W3, b3):
        import jax, jax.numpy as jnp
        import numpy as np
        N_NODES = 50000
        N_EDGES = 12500
        D_IN = 96
        D_HID = 96
        D_OUT = 96

        def gcn_conv(x, W, b, src, dst, num_nodes):
            deg = jax.ops.segment_sum(jnp.ones_like(dst, dtype=x.dtype), dst, num_segments=num_nodes)
            dinv = jnp.where(deg > 0, jax.lax.rsqrt(deg), 0.0)
            norm = dinv[src] * dinv[dst]
            h = x @ W
            msg = h[src] * norm[:, None]
            out = jax.ops.segment_sum(msg, dst, num_segments=num_nodes)
            return out + b
        num_nodes = x.shape[0]
        loop = jnp.arange(num_nodes, dtype=edge_index.dtype)
        src = jnp.concatenate([edge_index[0], loop])
        dst = jnp.concatenate([edge_index[1], loop])
        h = gcn_conv(x, W1, b1, src, dst, num_nodes)
        h = jax.nn.relu(h)
        h = gcn_conv(h, W2, b2, src, dst, num_nodes)
        h = jax.nn.relu(h)
        return gcn_conv(h, W3, b3, src, dst, num_nodes)

    def _L1_gnn_ref(x, W, att_src, att_dst, bias, edge_index):
        import jax, jax.numpy as jnp
        import numpy as np
        N_NODES = 50000
        N_EDGES = 12500
        D_IN = 96
        D_OUT = 96
        NEG_SLOPE = 0.2
        N = x.shape[0]
        h = x @ W
        loops = jnp.arange(N, dtype=edge_index.dtype)
        src = jnp.concatenate([edge_index[0], loops])
        dst = jnp.concatenate([edge_index[1], loops])
        a_src = h @ att_src
        a_dst = h @ att_dst
        e = jax.nn.leaky_relu(a_src[src] + a_dst[dst], NEG_SLOPE)
        m = jax.ops.segment_max(e, dst, num_segments=N)
        e = jnp.exp(e - m[dst])
        denom = jax.ops.segment_sum(e, dst, num_segments=N)
        alpha = e / (denom[dst] + 1e-16)
        out = jax.ops.segment_sum(h[src] * alpha[:, None], dst, num_segments=N)
        return jnp.tanh(out + bias)

    def _L2_gnn_ref(x, edge_index, edge_attr, W_node, b_node, g_node, beta_node, W_edge, b_edge, g_edge, beta_edge, W_msg, b_msg, g_msg, beta_msg):
        import jax, jax.numpy as jnp
        import numpy as np
        EPS = 1e-05

        def _mlp(h, W, b, gamma, beta):
            h = jax.nn.relu(h @ W + b)
            mu = jnp.mean(h, axis=0)
            var = jnp.mean(jnp.square(h - mu), axis=0)
            return gamma * (h - mu) * jax.lax.rsqrt(var + EPS) + beta
        node_feat = _mlp(x, W_node, b_node, g_node, beta_node)
        edge_feat = _mlp(edge_attr, W_edge, b_edge, g_edge, beta_edge)
        row, col = (edge_index[0], edge_index[1])
        message = jnp.concatenate([x[row], x[col], edge_feat], axis=1)
        message = _mlp(message, W_msg, b_msg, g_msg, beta_msg)
        agg = jax.ops.segment_sum(message, col, num_segments=node_feat.shape[0])
        return agg + node_feat

    def _L3_gnn_ref(h, src, dst):
        import jax, jax.numpy as jnp
        import numpy as np
        N_NODES = 50000
        N_EDGES = 12500
        D_FEAT = 96
        L = 0.5
        N = h.shape[0]
        deg = jax.ops.segment_sum(jnp.ones_like(dst, dtype=h.dtype), dst, num_segments=N)
        inv_deg = (1.0 / jnp.maximum(deg, 1.0))[:, None]

        def mean_agg(x):
            msg_sum = jax.ops.segment_sum(x[src], dst, num_segments=N)
            return msg_sum * inv_deg
        neigh1 = mean_agg(h)
        neigh2 = mean_agg(neigh1)
        return L * neigh1 + (1.0 - L) * neigh2
    edge_index = jnp.stack([src, dst])
    x = _layernorm(x + _L0_gnn_ref(x, edge_index, L0_gnn_W1, L0_gnn_b1, L0_gnn_W2, L0_gnn_b2, L0_gnn_W3, L0_gnn_b3), axis=-1)
    x = _layernorm(x + _L1_gnn_ref(x, L1_gnn_W, L1_gnn_att_src, L1_gnn_att_dst, L1_gnn_bias, edge_index), axis=-1)
    x = _layernorm(x + _L2_gnn_ref(x, edge_index, edge_attr_4, L2_gnn_W_node, L2_gnn_b_node, L2_gnn_g_node, L2_gnn_beta_node, L2_gnn_W_edge, L2_gnn_b_edge, L2_gnn_g_edge, L2_gnn_beta_edge, L2_gnn_W_msg, L2_gnn_b_msg, L2_gnn_g_msg, L2_gnn_beta_msg), axis=-1)
    x = _layernorm(x + _L3_gnn_ref(x, src, dst), axis=-1)
    return x

_drawn_inputs = setup_inputs


def setup_inputs(seed=0):
    import zlib

    import numpy as np

    out = dict(_drawn_inputs(seed))
    spreads = {'L0_gnn_b1': (0.0, 0.1),
     'L0_gnn_b2': (0.0, 0.1),
     'L0_gnn_b3': (0.0, 0.1),
     'L1_gnn_bias': (0.0, 0.1),
     'L2_gnn_b_node': (0.0, 0.1),
     'L2_gnn_g_node': (1.0, 0.2),
     'L2_gnn_beta_node': (0.0, 0.1),
     'L2_gnn_b_edge': (0.0, 0.342),
     'L2_gnn_g_edge': (1.0, 0.546),
     'L2_gnn_beta_edge': (0.0, 0.8),
     'L2_gnn_b_msg': (0.0, 0.342),
     'L2_gnn_g_msg': (1.0, 0.2),
     'L2_gnn_beta_msg': (0.0, 0.306)}
    factors = {'L1_gnn_att_dst': 3.152}
    for name, (base, spread) in spreads.items():
        noise = np.random.default_rng([zlib.crc32(name.encode()), seed]).standard_normal(out[name].shape)
        drawn = base * np.exp(spread * noise) if base else spread * noise
        out[name] = jnp.asarray(drawn.astype(out[name].dtype))
    for name, factor in factors.items():
        out[name] = (out[name] * factor).astype(out[name].dtype)
    return out
```

```python
from contextlib import ExitStack

import concourse.bass as bass
from concourse import mybir

ALU = mybir.AluOpType
ACT = mybir.ActivationFunctionType
F32 = mybir.dt.float32
U8 = mybir.dt.uint8
I32 = mybir.dt.int32
AX_X = mybir.AxisListType.X
ds = bass.ds

P = 128
N, D = 100000, 96
E, DE = 25000, 4
ET = -(-E // P)
EP = ET * P
TG = 4
GW = TG * P
NJ = 7
NI = ET // (TG * NJ)
NG = NI * NJ
TI = TG * NJ
HALF = 4
NR, RW = 80, 25
CH = 5
CR = RW // CH
CW = NR * CR
TURN = NR * RW
ND = N // TURN
NL = -(-EP // TURN)
LR = NL * TURN
BIG = 1.0e30
EPS = 1e-5
SLOPE = 0.2
ENGINES = 5
START = 1
RB = [(0, P), (P, ET - P)]
assert ET == TI * NI and N == ND * TURN
(B_1, B_2, B_3, B_G, B_N, B_3C, G_N, BE_N, G_E, BE_E, G_M, BE_M, A_N, S_N, A_E, S_E, A_M, S_M,
 C_N, B_M, NCOL) = range(21)


def build(nc, a):
    with ExitStack() as ctx:
        def sb(name, shape, dt=F32):
            return ctx.enter_context(nc.sbuf_tensor(name, shape, dt))

        def dram(name, shape, dt=F32):
            return nc.dram_tensor(name, shape, dt, kind="Internal").ap()

        sems = {}

        def sem(name):
            if name not in sems:
                sems[name] = ctx.enter_context(nc.semaphore(name))
            return sems[name]

        XS = dram("XS", (LR, D))
        XD = dram("XD", (EP, D))
        T = [None] + [dram(f"T{k}", (EP + LR, D)) for k in (1, 2, 3, 4, 5)]
        TN = dram("TN", (EP + P, D))
        GX = dram("GX", (EP, D))
        FR = dram("FR", (EP, D))
        TAB = dram("TAB", (N, 2))
        ACTV = dram("ACTV", (ND, TURN))
        X2T = dram("X2T", (ND, D, TURN))
        X2L = dram("X2L", (NL, D, TURN))
        NDT = dram("NDT", (NG, D, 2, GW))
        AGG = dram("AGG", (NG, D, GW))
        LID = dram("LID", (EP,), U8)
        LINE = dram("LINE", (3, EP))
        CONT = dram("CONT", (ET,))

        ps = ctx.enter_context(nc.psum_tensor("ps", [P, 8, 512], F32))
        ZB, OB, DB = 0, 2, 3

        ident = sb("ident", [P, P])
        cent = sb("cent", [D, D])
        avg = sb("avg", [D, D])
        W = {k: sb(f"W{k}", [D + 1, D]) for k in "123GI"}
        WN = sb("WN", [D + 1, D])
        WE = sb("WE", [DE + 2, D])
        WM = sb("WM", [D, 3, D])
        WM3 = sb("WM3", [D, D])
        W3C = sb("W3C", [D, D])
        AN = sb("AN", [D, D])
        AM = sb("AM", [D, D])
        col = sb("col", [D, NCOL])
        wt = sb("wt", [D, 2, D])
        att = sb("att", [D, 2])
        attB = sb("attB", [D, 2, P])
        uv = sb("uv", [P, 2, D])
        epsc = sb("epsc", [P, 2])
        ones = sb("ones", [P, P])
        zero = sb("zero", [P, 800])
        onesr = sb("onesr", [P, 2, P])
        nb2 = sb("nb2", [2, D])
        mb2 = sb("mb2", [2, D])
        sh2 = sb("sh2", [2, D])

        src_i = sb("src_i", [P, ET], I32)
        dst_i = sb("dst_i", [P, ET], I32)
        own = sb("own", [P, ET])
        lid = sb("lid", [P, ET])
        deg = sb("deg", [P, ET])
        isrep = sb("isrep", [P, ET])
        repf = sb("repf", [P, ET])
        wE = sb("wE", [P, ET])
        wS = sb("wS", [P, ET])
        one = sb("one", [P, ET])
        tmp = [sb(f"tmp{k}", [P, ET]) for k in range(4)]
        gs_i = sb("gs_i", [P, ET + TI], I32)
        gd_i = sb("gd_i", [P, ET + TI], I32)
        gi_i = sb("gi_i", [P, ET + TI], I32)
        gr_i = sb("gr_i", [P, ET + TI], I32)
        gn_i = sb("gn_i", [P, ET + TI], I32)
        go_i = sb("go_i", [P, ET + TI], I32)
        tabs = sb("tabs", [P, ET + TI, 2])
        stg = sb("stg", [P, 2, TI], I32)
        tabg = sb("tabg", [P, TI, 2])
        a_s = sb("a_s", [P, ET])
        a_d = sb("a_d", [P, ET])
        a_o = sb("a_o", [P, ET])
        dl_i = sb("dl_i", [P, 2, 3, P], I32)
        dl = sb("dl", [P, 2, 3, P])
        keepF = sb("keepF", [P, 2, P])
        keepB = sb("keepB", [P, 2, P])
        penF = sb("penF", [P, 2, P])
        penB = sb("penB", [P, 2, P])
        rv = [sb(f"rv{k}", [P, 2, P]) for k in range(8)]
        rcol = sb("rcol", [P, 2, 8])
        krow = sb("krow", [1, 4, ET])
        crow = sb("crow", [1, ET + 2])
        ownr = sb("ownr", [P, 2, P])
        lid_b = sb("lid_b", [P, 2, P], U8)
        lidB = sb("lidB", [P, EP], U8)
        contB = sb("contB", [P, ET])

        ringG = sb("ringG", [P, NJ, TG, D])
        ringS = sb("ringS", [P, NJ, TG, D])
        ringO = sb("ringO", [P, NJ, TG, D])
        Sm = sb("Sm", [P, 2, TG, P])
        Dg = sb("Dg", [P, 2, TG, P])
        cm = sb("cm", [D, TG, P])
        zT = sb("zT", [D + 1, 2, GW])
        yb = sb("yb", [P, 2, TG, D])
        st6 = sb("st6", [P, 2, TG, 6])
        mv = sb("mv", [P, 2, TG, 2])
        sdv = sb("sdv", [P, 2, TG])
        acc = sb("acc", [P, 2, TG, D])

        wx = sb("wx", [D, TURN])
        wh = sb("wh", [D, TURN])
        wc = sb("wc", [D, TURN])
        wq = sb("wq", [D, TURN])
        w1 = sb("w1", [D, TURN])
        w2 = sb("w2", [D + 1, TURN])
        xin = ringG[0:NR].rearrange("p j t f -> p (j t f)")[:, 0:CH * CR * D].rearrange("p (c f) -> p c f", c=CH)
        rows = ringS[0:NR].rearrange("p j t f -> p (j t f)")[:, 0:CH * CR * D].rearrange("p (c f) -> p c f", c=CH)
        stN = sb("stN", [D, 2, ND * CH + NG])
        stE = sb("stE", [D, 2, NG])

        resR = sb("resR", [P, 2, TG, D])
        aux = sb("aux", [DE + 2, NJ, GW])

        bar = sem("all_engines")
        bars = {}

        def barrier(eng, key):
            bars[key] = bars.get(key, 0) + 1
            eng.drain().then_inc(bar, 1)
            eng.wait_ge(bar, ENGINES * bars[key])

        chains = {}

        def link(eng, key, ins):
            chains[key] = chains.get(key, 0) + 1
            ins.then_inc(sem(f"{key}_chain"), 1)
            eng.wait_ge(sem(f"{key}_chain"), chains[key])

        def chunk(buf, c, p=D):
            return buf[0:p, c * CW:(c + 1) * CW]

        PASSES = {}
        order = []

        def start_of(w):
            return 0 if w in {f"g{j}" for j in range(NJ)} else START

        def add_pass(name, signals="", credit=0, staged=0, slots=(0, 0, 0, 0, 0), **k):
            uses = {w: NG for w in signals.split()}
            if "z" in uses:
                uses["z"] = TG * NG
            if "seg" in uses:
                uses["seg"] += credit
            uses["staged"] = staged
            for c, n in zip("gmsro", slots):
                for j in range(NJ):
                    uses[f"{c}{j}"] = 16 * n * NI
            names = set(uses) | {"S", "D", "seg", "mask", "z", "cv", "th", "y", "st", "mv", "sq", "rc", "out", "u"}
            k["uses"] = uses
            k["base"] = {w: start_of(w) + sum(PASSES[q]["uses"].get(w, 0) for q in order) for w in names}
            k.setdefault("ngather", 1)
            k.setdefault("own", False)
            k.setdefault("tail", None)
            PASSES[name] = k
            order.append(name)

        def S(name):
            return sem("e_" + name)

        def at(p, name, v):
            return v + p["base"][name]

        def before(i, j):
            return i * NJ + max(j - 1, 0)

        def table_rows(t, g, row0=0):
            return t[row0:row0 + EP].rearrange("(g t p) f -> g p t f", t=TG, p=P)[g]

        def load_group(p, sp, i, j):
            g = i * NJ + j
            if p.get("m"):
                sp.dma_start(ringG[:, j], table_rows(p["m"], g)).then_inc(S(f"m{j}"), 16)
            if p.get("s"):
                sp.dma_start(ringS[:, j], table_rows(p["s"], g)).then_inc(S(f"s{j}"), 16)

        def res_of(p, j):
            return resR[:, j % 2] if p.get("r") else ringS[:, j]

        def conv_sp(p):
            def store(i, j):
                sp.wait_ge(S("out"), at(p, "out", i * NJ + j + 1))
                sp.nop(nofuse=True)
                sp.dma_start(table_rows(p["out"], i * NJ + j), ringO[:, j]).then_inc(S(f"o{j}"), 16)

            def load_res(i, j):
                if p.get("r"):
                    sp.wait_ge(S("y"), at(p, "y", before(i, j)))
                    sp.nop(nofuse=True)
                    sp.dma_start(resR[:, j % 2], table_rows(p["r"], i * NJ + j)).then_inc(S(f"r{j}"), 16)

            sp = nc.sync
            for j in range(NJ):
                load_group(p, sp, 0, j)

            def turn(i, last):
                load_res(i, 0)
                for j in range(NJ):
                    if j + 1 < NJ:
                        load_res(i, j + 1)
                    store(i, j)
                    if not last:
                        load_group(p, sp, i + 1, j)
            with sp.Fori(0, NI - 1) as i:
                turn(i, False)
            turn(NI - 1, True)
            for j in range(NJ):
                sp.wait_ge(S(f"o{j}"), at(p, f"o{j}", 16 * NI))

        def gather_pool(p, rings, tables):
            pool = nc.gpsimd
            with pool.Fori(0, NI) as i:
                for j in range(NJ):
                    pool.wait_ge(S("staged"), at(p, "staged", 2 * i + (1 if j < HALF else 2)))
                    pool.nop(nofuse=True)
                    if p["kind"] in ("copy", "att"):
                        pool.wait_ge(S(f"o{j}"), at(p, f"o{j}", i * (16 * p["ngather"])))
                        pool.nop(nofuse=True)
                    else:
                        pool.wait_ge(S("seg"), at(p, "seg", i * NJ + j + 1))
                        pool.nop(nofuse=True)
                    for k, (ring, table) in enumerate(zip(rings, tables)):
                        for t in range(TG):
                            pool.indirect_dma_start(
                                ring[:, j, t, :], None, table,
                                bass.IndirectOffsetOnAxis(ap=stg[:, k, TG * j + t:TG * j + t + 1], axis=0)).then_inc(S(f"g{j}"), 16)

        def stage(p, i, half):
            lo, hi = (0, HALF * TG) if half == 0 else (HALF * TG, TI)
            idx = p["gather"]
            for k, g in enumerate(idx):
                ins = nc.vector.tensor_copy(stg[:, k, lo:hi], g[:, ds(i * TI + lo, hi - lo)])
            ins.then_inc(S("staged"), 1)

        def stage_after(p, i, half):
            js = range(HALF) if half == 0 else range(HALF, NJ)
            for j in js:
                nc.vector.wait_ge(S(f"g{j}"), at(p, f"g{j}", (i + 1) * (16 * TG * p.get("ngather", 1))))
            stage(p, i + 1, half)

        def build_S(p, i, j, w):
            dve = nc.vector
            dve.wait_ge(S("seg"), at(p, "seg", before(i, j) + NJ))
            for t in range(TG):
                tile = (i * NJ + j) * TG + t
                ins = dve.tensor_scalar(Sm[:, j % 2, t], lidB[:, ds(tile * P, P)], lid[:, ds(tile, 1)],
                                        w[:, ds(tile, 1)], ALU.is_equal, ALU.mult)
            ins.then_inc(S("S"), 1)

        def add_carry(p, i, j):
            dve = nc.vector
            g = i * NJ + j
            dve.wait_ge(S("z"), at(p, "z", g * TG))
            dve.tensor_tensor(
                cm[:], lidB[0:D, ds(g * GW, GW)].rearrange("p (t e) -> p t e", t=TG),
                contB[0:D, ds(g * TG, TG)].unsqueeze(2).to_broadcast([D, TG, P]), ALU.is_equal).then_inc(S("mask"), 1)
            dve.wait_ge(S("mask"), at(p, "mask", g + 1))
            dve.wait_ge(S("seg"), at(p, "seg", g + 1 + NJ))
            dve.wait_ge(S("cv"), at(p, "cv", before(i, j)))
            b = j % 2
            for t in range(TG):
                if t:
                    dve.wait_ge(S("z"), at(p, "z", g * TG + t))
                before_ = zT[0:D, b, t * P - 1:t * P] if t else zT[0:D, (b + 1) % 2 if j else 0, GW - 1:GW]
                dve.scalar_tensor_tensor(
                    out=zT[0:D, b, t * P:(t + 1) * P], in0=cm[:, t], scalar=before_,
                    in1=ps[0:D, ZB + b, t * P:(t + 1) * P], op0=ALU.mult, op1=ALU.add).then_inc(S("z"), 1)

        def ln_sum(p, i, j):
            dve = nc.vector
            b, g = j % 2, i * NJ + j
            o = ps[:, OB, 0:TG * D].rearrange("p (t f) -> p t f", t=TG)
            if p["tail"] == "tanh":
                dve.wait_ge(S("th"), at(p, "th", g + 1))
            else:
                dve.wait_ge(S("cv"), at(p, "cv", g + 1))
            if p.get("r"):
                dve.wait_ge(S(f"r{j}"), at(p, f"r{j}", (i + 1) * 16))
            if p.get("s"):
                dve.wait_ge(S(f"s{j}"), at(p, f"s{j}", (i + 1) * 16))
            if p["tail"] == "tanh":
                dve.tensor_tensor(yb[:, b], yb[:, b], res_of(p, j), ALU.add).then_inc(S("y"), 1)
            elif p["tail"] == "ln":
                dve.tensor_tensor(yb[:, b], o, res_of(p, j), ALU.add).then_inc(S("y"), 1)
            elif p["tail"] == "copy":
                dve.tensor_copy(yb[:, b], o).then_inc(S("y"), 1)
            else:
                dve.scalar_tensor_tensor(out=ringS[:, j], in0=resR[:, b], scalar=0.5,
                                                in1=ringS[:, j], op0=ALU.mult, op1=ALU.add).then_inc(S("u"), 1)
                dve.wait_ge(S("u"), at(p, "u", g + 1))
                dve.scalar_tensor_tensor(out=yb[:, b], in0=o, scalar=0.5, in1=ringS[:, j],
                                                op0=ALU.mult, op1=ALU.add).then_inc(S("y"), 1)
            dve.wait_ge(S("y"), at(p, "y", g + 1))
            for t in range(TG):
                ins = dve.bn_stats(st6[:, b, t], yb[:, b, t])
            ins.then_inc(S("st"), 1)
            dve.wait_ge(S("st"), at(p, "st", g + 1))
            dve.nop(nofuse=True)
            for t in range(TG):
                ins = dve.bn_aggr(mv[:, b, t], st6[:, b, t])
            ins.then_inc(S("mv"), 1)

        def ln_scale(p, i, j):
            dve = nc.vector
            b, g = j % 2, i * NJ + j
            dve.wait_ge(S("sq"), at(p, "sq", g + 1))
            dve.reciprocal(sdv[:, b], sdv[:, b]).then_inc(S("rc"), 1)
            dve.wait_ge(S("rc"), at(p, "rc", g + 1))
            dve.wait_ge(S(f"o{j}"), at(p, f"o{j}", i * 16))
            for t in range(TG):
                ins = dve.tensor_scalar(ringO[:, j, t], yb[:, b, t], mv[:, b, t, 0:1], sdv[:, b, t:t + 1],
                                        ALU.subtract, ALU.mult)
            ins.then_inc(S("out"), 1)

        def conv_dve(p):
            dve = nc.vector
            link(dve, "dve", dve.memset(zT[0:D], 0.0))
            if p.get("gather"):
                stage(p, 0, 0)
                stage(p, 0, 1)
            ln = p["tail"] != "relu" and p["tail"] != "plain"
            with dve.Fori(0, NI) as i:
                build_S(p, i, 0, p["w"])
                for j in range(NJ):
                    if j + 1 < NJ:
                        build_S(p, i, j + 1, p["w"])
                    add_carry(p, i, j)
                    if p.get("gather") and j == HALF:
                        stage_after(p, i, 0)
                    if ln and j:
                        ln_scale(p, i, j - 1)
                    if ln:
                        ln_sum(p, i, j)
                if p.get("gather"):
                    stage_after(p, i, 1)
                if ln:
                    ln_scale(p, i, NJ - 1)

        def conv_pe(p):
            pe = nc.tensor
            pe.sem_inc(S("seg"), NJ)
            rhs = p["W"]

            def seg(i, j):
                g, b = i * NJ + j, j % 2
                pe.wait_ge(S("S"), at(p, "S", g + 1))
                if p.get("m"):
                    pe.wait_ge(S(f"m{j}"), at(p, f"m{j}", (i + 1) * 16))
                else:
                    pe.wait_ge(S(f"g{j}"), at(p, f"g{j}", (i + 1) * (16 * TG)))
                if p["own"]:
                    pe.wait_ge(S(f"s{j}"), at(p, f"s{j}", (i + 1) * 16))
                    pe.wait_ge(S("D"), at(p, "D", g + 1))
                pe.wait_ge(S("z"), at(p, "z", before(i, j) * TG))
                for t in range(TG):
                    o = ps[0:D, ZB + b, t * P:(t + 1) * P]
                    ins = pe.matmul(o, ringG[:, j, t], Sm[:, b, t], start=True, stop=not p["own"])
                    if p["own"]:
                        ins = pe.matmul(o, ringS[:, j, t], Dg[:, b, t], start=False, stop=True)
                ins.then_inc(S("seg"), 1)

            def rows_(i, j):
                g, b = i * NJ + j, j % 2
                pe.wait_ge(S("z"), at(p, "z", (g + 1) * TG))
                pe.wait_ge(S("out" if p["tail"] in ("relu", "plain") else "th" if p["tail"] == "tanh" else "y"), at(p, "out" if p["tail"] in ("relu", "plain") else "th" if p["tail"] == "tanh" else "y", g))
                for t in range(TG):
                    ins = pe.matmul(ps[:, OB, t * D:(t + 1) * D], zT[:, b, t * P:(t + 1) * P], rhs[:],
                                    start=True, stop=True)
                ins.then_inc(S("cv"), 1)

            with pe.Fori(0, NI) as i:
                seg(i, 0)
                for j in range(NJ):
                    if j + 1 < NJ:
                        seg(i, j + 1)
                    rows_(i, j)

        def conv_act(p):
            act = nc.scalar
            o = ps[:, OB, 0:TG * D]

            def diag(i, j):
                act.wait_ge(S("seg"), at(p, "seg", before(i, j) + NJ))
                for t in range(TG):
                    tile = (i * NJ + j) * TG + t
                    ins = act.activation(Dg[:, j % 2, t], ident[:], ACT.Copy, scale=wS[:, ds(tile, 1)])
                ins.then_inc(S("D"), 1)

            def tail(i, j):
                g, b = i * NJ + j, j % 2
                if p["tail"] in ("relu", "plain"):
                    act.wait_ge(S("cv"), at(p, "cv", g + 1))
                    act.wait_ge(S(f"o{j}"), at(p, f"o{j}", i * 16))
                    act.activation(ringO[:, j].rearrange("p t f -> p (t f)"), o,
                                          ACT.Relu if p["tail"] == "relu" else ACT.Copy).then_inc(S("out"), 1)
                elif p["tail"] == "tanh":
                    act.wait_ge(S("cv"), at(p, "cv", g + 1))
                    act.wait_ge(S("out"), at(p, "out", before(i, j)))
                    act.activation(yb[:, b].rearrange("p t f -> p (t f)"), o, ACT.Tanh).then_inc(S("th"), 1)

            def root(i, j):
                act.wait_ge(S("mv"), at(p, "mv", i * NJ + j + 1))
                act.activation(sdv[:, j % 2], mv[:, j % 2, :, 1], ACT.Sqrt, bias=epsc[:, 0:1]).then_inc(S("sq"), 1)

            ln = p["tail"] not in ("relu", "plain")
            if not (p["own"] or p["tail"] in ("relu", "plain", "tanh") or ln):
                return
            with act.Fori(0, NI) as i:
                if p["own"]:
                    diag(i, 0)
                for j in range(NJ):
                    if p["own"] and j + 1 < NJ:
                        diag(i, j + 1)
                    tail(i, j)
                    if ln:
                        root(i, j)

        nscan = {"dve": 0, "pe": 0}
        nmove = {"dve": 0, "pe": 0}

        def scan_dve(outv, data, keep, keep_row, fwd, summed=True):
            dve = nc.vector
            k = nscan["dve"] = nscan["dve"] + 1
            op0, op1 = (ALU.mult, ALU.add) if summed else (ALU.add, ALU.max)
            init = 0.0 if summed else -BIG
            f = (lambda ap: ap) if fwd else (lambda ap: ap[:, ::-1])
            for b, (_, n) in enumerate(RB):
                ins = dve.tensor_tensor_scan(f(outv[0:n, b]), f(keep[0:n, b]), f(data[0:n, b]), init, op0, op1)
            ins.then_inc(sem("scan_tile"), 1)
            dve.wait_ge(sem("scan_last"), k)
            link(dve, "dve", dve.memset(crow[:], init))
            to = crow[0:1, 1:ET + 1]
            dve.tensor_tensor_scan(f(to), f(keep_row), f(ps[0:1, ZB, 0:ET]), init, op0, op1).then_inc(sem("scan_row"), 1)
            dve.wait_ge(sem("scan_carry"), k)
            for b, (_, n) in enumerate(RB):
                link(dve, "dve", dve.tensor_copy(rcol[0:n, b, 0:1], ps[0:n, ZB + 1, 8 * b:8 * b + 1]))
            for b, (_, n) in enumerate(RB):
                link(dve, "dve", dve.tensor_tensor_scan(f(outv[0:n, b]), f(keep[0:n, b]), f(data[0:n, b]),
                                                        rcol[0:n, b, 0:1], op0, op1))

        def scan_pe(outv, fwd):
            pe = nc.tensor
            k = nscan["pe"] = nscan["pe"] + 1
            pe.wait_ge(sem("scan_tile"), k)
            c = P - 1 if fwd else 0
            for b, (t0, n) in enumerate(RB):
                ins = pe.transpose(ps[0:1, ZB, t0:t0 + n], outv[0:n, b, c:c + 1], ident[0:n, 0:n])
            ins.then_inc(sem("scan_last"), 1)
            pe.wait_ge(sem("scan_row"), k)
            off = 0 if fwd else 2
            for b, (t0, n) in enumerate(RB):
                ins = pe.matmul(ps[0:n, ZB + 1, 8 * b:8 * b + 1], crow[0:1, off + t0:off + t0 + n],
                                ones[0:1, 0:1], start=True, stop=True)
            ins.then_inc(sem("scan_carry"), 1)

        def to_cols_dve(dst):
            dve = nc.vector
            k = nmove["dve"] = nmove["dve"] + 1
            dve.sem_inc(sem("move_ready"), 1)
            dve.wait_ge(sem("move_done"), k)
            link(dve, "dve", dve.tensor_copy(dst[:, 0:ET], ps[:, OB, 0:ET]))

        def to_cols_pe(srcv):
            pe = nc.tensor
            k = nmove["pe"] = nmove["pe"] + 1
            pe.wait_ge(sem("move_ready"), k)
            for b, (t0, n) in enumerate(RB):
                ins = pe.transpose(ps[:, OB, t0:t0 + n], srcv[0:n, b], ident[0:n, 0:n])
            ins.then_inc(sem("move_done"), 1)

        def to_rows_dve(dst):
            dve = nc.vector
            k = nmove["dve"] = nmove["dve"] + 1
            dve.sem_inc(sem("move_ready"), 1)
            dve.wait_ge(sem("move_done"), k)
            for b, (_, n) in enumerate(RB):
                link(dve, "dve", dve.tensor_copy(dst[0:n, b], ps[0:n, OB, b * P:(b + 1) * P]))

        def to_rows_pe(srcv):
            pe = nc.tensor
            k = nmove["pe"] = nmove["pe"] + 1
            pe.wait_ge(sem("move_ready"), k)
            for b, (t0, n) in enumerate(RB):
                ins = pe.transpose(ps[0:n, OB, b * P:(b + 1) * P], srcv[:, t0:t0 + n], ident[:])
            ins.then_inc(sem("move_done"), 1)

        def blocks(fn):
            for b, (_, n) in enumerate(RB):
                link(nc.vector, "dve", fn(n, b))


        def copy_sp(p):
            sp = nc.sync
            with sp.Fori(0, NI) as i:
                for j in range(NJ):
                    sp.wait_ge(S(f"g{j}"), at(p, f"g{j}", (i + 1) * (16 * TG * p["ngather"])))
                    sp.nop(nofuse=True)
                    for ring, t in zip((ringG, ringS), p["to"]):
                        sp.dma_start(table_rows(t, i * NJ + j), ring[:, j]).then_inc(S(f"o{j}"), 16)
            for j in range(NJ):
                sp.wait_ge(S(f"o{j}"), at(p, f"o{j}", 16 * NI * p["ngather"]))

        def copy_dve(p):
            stage(p, 0, 0)
            stage(p, 0, 1)
            with nc.vector.Fori(0, NI) as i:
                stage_after(p, i, 0)
                stage_after(p, i, 1)

        def att_sp(p):
            sp = nc.sync
            for j in range(NJ):
                load_group(p, sp, 0, j)

            def turn(i, last):
                for j in range(NJ):
                    sp.wait_ge(S("out"), at(p, "out", i * NJ + j + 1))
                    sp.nop(nofuse=True)
                    sp.dma_start(table_rows(GX, i * NJ + j), ringG[:, j]).then_inc(S(f"o{j}"), 16)
                    if not last:
                        load_group(p, sp, i + 1, j)
            with sp.Fori(0, NI - 1) as i:
                turn(i, False)
            turn(NI - 1, True)
            for j in range(NJ):
                sp.wait_ge(S(f"o{j}"), at(p, f"o{j}", 16 * NI))

        def att_dve(p):
            dve = nc.vector
            stage(p, 0, 0)
            stage(p, 0, 1)
            with dve.Fori(0, NI) as i:
                for j in range(NJ):
                    g = i * NJ + j
                    dve.wait_ge(S(f"g{j}"), at(p, f"g{j}", (i + 1) * (16 * TG)))
                    dve.wait_ge(S(f"s{j}"), at(p, f"s{j}", (i + 1) * 16))
                    dve.wait_ge(S("out"), at(p, "out", g))
                    for k, (ring, v) in enumerate(((ringG, 0), (ringS, 0), (ringS, 1))):
                        ins = dve.tensor_tensor(att3[:, k], ring[:, j], uv[:, v:v + 1].to_broadcast([P, TG, D]), ALU.mult)
                    ins.then_inc(S("y"), 1)
                    dve.wait_ge(S("y"), at(p, "y", g + 1))
                    for k, dst in enumerate((a_s, a_o, a_d)):
                        ins = dve.tensor_reduce(dst[:, ds(g * TG, TG)], att3[:, k], AX_X, ALU.add)
                    ins.then_inc(S("out"), 1)
                    if j == HALF:
                        stage_after(p, i, 0)
                stage_after(p, i, 1)

        att3 = ringO[:, 0:3]

        def mlp_sp(p):
            sp = nc.sync

            def load(i, j):
                g = i * NJ + j
                sp.dma_start(aux[0:2, j], LINE[1:3].rearrange("r (g e) -> g r e", e=GW)[g]).then_inc(S(f"m{j}"), 16)
            for j in range(NJ):
                load_group(dict(p, m=None), sp, 0, j)
                load(0, j)

            def turn(i, last):
                for j in range(NJ):
                    sp.wait_ge(S("out"), at(p, "out", i * NJ + j + 1))
                    sp.nop(nofuse=True)
                    sp.dma_start(NDT[i * NJ + j], ndt(j % 2)).then_inc(S(f"o{j}"), 16)
                    if not last:
                        load_group(dict(p, m=None), sp, i + 1, j)
                        load(i + 1, j)
            with sp.Fori(0, NI - 1) as i:
                turn(i, False)
            turn(NI - 1, True)
            for j in range(NJ):
                sp.wait_ge(S(f"o{j}"), at(p, f"o{j}", 16 * NI))

        def ndt(b):
            return (wc, wq)[b][:, 0:2 * GW].rearrange("p (k e) -> p k e", k=2)

        def mlp_pe(p):
            pe = nc.tensor
            with pe.Fori(0, NI) as i:
                for j in range(NJ):
                    g = i * NJ + j
                    pe.wait_ge(S(f"s{j}"), at(p, f"s{j}", (i + 1) * 16))
                    pe.wait_ge(S(f"m{j}"), at(p, f"m{j}", (i + 1) * 16))
                    pe.wait_ge(S("y"), at(p, "y", g))
                    for t in range(TG):
                        ins = pe.transpose(ps[0:D, DB, t * P:(t + 1) * P], ringS[:, j, t], ident[:])
                    ins.then_inc(S("seg"), 1)
                    pe.wait_ge(S("y"), at(p, "y", g + 1))
                    pe.wait_ge(S("th"), at(p, "th", g))
                    pe.matmul(ps[0:D, DB + 1, 0:GW], WN[0:D], ndt(j % 2)[:, 0], start=True, stop=False)
                    pe.matmul(ps[0:D, DB + 1, 0:GW], nb2[:], aux[0:2, j], start=False, stop=True).then_inc(S("cv"), 1)

        def mlp_dve(p):
            dve = nc.vector
            with dve.Fori(0, NI) as i:
                for j in range(NJ):
                    g = i * NJ + j
                    dve.wait_ge(S("seg"), at(p, "seg", g + 1))
                    if j > 1:
                        dve.wait_ge(S(f"o{j - 2}"), at(p, f"o{j - 2}", (i + 1) * 16))
                    else:
                        dve.wait_ge(S(f"o{NJ - 1 - j}"), at(p, f"o{NJ - 1 - j}", i * 16))
                        if j:
                            dve.wait_ge(S(f"o{NJ - 1}"), at(p, f"o{NJ - 1}", i * 16))
                    dve.tensor_copy(ndt(j % 2)[:, 0], ps[0:D, DB, 0:GW]).then_inc(S("y"), 1)

        def mlp_act(p):
            act = nc.scalar
            with act.Fori(0, NI) as i:
                for j in range(NJ):
                    g = i * NJ + j
                    act.wait_ge(S("cv"), at(p, "cv", g + 1))
                    h = ndt(j % 2)[:, 1]
                    act.wait_ge(S("out"), at(p, "out", g))
                    act.activation(h, ps[0:D, DB + 1, 0:GW], ACT.Relu,
                                          accum_out=stN[:, 0, ds(g + ND * CH, 1)]).then_inc(S("th"), 1)
                    act.wait_ge(S("th"), at(p, "th", g + 1))
                    act.activation(wh[:, 0:GW], h, ACT.Square,
                                          accum_out=stN[:, 1, ds(g + ND * CH, 1)]).then_inc(S("out"), 1)

        def emlp_sp(p):
            sp = nc.sync

            def load(i, j):
                sp.dma_start(aux[:, j], a["auxe"].rearrange("r (g e) -> g r e", e=GW)[i * NJ + j]).then_inc(S(f"m{j}"), 16)
            for j in range(NJ):
                load(0, j)
            with sp.Fori(0, NI - 1) as i:
                for j in range(NJ):
                    sp.wait_ge(S("cv"), at(p, "cv", i * NJ + j + 1))
                    sp.nop(nofuse=True)
                    load(i + 1, j)

        def emlp_pe(p):
            pe = nc.tensor
            with pe.Fori(0, NI) as i:
                for j in range(NJ):
                    g = i * NJ + j
                    pe.wait_ge(S(f"m{j}"), at(p, f"m{j}", (i + 1) * 16))
                    pe.wait_ge(S("th"), at(p, "th", before(i, j)))
                    pe.matmul(ps[0:D, DB + j % 2, 0:GW], WE[:], aux[:, j], start=True, stop=True).then_inc(S("cv"), 1)

        def emlp_act(p):
            act = nc.scalar
            with act.Fori(0, NI) as i:
                for j in range(NJ):
                    g = i * NJ + j
                    act.wait_ge(S("cv"), at(p, "cv", g + 1))
                    act.wait_ge(S("out"), at(p, "out", g))
                    act.activation(wh[:, 0:GW], ps[0:D, DB + j % 2, 0:GW], ACT.Relu,
                                          accum_out=stE[:, 0, ds(g, 1)]).then_inc(S("th"), 1)
                    act.wait_ge(S("th"), at(p, "th", g + 1))
                    act.activation(wh[:, 0:GW], wh[:, 0:GW], ACT.Square,
                                          accum_out=stE[:, 1, ds(g, 1)]).then_inc(S("out"), 1)

        xsT, xdT, heT = wc[:, 0:GW], wc[:, GW:2 * GW], wc[:, 2 * GW:3 * GW]
        msq = wq[0:D, 0:TG * D]

        def msg_sp(p):
            sp = nc.sync

            def load(i, j):
                sp.dma_start(aux[:, j], a["auxe"].rearrange("r (g e) -> g r e", e=GW)[i * NJ + j]).then_inc(S(f"m{j}"), 16)
            for j in range(NJ):
                load(0, j)

            def turn(i, last):
                for j in range(NJ):
                    g = i * NJ + j
                    sp.wait_ge(S("z"), at(p, "z", (g + 1) * TG))
                    sp.nop(nofuse=True)
                    sp.dma_start(AGG[g], zT[0:D, j % 2]).then_inc(S(f"o{j}"), 16)
                    if not last:
                        load(i + 1, j)
            with sp.Fori(0, NI - 1) as i:
                turn(i, False)
            turn(NI - 1, True)
            for j in range(NJ):
                sp.wait_ge(S(f"o{j}"), at(p, f"o{j}", 16 * NI))

        def msg_pe(p):
            pe = nc.tensor
            pe.sem_inc(S("seg"), NJ)

            def turned(i, j):
                g = i * NJ + j
                pe.wait_ge(S(f"g{j}"), at(p, f"g{j}", (i + 1) * (16 * TG * 2)))
                pe.wait_ge(S(f"m{j}"), at(p, f"m{j}", (i + 1) * 16))
                pe.wait_ge(S("y"), at(p, "y", g))
                pe.wait_ge(S("th"), at(p, "th", g))
                for t in range(TG):
                    pe.transpose(ps[0:D, DB, t * P:(t + 1) * P], ringG[:, j, t], ident[:])
                for t in range(TG):
                    pe.transpose(ps[0:D, DB + 1, t * P:(t + 1) * P], ringS[:, j, t], ident[:])
                pe.matmul(ps[0:D, DB + 2, 0:GW], WE[:], aux[:, j], start=True, stop=True).then_inc(S("D"), 1)

            def message(i, j):
                g = i * NJ + j
                pe.wait_ge(S("y"), at(p, "y", g + 1))
                pe.wait_ge(S("th"), at(p, "th", g + 1))
                pe.wait_ge(S("u"), at(p, "u", g))
                for t in range(TG):
                    o = ps[:, OB, t * D:(t + 1) * D]
                    e = slice(t * P, (t + 1) * P)
                    pe.matmul(o, xsT[:, e], WM[:, 0], start=True, stop=False)
                    pe.matmul(o, xdT[:, e], WM[:, 1], start=False, stop=False)
                    pe.matmul(o, heT[:, e], WM3[:], start=False, stop=False)
                    ins = pe.matmul(o, aux[0:2, j, e], mb2[:], start=False, stop=True)
                ins.then_inc(S("cv"), 1)

            def seg(i, j):
                g, b = i * NJ + j, j % 2
                pe.wait_ge(S("S"), at(p, "S", g + 1))
                pe.wait_ge(S("u"), at(p, "u", g + 1))
                pe.wait_ge(S("z"), at(p, "z", before(i, j) * TG))
                for t in range(TG):
                    ins = pe.matmul(ps[0:D, ZB + b, t * P:(t + 1) * P], ringO[:, j, t], Sm[:, b, t],
                                    start=True, stop=True)
                ins.then_inc(S("seg"), 1)

            with pe.Fori(0, NI) as i:
                for j in range(NJ):
                    turned(i, j)
                    message(i, j)
                    seg(i, j)

        def msg_act(p):
            act = nc.scalar
            with act.Fori(0, NI) as i:
                for j in range(NJ):
                    g = i * NJ + j
                    act.wait_ge(S("D"), at(p, "D", g + 1))
                    act.wait_ge(S("cv"), at(p, "cv", g))
                    act.activation(xdT, ps[0:D, DB + 1, 0:GW], ACT.Copy)
                    act.activation(heT, ps[0:D, DB + 2, 0:GW], ACT.Relu).then_inc(S("th"), 1)
                    act.wait_ge(S("cv"), at(p, "cv", g + 1))
                    act.wait_ge(S("seg"), at(p, "seg", g + 1))
                    act.wait_ge(S("out"), at(p, "out", g))
                    act.activation(ringO[:, j].rearrange("p t f -> p (t f)"), ps[:, OB, 0:TG * D], ACT.Relu).then_inc(S("u"), 1)
                    act.wait_ge(S("u"), at(p, "u", g + 1))
                    act.activation(yb[:, 0].rearrange("p t f -> p (t f)"),
                                          ringO[:, j].rearrange("p t f -> p (t f)"), ACT.Square).then_inc(S("sq"), 1)

        def msg_dve(p):
            dve = nc.vector
            link(dve, "dve", dve.memset(zT[0:D], 0.0))
            link(dve, "dve", dve.memset(acc[:], 0.0))
            stage(p, 0, 0)
            stage(p, 0, 1)
            with dve.Fori(0, NI) as i:
                for j in range(NJ):
                    g = i * NJ + j
                    build_S(p, i, j, one)
                    dve.wait_ge(S("D"), at(p, "D", g + 1))
                    dve.wait_ge(S("cv"), at(p, "cv", g))
                    dve.tensor_copy(xsT, ps[0:D, DB, 0:GW]).then_inc(S("y"), 1)
                    dve.wait_ge(S("u"), at(p, "u", g + 1))
                    dve.wait_ge(S("out"), at(p, "out", g))
                    dve.tensor_tensor(acc[:, 0], acc[:, 0], ringO[:, j], ALU.add)
                    dve.wait_ge(S("sq"), at(p, "sq", g + 1))
                    dve.tensor_tensor(acc[:, 1], acc[:, 1], yb[:, 0], ALU.add).then_inc(S("out"), 1)
                    if j > 1:
                        dve.wait_ge(S(f"o{j - 2}"), at(p, f"o{j - 2}", (i + 1) * 16))
                    else:
                        dve.wait_ge(S(f"o{NJ - 1 - j}"), at(p, f"o{NJ - 1 - j}", i * 16))
                        if j:
                            dve.wait_ge(S(f"o{NJ - 1}"), at(p, f"o{NJ - 1}", i * 16))
                    add_carry(dict(p, nocv=True), i, j)
                    if j == HALF:
                        stage_after(p, i, 0)
                stage_after(p, i, 1)

        def join_buf(b):
            return (wc, wq)[b][:, 0:3 * GW].rearrange("p (k e) -> p k e", k=3)

        def join_sp(p):
            sp = nc.sync

            def load(i, j):
                g = i * NJ + j
                sp.wait_ge(S("cv"), at(p, "cv", before(i, j)))
                sp.nop(nofuse=True)
                sp.dma_start(join_buf(j % 2)[:, 0:2], NDT[g]).then_inc(S(f"m{j}"), 16)
                sp.dma_start(join_buf(j % 2)[:, 2], AGG[g]).then_inc(S(f"r{j}"), 16)
                sp.dma_start(aux[0:2, j], LINE[0:2].rearrange("r (g e) -> g r e", e=GW)[g]).then_inc(S(f"s{j}"), 16)
            with sp.Fori(0, NI) as i:
                load(i, 0)
                for j in range(NJ):
                    if j + 1 < NJ:
                        load(i, j + 1)
                    sp.wait_ge(S("out"), at(p, "out", i * NJ + j + 1))
                    sp.nop(nofuse=True)
                    sp.dma_start(table_rows(T[5], i * NJ + j), ringO[:, j]).then_inc(S(f"o{j}"), 16)
            for j in range(NJ):
                sp.wait_ge(S(f"o{j}"), at(p, f"o{j}", 16 * NI))

        def join_pe(p):
            pe = nc.tensor
            with pe.Fori(0, NI) as i:
                for j in range(NJ):
                    g = i * NJ + j
                    for r in "mrs":
                        pe.wait_ge(S(f"{r}{j}"), at(p, f"{r}{j}", (i + 1) * 16))
                    pe.wait_ge(S("y"), at(p, "y", g))
                    for t in range(TG):
                        o = ps[:, OB, t * D:(t + 1) * D]
                        e = slice(t * P, (t + 1) * P)
                        pe.matmul(o, join_buf(j % 2)[:, 0, e], cent[:], start=True, stop=False)
                        pe.matmul(o, join_buf(j % 2)[:, 1, e], AN[:], start=False, stop=False)
                        pe.matmul(o, join_buf(j % 2)[:, 2, e], AM[:], start=False, stop=False)
                        ins = pe.matmul(o, aux[0:2, j, e], sh2[:], start=False, stop=True)
                    ins.then_inc(S("cv"), 1)

        def join_dve(p):
            with nc.vector.Fori(0, NI) as i:
                for j in range(NJ):
                    ln_sum(p, i, j)
                    ln_scale(p, i, j)

        def put_sp(p):
            sp = nc.sync
            for j in range(NJ):
                load_group(p, sp, 0, j)
            with sp.Fori(0, NI - 1) as i:
                for j in range(NJ):
                    sp.wait_ge(S(f"g{j}"), at(p, f"g{j}", (i + 1) * (16 * TG)))
                    sp.nop(nofuse=True)
                    load_group(p, sp, i + 1, j)

        def put_pool(p):
            pool = nc.gpsimd
            with pool.Fori(0, NI) as i:
                for j in range(NJ):
                    pool.wait_ge(S("staged"), at(p, "staged", 2 * i + (1 if j < HALF else 2)))
                    pool.nop(nofuse=True)
                    pool.wait_ge(S(f"s{j}"), at(p, f"s{j}", (i + 1) * 16))
                    pool.nop(nofuse=True)
                    for t in range(TG):
                        pool.indirect_dma_start(
                            a["out"], bass.IndirectOffsetOnAxis(ap=stg[:, 0, TG * j + t:TG * j + t + 1], axis=0),
                            ringS[:, j, t, :], None, bounds_check=N - 1, oob_is_err=False).then_inc(S(f"g{j}"), 16)
            for j in range(NJ):
                pool.wait_ge(S(f"g{j}"), at(p, f"g{j}", 16 * TG * NI))

        def tab_put_dve(p):
            dve = nc.vector
            dve.tensor_copy(tabg[:], tabs[:, 0:TI, :])
            dve.tensor_copy(stg[:, 0], go_i[:, 0:TI]).then_inc(S("staged"), 1)
            with dve.Fori(0, NI - 1) as i:
                for j in range(NJ):
                    dve.wait_ge(S(f"g{j}"), at(p, f"g{j}", (i + 1) * (16 * TG)))
                dve.tensor_copy(tabg[:], tabs[:, ds((i + 1) * TI, TI), :])
                dve.tensor_copy(stg[:, 0], go_i[:, ds((i + 1) * TI, TI)]).then_inc(S("staged"), 1)

        def tab_put_pool(p):
            pool = nc.gpsimd
            with pool.Fori(0, NI) as i:
                pool.wait_ge(S("staged"), at(p, "staged", i + 1))
                pool.nop(nofuse=True)
                for j in range(NJ):
                    for t in range(j * TG, (j + 1) * TG):
                        pool.indirect_dma_start(
                            TAB, bass.IndirectOffsetOnAxis(ap=stg[:, 0, t:t + 1], axis=0), tabg[:, t, :], None,
                            bounds_check=N - 1, oob_is_err=False).then_inc(S(f"g{j}"), 16)
            for j in range(NJ):
                pool.wait_ge(S(f"g{j}"), at(p, f"g{j}", 16 * TG * NI))

        def tab_get_dve(p):
            dve = nc.vector
            dve.tensor_copy(stg[:, 0], gs_i[:, 0:TI]).then_inc(S("staged"), 1)
            with dve.Fori(0, NI) as i:
                for j in range(NJ):
                    dve.wait_ge(S(f"g{j}"), at(p, f"g{j}", (i + 1) * (16 * TG)))
                dve.tensor_copy(tabs[:, ds(i * TI, TI), :], tabg[:])
                dve.tensor_copy(stg[:, 0], gs_i[:, ds((i + 1) * TI, TI)]).then_inc(S("staged"), 1)
            link(dve, "dve", dve.drain())

        def tab_get_pool(p):
            pool = nc.gpsimd
            with pool.Fori(0, NI) as i:
                pool.wait_ge(S("staged"), at(p, "staged", i + 1))
                pool.nop(nofuse=True)
                for j in range(NJ):
                    for t in range(j * TG, (j + 1) * TG):
                        pool.indirect_dma_start(
                            tabg[:, t, :], None, TAB,
                            bass.IndirectOffsetOnAxis(ap=stg[:, 0, t:t + 1], axis=0)).then_inc(S(f"g{j}"), 16)

        DENSE, dorder = {}, []

        def add_dense(name, signals, **k):
            n = CH * k["turns"]
            uses = {w: n for w in signals.split()}
            for w in ("tp", "ev"):
                if w in uses:
                    uses[w] = 4 * n
            uses[k["last"]] += CH
            for c in range(CH):
                for w, m in k["slots"].items():
                    uses[f"{w}{c}"] = 16 * m * k["turns"]
            names = set(uses) | {f"{w}{c}" for w in ("ld", "mk", "o", "ro") for c in range(CH)} | set(CHAIN.split())
            k["uses"] = uses
            k["base"] = {w: START + sum(DENSE[q]["uses"].get(w, 0) for q in dorder) for w in names}
            DENSE[name] = k
            dorder.append(name)

        def R(name):
            return sem("d_" + name)

        def dat(p, name, v):
            return v + p["base"][name] + (CH if name == p["last"] else 0)

        def chunk_rows(t, i, c, row0=0, n=TURN):
            v = t[row0:row0 + n].rearrange("(i p r) f -> i p (r f)", p=NR, r=RW)[i]
            return v[:, c * CR * D:(c + 1) * CR * D]

        def stages(fn, i):
            for c in range(CH):
                fn(c, i * CH + c)

        def chain_sp(p):
            sp = nc.sync
            src, n = p["x"], TURN * p["turns"]

            def load(i, c):
                sp.dma_start(xin[:, c], chunk_rows(src, i, c, 0, n)).then_inc(R(f"ld{c}"), 16)

            def mask(i, c):
                if p["stats"]:
                    sp.dma_start(w2[D:D + 1, c * CW:(c + 1) * CW], ACTV[i:i + 1, c * CW:(c + 1) * CW] if isinstance(i, int) else ACTV[ds(i, 1), c * CW:(c + 1) * CW]).then_inc(R(f"mk{c}"), 16)

            for c in range(CH):
                load(0, c)
                mask(0, c)

            def turn(i, last):
                for c in range(CH):
                    sp.wait_ge(R("tr"), dat(p, "tr", i * CH + c + 1))
                    sp.nop(nofuse=True)
                    if not last:
                        load(i + 1, c)
                for s in range(p["nrows"]):
                    for c in range(CH):
                        sp.wait_ge(R("ev"), dat(p, "ev", i * (4 * CH) + s * CH + c + 1))
                        sp.nop(nofuse=True)
                        sp.dma_start(chunk_rows(T[s + 1], i, c, EP, LR), rows[:, c]).then_inc(R(f"ro{c}"), 16)
                for c in range(CH):
                    sp.wait_ge(R("x2"), dat(p, "x2", i * CH + c + 1))
                    sp.nop(nofuse=True)
                    sp.dma_start(p["to"][i, :, c * CW:(c + 1) * CW], chunk(w2, c)).then_inc(R(f"o{c}"), 16)
                    if p["stats"] and not last:
                        sp.wait_ge(R("pn"), dat(p, "pn", i * CH + c + 1))
                        sp.nop(nofuse=True)
                        mask(i + 1, c)
            with sp.Fori(0, p["turns"] - 1) as i:
                turn(i, False)
            turn(p["turns"] - 1, True)
            for c in range(CH):
                sp.wait_ge(R(f"o{c}"), dat(p, f"o{c}", 16 * p["turns"]))
                if p["nrows"]:
                    sp.wait_ge(R(f"ro{c}"), dat(p, f"ro{c}", 16 * p["turns"] * p["nrows"]))

        def bank(c, p=D, w=CW):
            return ps[0:p, DB + c, 0:w]

        def chain_pe(p):
            pe = nc.tensor
            pe.sem_inc(R(p["last"]), CH)

            def put_rows(s, c, i, buf):
                e = i * (4 * CH) + s * CH + c
                if isinstance(e, int):
                    e = e
                k = (s * CH + c) % 2
                pe.wait_ge(R("ev"), dat(p, "ev", e if (s * CH + c) == 0 else e - 1))
                for q in range(CR):
                    ins = pe.transpose(ps[0:NR, ZB + k, q * D:(q + 1) * D],
                                       buf[0:D, c * CW + q * NR:c * CW + (q + 1) * NR], ident[0:D, 0:D])
                ins.then_inc(R("tp"), 1)

            with pe.Fori(0, p["turns"]) as i:
                for c in range(CH):
                    g = i * CH + c
                    pe.wait_ge(R(f"ld{c}"), dat(p, f"ld{c}", (i + 1) * 16))
                    pe.wait_ge(R(p["last"]), dat(p, p["last"], g + 1 - CH))
                    for q in range(CR):
                        ins = pe.transpose(ps[0:D, DB + c, q * NR:(q + 1) * NR],
                                           xin[:, c, q * D:(q + 1) * D], ident[0:NR, 0:NR])
                    ins.then_inc(R("tr"), 1)
                for c in range(CH):
                    pe.wait_ge(R("x0"), dat(p, "x0", i * CH + c + 1))
                    pe.matmul(bank(c), W["1"][0:D], chunk(wx, c), start=True, stop=True).then_inc(R("p1"), 1)
                for c in range(CH):
                    pe.wait_ge(R("h1"), dat(p, "h1", i * CH + c + 1))
                    if p["nrows"]:
                        put_rows(0, c, i, wh)
                    pe.matmul(bank(c), W["2"][0:D], chunk(wh, c), start=True, stop=True).then_inc(R("p2"), 1)
                for c in range(CH):
                    pe.wait_ge(R("h2"), dat(p, "h2", i * CH + c + 1))
                    if p["nrows"]:
                        put_rows(1, c, i, wh)
                    pe.matmul(bank(c), cent[:], chunk(wx, c), start=True, stop=False)
                    pe.matmul(bank(c), W3C[:], chunk(wh, c), start=False, stop=True).then_inc(R("p3"), 1)
                for c in range(CH):
                    pe.wait_ge(R("q1"), dat(p, "q1", i * CH + c + 1))
                    pe.wait_ge(R("c1"), dat(p, "c1", i * CH + c + 1))
                    pe.matmul(bank(c), avg[:], chunk(wq, c), start=True, stop=True).then_inc(R("v1"), 1)
                for c in range(CH):
                    pe.wait_ge(R("x1"), dat(p, "x1", i * CH + c + 1))
                    if p["nrows"]:
                        put_rows(2, c, i, w1)
                    pe.matmul(bank(c), W["G"][0:D], chunk(w1, c), start=True, stop=True).then_inc(R("pg"), 1)
                for c in range(CH):
                    pe.wait_ge(R("th"), dat(p, "th", i * CH + c + 1))
                    pe.matmul(bank(c), cent[:], chunk(w1, c), start=True, stop=False)
                    pe.matmul(bank(c), cent[:], chunk(wh, c), start=False, stop=True).then_inc(R("p4"), 1)
                for c in range(CH):
                    pe.wait_ge(R("q2"), dat(p, "q2", i * CH + c + 1))
                    pe.wait_ge(R("c2"), dat(p, "c2", i * CH + c + 1))
                    pe.matmul(bank(c), avg[:], chunk(wq, c), start=True, stop=True).then_inc(R("v2"), 1)
                for c in range(CH):
                    pe.wait_ge(R("x2"), dat(p, "x2", i * CH + c + 1))
                    if p["nrows"]:
                        put_rows(3, c, i, w2)
                    if p["stats"]:
                        pe.wait_ge(R(f"mk{c}"), dat(p, f"mk{c}", (i + 1) * 16))
                        pe.wait_ge(R("d2"), dat(p, "d2", i * CH + c + 1))
                        pe.matmul(bank(c), WN[:], chunk(w2, c, D + 1), start=True, stop=True).then_inc(R("pn"), 1)

        def chain_act(p):
            act = nc.scalar

            def evict(s, i):
                for c in range(CH):
                    e = i * (4 * CH) + s * CH + c
                    act.wait_ge(R("tp"), dat(p, "tp", e + 1))
                    act.wait_ge(R(f"ro{c}"), dat(p, f"ro{c}", i * (16 * 4) + 16 * s))
                    act.activation(rows[:, c], ps[0:NR, ZB + (s * CH + c) % 2, 0:CR * D], ACT.Copy).then_inc(R("ev"), 1)

            with act.Fori(0, p["turns"]) as i:
                for c in range(CH):
                    act.wait_ge(R("p1"), dat(p, "p1", i * CH + c + 1))
                    if p["stats"]:
                        act.wait_ge(R("qn"), dat(p, "qn", i * CH))
                    act.activation(chunk(wh, c), bank(c), ACT.Relu, bias=col[:, B_1:B_1 + 1]).then_inc(R("h1"), 1)
                if p["nrows"]:
                    evict(0, i)
                    evict(1, i)
                for c in range(CH):
                    act.wait_ge(R("c1"), dat(p, "c1", i * CH + c + 1))
                    act.activation(chunk(wq, c), chunk(wc, c), ACT.Square).then_inc(R("q1"), 1)
                for c in range(CH):
                    act.wait_ge(R("v1"), dat(p, "v1", i * CH + c + 1))
                    act.activation(chunk(wq, c), bank(c), ACT.Sqrt, bias=epsc[0:D, 0:1]).then_inc(R("d1"), 1)
                if p["nrows"]:
                    evict(2, i)
                for c in range(CH):
                    act.wait_ge(R("pg"), dat(p, "pg", i * CH + c + 1))
                    act.activation(chunk(wh, c), bank(c), ACT.Tanh, bias=col[:, B_G:B_G + 1]).then_inc(R("th"), 1)
                for c in range(CH):
                    act.wait_ge(R("c2"), dat(p, "c2", i * CH + c + 1))
                    act.activation(chunk(wq, c), chunk(wc, c), ACT.Square).then_inc(R("q2"), 1)
                for c in range(CH):
                    act.wait_ge(R("v2"), dat(p, "v2", i * CH + c + 1))
                    act.activation(chunk(wq, c), bank(c), ACT.Sqrt, bias=epsc[0:D, 0:1]).then_inc(R("d2"), 1)
                if p["nrows"]:
                    evict(3, i)
                if p["stats"]:
                    for c in range(CH):
                        g = i * CH + c
                        act.wait_ge(R("pn"), dat(p, "pn", g + 1))
                        act.activation(chunk(wh, c), bank(c), ACT.Relu, bias=col[:, B_N:B_N + 1],
                                            accum_out=stN[:, 0, ds(g, 1)]).then_inc(R("rn"), 1)
                    for c in range(CH):
                        g = i * CH + c
                        act.wait_ge(R("rn"), dat(p, "rn", g + 1))
                        act.activation(chunk(wh, c), chunk(wh, c), ACT.Square,
                                            accum_out=stN[:, 1, ds(g, 1)]).then_inc(R("qn"), 1)

        def chain_dve(p):
            dve = nc.vector
            with dve.Fori(0, p["turns"]) as i:
                for c in range(CH):
                    dve.wait_ge(R("tr"), dat(p, "tr", i * CH + c + 1))
                    dve.tensor_copy(chunk(wx, c), bank(c)).then_inc(R("x0"), 1)
                for c in range(CH):
                    dve.wait_ge(R("p2"), dat(p, "p2", i * CH + c + 1))
                    dve.tensor_scalar(chunk(wh, c), bank(c), col[:, B_2:B_2 + 1], 0.0, ALU.add, ALU.max).then_inc(R("h2"), 1)
                for c in range(CH):
                    dve.wait_ge(R("p3"), dat(p, "p3", i * CH + c + 1))
                    dve.tensor_scalar(chunk(wc, c), bank(c), col[:, B_3C:B_3C + 1], None, ALU.add).then_inc(R("c1"), 1)
                for c in range(CH):
                    dve.wait_ge(R("d1"), dat(p, "d1", i * CH + c + 1))
                    dve.reciprocal(chunk(wq, c), chunk(wq, c)).then_inc(R("r1"), 1)
                for c in range(CH):
                    dve.wait_ge(R("r1"), dat(p, "r1", i * CH + c + 1))
                    dve.tensor_tensor(chunk(w1, c), chunk(wc, c), chunk(wq, c), ALU.mult).then_inc(R("x1"), 1)
                for c in range(CH):
                    dve.wait_ge(R("p4"), dat(p, "p4", i * CH + c + 1))
                    dve.tensor_copy(chunk(wc, c), bank(c)).then_inc(R("c2"), 1)
                for c in range(CH):
                    dve.wait_ge(R("d2"), dat(p, "d2", i * CH + c + 1))
                    dve.reciprocal(chunk(wq, c), chunk(wq, c)).then_inc(R("r2"), 1)
                for c in range(CH):
                    dve.wait_ge(R("r2"), dat(p, "r2", i * CH + c + 1))
                    dve.wait_ge(R(f"o{c}"), dat(p, f"o{c}", i * 16))
                    dve.tensor_tensor(chunk(w2, c), chunk(wc, c), chunk(wq, c), ALU.mult).then_inc(R("x2"), 1)

        def end_sp(p):
            sp = nc.sync

            def load(i, c):
                sp.dma_start(chunk(w2, c), p["x"][i, :, c * CW:(c + 1) * CW]).then_inc(R(f"ld{c}"), 16)
            for c in range(CH):
                load(0, c)

            def turn(i, last):
                for c in range(CH):
                    sp.wait_ge(R("p3"), dat(p, "p3", i * CH + c + 1))
                    sp.nop(nofuse=True)
                    if not last:
                        load(i + 1, c)
                for c in range(CH):
                    sp.wait_ge(R("eb"), dat(p, "eb", i * CH + c + 1))
                    sp.nop(nofuse=True)
                    sp.dma_start(chunk_rows(p["to"], i, c, p["row0"], TURN * p["turns"]), rows[:, c]).then_inc(R(f"ro{c}"), 16)
            with sp.Fori(0, p["turns"] - 1) as i:
                turn(i, False)
            turn(p["turns"] - 1, True)
            for c in range(CH):
                sp.wait_ge(R(f"ro{c}"), dat(p, f"ro{c}", 16 * p["turns"]))

        def end_pe(p):
            pe = nc.tensor
            pe.sem_inc(R("eb"), CH)
            with pe.Fori(0, p["turns"]) as i:
                for c in range(CH):
                    pe.wait_ge(R(f"ld{c}"), dat(p, f"ld{c}", (i + 1) * 16))
                    pe.wait_ge(R("eb"), dat(p, "eb", i * CH + c + 1 - CH))
                    pe.matmul(bank(c), WN[0:D], chunk(w2, c), start=True, stop=True).then_inc(R("pn"), 1)
                for c in range(CH):
                    pe.wait_ge(R("rn"), dat(p, "rn", i * CH + c + 1))
                    pe.matmul(bank(c), cent[:], chunk(w2, c), start=True, stop=False)
                    pe.matmul(bank(c), AN[:], chunk(wh, c), start=False, stop=True).then_inc(R("p3"), 1)
                for c in range(CH):
                    pe.wait_ge(R("q1"), dat(p, "q1", i * CH + c + 1))
                    pe.wait_ge(R("c1"), dat(p, "c1", i * CH + c + 1))
                    pe.matmul(bank(c), avg[:], chunk(wq, c), start=True, stop=True).then_inc(R("v1"), 1)
                for c in range(CH):
                    pe.wait_ge(R("y"), dat(p, "y", i * CH + c + 1))
                    pe.wait_ge(R("d1"), dat(p, "d1", i * CH + c + 1))
                    for q in range(CR):
                        ins = pe.transpose(ps[0:NR, DB + c, q * D:(q + 1) * D],
                                           w1[0:D, c * CW + q * NR:c * CW + (q + 1) * NR], ident[0:D, 0:D])
                    ins.then_inc(R("tb"), 1)

        def end_act(p):
            act = nc.scalar
            sc, bi = (1.0, epsc[0:D, 0:1]) if p["row0"] else (1.0 + EPS, epsc[0:D, 1:2])
            with act.Fori(0, p["turns"]) as i:
                for c in range(CH):
                    act.wait_ge(R("pn"), dat(p, "pn", i * CH + c + 1))
                    act.activation(chunk(wh, c), bank(c), ACT.Relu, bias=col[:, B_N:B_N + 1]).then_inc(R("rn"), 1)
                for c in range(CH):
                    act.wait_ge(R("c1"), dat(p, "c1", i * CH + c + 1))
                    act.activation(chunk(wq, c), chunk(wc, c), ACT.Square).then_inc(R("q1"), 1)
                for c in range(CH):
                    act.wait_ge(R("v1"), dat(p, "v1", i * CH + c + 1))
                    act.activation(chunk(wq, c), bank(c), ACT.Sqrt, bias=bi, scale=sc).then_inc(R("d1"), 1)
                for c in range(CH):
                    act.wait_ge(R("tb"), dat(p, "tb", i * CH + c + 1))
                    act.wait_ge(R(f"ro{c}"), dat(p, f"ro{c}", i * 16))
                    act.activation(rows[:, c], ps[0:NR, DB + c, 0:CR * D], ACT.Copy).then_inc(R("eb"), 1)

        def end_dve(p):
            dve = nc.vector
            with dve.Fori(0, p["turns"]) as i:
                for c in range(CH):
                    dve.wait_ge(R("p3"), dat(p, "p3", i * CH + c + 1))
                    dve.tensor_scalar(chunk(wc, c), bank(c), col[:, C_N:C_N + 1], None, ALU.add).then_inc(R("c1"), 1)
                for c in range(CH):
                    dve.wait_ge(R("d1"), dat(p, "d1", i * CH + c + 1))
                    dve.reciprocal(chunk(wq, c), chunk(wq, c)).then_inc(R("r1"), 1)
                for c in range(CH):
                    dve.wait_ge(R("r1"), dat(p, "r1", i * CH + c + 1))
                    dve.tensor_tensor(chunk(w1, c), chunk(wc, c), chunk(wq, c), ALU.mult).then_inc(R("y"), 1)

        def norm_dve(k, s, q, count, g, b, ac, sc):
            dve = nc.vector
            t = tmp[0][0:D]
            link(dve, "dve", dve.tensor_scalar(t[:, 0:1], s, 1.0 / count, None, ALU.mult))
            link(dve, "dve", dve.tensor_scalar(t[:, 1:2], q, 1.0 / count, None, ALU.mult))
            link(dve, "dve", dve.tensor_tensor(t[:, 2:3], t[:, 0:1], t[:, 0:1], ALU.mult))
            dve.tensor_tensor(t[:, 3:4], t[:, 1:2], t[:, 2:3], ALU.subtract).then_inc(sem("norm_var"), 1)
            dve.wait_ge(sem("norm_root"), k)
            link(dve, "dve", dve.reciprocal(t[:, 5:6], t[:, 4:5]))
            link(dve, "dve", dve.tensor_tensor(col[:, ac:ac + 1], col[:, g:g + 1], t[:, 5:6], ALU.mult))
            link(dve, "dve", dve.tensor_tensor(t[:, 6:7], t[:, 0:1], col[:, ac:ac + 1], ALU.mult))
            link(dve, "dve", dve.tensor_tensor(col[:, sc:sc + 1], col[:, b:b + 1], t[:, 6:7], ALU.subtract))

        def norm_act(k):
            act = nc.scalar
            act.wait_ge(sem("norm_var"), k)
            act.activation(tmp[0][0:D, 4:5], tmp[0][0:D, 3:4], ACT.Sqrt, bias=epsc[0:D, 0:1]).then_inc(sem("norm_root"), 1)

        CHAIN = "tr x0 p1 h1 p2 h2 p3 c1 q1 v1 d1 r1 x1 pg th p4 c2 q2 v2 d2 r2 x2 pn rn qn tp ev y tb eb"
        chain_sig = "tr x0 p1 h1 p2 h2 p3 c1 q1 v1 d1 r1 x1 pg th p4 c2 q2 v2 d2 r2 x2"
        end_sig = "pn rn p3 c1 q1 v1 d1 r1 y tb eb"
        ln_sig = "S seg mask z cv out y st mv sq rc "
        GS = 2 + 2 * NI
        add_pass("tab_put", kind="tab", staged=NI, slots=(TG, 0, 0, 0, 0))
        add_pass("tab_get", kind="tab", staged=NI + 1, slots=(TG, 0, 0, 0, 0))
        add_pass("copy", kind="copy", gather=(gs_i, gd_i), ngather=2, to=(XS, XD), staged=GS,
                 slots=(2 * TG, 0, 0, 0, 2))
        add_pass("conv1", "S D seg mask z cv out", NJ, slots=(0, 1, 1, 0, 1), kind="conv", m=XS, s=XD, own=True,
                 w=wE, W=W["1"], tail="relu", out=T[1])
        add_pass("conv2", "S D seg mask z cv out", NJ, GS, slots=(TG, 0, 1, 0, 1), kind="conv", gather=(gi_i,),
                 table=T[1], s=T[1], own=True, w=wE, W=W["2"], tail="relu", out=T[2])
        add_pass("conv3", ln_sig + "D", NJ, GS, slots=(TG, 0, 1, 1, 1), kind="conv", gather=(gi_i,),
                 table=T[2], s=T[2], r=XD, own=True, w=wE, W=W["3"], tail="ln", out=T[3])
        add_pass("att", "y out", 0, GS, slots=(TG, 0, 1, 0, 1), kind="att", gather=(gi_i,), s=T[3])
        add_pass("gat", ln_sig + "D th", NJ, slots=(0, 1, 1, 0, 1), kind="conv", m=GX, s=T[3], own=True,
                 w=wE, W=W["G"], tail="tanh", out=T[4])
        add_pass("mlp", "seg y cv th out", slots=(0, 1, 1, 0, 1), kind="mlp", s=T[4])
        add_pass("emlp", "cv th out", slots=(0, 1, 0, 0, 0), kind="emlp")
        add_pass("msg", "S D seg mask z cv y th u sq out", NJ, GS, slots=(2 * TG, 1, 0, 0, 1), kind="msg",
                 gather=(gi_i, gr_i), ngather=2)
        add_pass("join", "cv y st mv sq rc out", slots=(0, 1, 1, 1, 1), kind="join", tail="copy")
        add_pass("hop1", "S seg mask z cv out", NJ, GS, slots=(TG, 0, 0, 0, 1), kind="conv", gather=(gi_i,),
                 table=T[5], w=wE, W=W["I"], tail="plain", out=TN)
        add_pass("hop2", ln_sig + "u", NJ, GS, slots=(TG, 0, 1, 1, 1), kind="conv", gather=(gn_i,),
                 table=TN, s=T[5], r=TN, w=wE, W=W["I"], tail="half", out=FR)
        add_pass("put", staged=GS, slots=(TG, 0, 1, 0, 0), kind="put", gather=(go_i,), s=FR)
        add_dense("source", chain_sig + " tp ev", turns=NL, x=XS, to=X2L, nrows=4, stats=False, last="d2",
                  slots=dict(ld=1, o=1, ro=4), row0=0)
        add_dense("dense", chain_sig + " pn rn qn", turns=ND, x=a["x"], to=X2T, nrows=0, stats=True, last="rn",
                  slots=dict(ld=1, o=1, mk=1), row0=0)
        add_dense("source3", end_sig, turns=NL, x=X2L, to=T[5], row0=EP, last="eb", slots=dict(ld=1, ro=1), nrows=0)
        add_dense("final", end_sig, turns=ND, x=X2T, to=a["out"], row0=0, last="eb", slots=dict(ld=1, ro=1), nrows=0)
        PQ, DQ = PASSES, DENSE
        loaded = sem("loaded")
        n_loads = [0]

        def prepare_sp():
            sp = nc.sync
            sp.wait_ge(sem("cleared"), 1)

            def ld(dst, src):
                n_loads[0] += 1
                sp.dma_start(dst, src).then_inc(loaded, 16)
            r = lambda v: a[v].rearrange("(o f) -> o f", o=1)
            c = lambda v: a[v].rearrange("(f o) -> f o", o=1)
            ld(ident[:], a["ident"])
            ld(cent[:], a["cent"])
            ld(avg[:], a["avg"])
            for k, wn, bn in (("1", "L0_gnn_W1", "L0_gnn_b1"), ("2", "L0_gnn_W2", "L0_gnn_b2"),
                              ("3", "L0_gnn_W3", "L0_gnn_b3"), ("G", "L1_gnn_W", "L1_gnn_bias")):
                ld(W[k][0:D], a[wn])
                ld(W[k][D:D + 1], r(bn))
            ld(W["I"][:], a["eye_row"])
            ld(WN[0:D], a["L2_gnn_W_node"])
            ld(WE[2:2 + DE], a["L2_gnn_W_edge"])
            ld(WE[0:1], r("L2_gnn_b_edge"))
            ld(WM[:], a["L2_gnn_W_msg"].rearrange("(k f) n -> f k n", k=3))
            ld(nb2[0:1], r("L2_gnn_b_node"))
            ld(mb2[0:1], r("L2_gnn_b_msg"))
            for k, v in ((B_1, "L0_gnn_b1"), (B_2, "L0_gnn_b2"), (B_3, "L0_gnn_b3"), (B_G, "L1_gnn_bias"),
                         (B_N, "L2_gnn_b_node"), (B_M, "L2_gnn_b_msg"), (G_N, "L2_gnn_g_node"),
                         (BE_N, "L2_gnn_beta_node"), (G_E, "L2_gnn_g_edge"), (BE_E, "L2_gnn_beta_edge"),
                         (G_M, "L2_gnn_g_msg"), (BE_M, "L2_gnn_beta_msg")):
                ld(col[:, k:k + 1], c(v))
            ld(att[:, 0:1], c("L1_gnn_att_src"))
            ld(att[:, 1:2], c("L1_gnn_att_dst"))
            ld(src_i[:], a["src_cols"])
            ld(dst_i[:], a["dst_cols"])
            ld(own[:], a["own_cols"])
            ld(ownr[:], a["own_rows"])
            for b, (t0, n) in enumerate(RB):
                for k in range(3):
                    ld(dl_i[0:n, b, k], a["dst_line"][k + t0 * P:k + (t0 + n) * P].rearrange("(t e) -> t e", e=P))
            ld(XS[EP:LR].rearrange("(p a) f -> p (a f)", p=114), zero[0:114, 0:(LR - EP) // 114 * D])
            for h in range(2):
                ld(TAB[h * N // 2:(h + 1) * N // 2].rearrange("(p a) f -> p (a f)", p=125), zero[0:125, 0:800])
            ld(TN[EP:EP + P], zero[:, 0:D])
            sp.wait_ge(loaded, 16 * n_loads[0])
            sp.sem_inc(sem("ready"), 1)
            sp.wait_ge(sem("lines"), 1)
            m = 0
            for b, (t0, n) in enumerate(RB):
                v = lambda t: t[t0 * P:(t0 + n) * P].rearrange("(t e) -> t e", e=P)
                for dst, src in ((v(LID), lid_b[0:n, b]), (v(LINE[0]), rv[5][0:n, b]), (v(LINE[1]), onesr[0:n, b]),
                                 (v(LINE[2]), rv[2][0:n, b]),
                                 (CONT[t0:t0 + n].rearrange("(t o) -> t o", o=1), rcol[0:n, b, 6:7])):
                    sp.dma_start(dst, src).then_inc(sem("lined"), 16)
                    m += 16
            sp.wait_ge(sem("lined"), m)
            sp.dma_start(lidB[:], LID.rearrange("(o e) -> o e", o=1).to_broadcast([P, EP])).then_inc(sem("lined"), 16)
            sp.dma_start(contB[:], CONT.rearrange("(o e) -> o e", o=1).to_broadcast([P, ET])).then_inc(sem("lined"), 16)
            sp.wait_ge(sem("lined"), m + 32)

        def prepare_dve():
            dve = nc.vector
            for t, v in ((ones, 1.0), (onesr, 1.0), (one, 1.0), (zero, 0.0), (WE, 0.0), (nb2, -BIG), (mb2, -BIG),
                         (zT, 1.0), (gs_i, 0), (gd_i, 0), (gi_i, 0), (gr_i, 0), (gn_i, 0), (go_i, N), (tabs, 0.0)):
                link(dve, "dve", dve.memset(t[:], v))
            link(dve, "dve", dve.memset(WN[D:D + 1], -BIG))
            link(dve, "dve", dve.memset(epsc[:, 0:1], EPS))
            link(dve, "dve", dve.memset(epsc[:, 1:2], EPS * EPS))
            dve.sem_inc(sem("cleared"), 1)
            dve.wait_ge(sem("ready"), 1)
            L = lambda ins: link(dve, "dve", ins)
            dve.wait_ge(sem("w_pe"), 1)
            L(dve.tensor_copy(wt[:, 0], ps[0:D, DB, 0:D]))
            L(dve.tensor_copy(wt[:, 1], ps[0:D, DB, D:2 * D]))
            L(dve.tensor_scalar(attB[:, 0], ones[0:D], att[:, 0:1], None, ALU.mult))
            dve.tensor_scalar(attB[:, 1], ones[0:D], att[:, 1:2], None, ALU.mult).then_inc(sem("w_dve"), 1)
            dve.wait_ge(sem("w_pe"), 2)
            L(dve.tensor_copy(W3C[:], ps[0:D, DB + 1, 0:D]))
            L(dve.tensor_copy(col[:, B_3C:B_3C + 1], ps[0:D, DB + 1, D:D + 1]))
            for k in range(2):
                L(dve.tensor_copy(uv[:, k], ps[:, DB + 2, k * P:k * P + D]))
            L(dve.tensor_copy(gs_i[:, 0:ET], src_i[:]))
            L(dve.tensor_copy(tmp[1][:], dst_i[:]))
            L(dve.tensor_scalar(gd_i[:, 0:ET], tmp[1][:], float(N - 1), None, ALU.min))
            blocks(lambda n, b: dve.tensor_copy(dl[0:n, b], dl_i[0:n, b]))
            blocks(lambda n, b: dve.tensor_tensor(keepF[0:n, b], dl[0:n, b, 1], dl[0:n, b, 0], ALU.is_equal))
            blocks(lambda n, b: dve.tensor_tensor(keepB[0:n, b], dl[0:n, b, 1], dl[0:n, b, 2], ALU.is_equal))
            blocks(lambda n, b: dve.tensor_scalar(penF[0:n, b], keepF[0:n, b], 1.0, BIG, ALU.subtract, ALU.mult))
            blocks(lambda n, b: dve.tensor_scalar(penB[0:n, b], keepB[0:n, b], 1.0, BIG, ALU.subtract, ALU.mult))
            for k, v in enumerate((keepF, keepB, penF, penB)):
                blocks(lambda n, b: dve.tensor_reduce(rcol[0:n, b, 1 + k:2 + k], v[0:n, b], AX_X, ALU.min))
            dve.sem_inc(sem("keep_cols"), 1)
            dve.wait_ge(sem("keep_rows"), 1)
            for k in range(4):
                L(dve.tensor_copy(krow[0:1, k], ps[0:1, DB + k, 0:ET]))
            blocks(lambda n, b: dve.tensor_scalar(rv[0][0:n, b], keepF[0:n, b], -1.0, 1.0, ALU.mult, ALU.add))
            blocks(lambda n, b: dve.memset(rv[0][0:n, b, 0:1], 0.0))
            blocks(lambda n, b: dve.tensor_tensor_scan(rv[1][0:n, b], onesr[0:n, b], rv[0][0:n, b], 0.0, ALU.mult, ALU.add))
            blocks(lambda n, b: dve.tensor_copy(lid_b[0:n, b], rv[1][0:n, b]))
            blocks(lambda n, b: dve.tensor_scalar(rcol[0:n, b, 6:7], keepF[0:n, b, 0:1], 1.0, None, ALU.subtract))
            to_cols_dve(lid)
            scan_dve(rv[3], onesr, keepF, krow[0:1, 0], True)
            scan_dve(rv[4], onesr, keepB, krow[0:1, 1], False)
            blocks(lambda n, b: dve.scalar_tensor_tensor(out=rv[5][0:n, b], in0=rv[3][0:n, b], scalar=-1.0,
                                                         in1=rv[4][0:n, b], op0=ALU.add, op1=ALU.add))
            blocks(lambda n, b: dve.scalar_tensor_tensor(out=rv[6][0:n, b], in0=rv[4][0:n, b], scalar=-1.0,
                                                         in1=ownr[0:n, b], op0=ALU.add, op1=ALU.add))
            blocks(lambda n, b: dve.tensor_scalar(rv[0][0:n, b], keepB[0:n, b], -1.0, 1.0, ALU.mult, ALU.add))
            blocks(lambda n, b: dve.scalar_tensor_tensor(out=rv[7][0:n, b], in0=dl[0:n, b, 1], scalar=float(N),
                                                         in1=rv[0][0:n, b], op0=ALU.is_lt, op1=ALU.mult))
            blocks(lambda n, b: dve.tensor_scalar(rv[2][0:n, b], rv[7][0:n, b], -1.0, 1.0, ALU.mult, ALU.add))
            dve.sem_inc(sem("lines"), 1)
            to_cols_dve(deg)
            to_cols_dve(repf)
            to_cols_dve(isrep)
            L(dve.tensor_copy(gr_i[:, 0:ET], repf[:]))
            L(dve.tensor_scalar(tmp[1][:], tmp[1][:], float(N), None, ALU.subtract))
            L(dve.tensor_tensor(tmp[1][:], tmp[1][:], isrep[:], ALU.mult))
            L(dve.tensor_scalar(go_i[:, 0:ET], tmp[1][:], float(N), None, ALU.add))
            L(dve.tensor_copy(tabs[:, 0:ET, 0], repf[:]))
            L(dve.tensor_copy(tabs[:, 0:ET, 1], deg[:]))

        def prepare_pe():
            pe = nc.tensor
            pe.wait_ge(sem("ready"), 1)
            pe.transpose(ps[0:D, DB, 0:D], W["3"][0:D], ident[0:D, 0:D])
            pe.transpose(ps[0:D, DB, D:2 * D], W["G"][0:D], ident[0:D, 0:D]).then_inc(sem("w_pe"), 1)
            pe.wait_ge(sem("w_dve"), 1)
            pe.matmul(ps[0:D, DB + 1, 0:D], wt[:, 0], cent[:], start=True, stop=True)
            pe.matmul(ps[0:D, DB + 1, D:D + 1], cent[:], col[:, B_3:B_3 + 1], start=True, stop=True)
            for k in range(2):
                ins = pe.matmul(ps[:, DB + 2, k * P:k * P + D], attB[:, k], wt[:, 1], start=True, stop=True)
            ins.then_inc(sem("w_pe"), 1)
            pe.wait_ge(sem("keep_cols"), 1)
            for k in range(4):
                for b, (t0, n) in enumerate(RB):
                    ins = pe.transpose(ps[0:1, DB + k, t0:t0 + n], rcol[0:n, b, 1 + k:2 + k], ident[0:n, 0:n])
            ins.then_inc(sem("keep_rows"), 1)
            to_cols_pe(rv[1])
            scan_pe(rv[3], True)
            scan_pe(rv[4], False)
            to_cols_pe(rv[5])
            to_cols_pe(rv[6])
            to_cols_pe(rv[7])

        def index_dve():
            dve = nc.vector
            L = lambda ins: link(dve, "dve", ins)
            s_, d_, A, B = tabs[:, 0:ET, 0], tabs[:, 0:ET, 1], tmp[2][:], tmp[3][:]
            L(dve.tensor_scalar(A, d_, 0.0, None, ALU.is_gt))
            L(dve.tensor_tensor(B, s_, own[:], ALU.subtract))
            L(dve.tensor_scalar(B, B, float(EP), None, ALU.subtract))
            L(dve.tensor_tensor(B, B, A, ALU.mult))
            L(dve.tensor_tensor(B, B, own[:], ALU.add))
            L(dve.tensor_scalar(gi_i[:, 0:ET], B, float(EP), None, ALU.add))
            L(dve.tensor_scalar(B, s_, float(EP), None, ALU.subtract))
            L(dve.tensor_tensor(B, B, A, ALU.mult))
            L(dve.tensor_scalar(gn_i[:, 0:ET], B, float(EP), None, ALU.add))
            L(dve.tensor_scalar(A, d_, 1.0, None, ALU.add))
            dve.tensor_scalar(B, deg[:], 1.0, None, ALU.add).then_inc(sem("deg1"), 1)
            dve.wait_ge(sem("deg_root"), 1)
            L(dve.reciprocal(A, A))
            L(dve.reciprocal(B, B))
            L(dve.tensor_tensor(wE[:], A, B, ALU.mult))
            L(dve.tensor_tensor(B, B, B, ALU.mult))
            L(dve.tensor_tensor(wS[:], B, isrep[:], ALU.mult))
            half = TURN // 2
            dve.wait_ge(sem("tab_in"), 32)
            for h, t in enumerate((wx, wh)):
                src = t[0:ND, 0:2 * half].rearrange("i (p r two) -> i r p two", r=RW, two=2)[:, :, :, 1]
                dst = wc[0:ND, 0:TURN].rearrange("i (r p) -> i r p", r=RW)[:, :, h * (NR // 2):(h + 1) * (NR // 2)]
                L(dve.tensor_scalar(dst, src, 0.0, None, ALU.is_gt))
            dve.sem_inc(sem("active"), 1)

        def index_act():
            act = nc.scalar
            act.wait_ge(sem("deg1"), 1)
            act.activation(tmp[2][:], tmp[2][:], ACT.Sqrt)
            act.activation(tmp[3][:], tmp[3][:], ACT.Sqrt).then_inc(sem("deg_root"), 1)

        def index_sp():
            sp = nc.sync
            half = TURN // 2
            for h, t in enumerate((wx, wh)):
                sp.dma_start(t[0:ND, 0:2 * half],
                             TAB.rearrange("(i h n) two -> i h (n two)", h=2, n=half)[:, h]).then_inc(sem("tab_in"), 16)
            sp.wait_ge(sem("active"), 1)
            sp.dma_start(ACTV, wc[0:ND, 0:TURN]).then_inc(sem("active_out"), 16)
            sp.wait_ge(sem("active_out"), 16)

        def soft_dve():
            dve = nc.vector
            asr, adr, aor = rv[0], rv[1], rv[2]
            to_rows_dve(asr)
            to_rows_dve(adr)
            to_rows_dve(aor)
            blocks(lambda n, b: dve.tensor_scalar(rv[7][0:n, b], keepB[0:n, b], -1.0, 1.0, ALU.mult, ALU.add))
            blocks(lambda n, b: dve.tensor_tensor(adr[0:n, b], adr[0:n, b], rv[7][0:n, b], ALU.mult))
            blocks(lambda n, b: dve.tensor_tensor(aor[0:n, b], aor[0:n, b], rv[7][0:n, b], ALU.mult))
            scan_dve(rv[3], adr, keepB, krow[0:1, 1], False)
            scan_dve(rv[4], aor, keepB, krow[0:1, 1], False)
            for x in (asr, rv[4]):
                blocks(lambda n, b: dve.tensor_tensor(x[0:n, b], x[0:n, b], rv[3][0:n, b], ALU.add))
                blocks(lambda n, b: dve.scalar_tensor_tensor(out=x[0:n, b], in0=x[0:n, b], scalar=SLOPE, in1=x[0:n, b],
                                                             op0=ALU.mult, op1=ALU.max))
            scan_dve(rv[1], asr, penF, krow[0:1, 2], True, summed=False)
            scan_dve(rv[2], asr, penB, krow[0:1, 3], False, summed=False)
            blocks(lambda n, b: dve.tensor_tensor(rv[1][0:n, b], rv[1][0:n, b], rv[2][0:n, b], ALU.max))
            blocks(lambda n, b: dve.tensor_tensor(rv[1][0:n, b], rv[1][0:n, b], rv[4][0:n, b], ALU.max))
            blocks(lambda n, b: dve.tensor_tensor(rv[5][0:n, b], asr[0:n, b], rv[1][0:n, b], ALU.subtract))
            blocks(lambda n, b: dve.tensor_tensor(rv[6][0:n, b], rv[4][0:n, b], rv[1][0:n, b], ALU.subtract))
            dve.sem_inc(sem("logits"), 1)
            dve.wait_ge(sem("exps"), 1)
            scan_dve(rv[1], rv[5], keepF, krow[0:1, 0], True)
            scan_dve(rv[2], rv[5], keepB, krow[0:1, 1], False)
            blocks(lambda n, b: dve.tensor_tensor(rv[1][0:n, b], rv[1][0:n, b], rv[5][0:n, b], ALU.subtract))
            blocks(lambda n, b: dve.tensor_tensor(rv[1][0:n, b], rv[1][0:n, b], rv[2][0:n, b], ALU.add))
            blocks(lambda n, b: dve.tensor_tensor(rv[1][0:n, b], rv[1][0:n, b], rv[6][0:n, b], ALU.add))
            blocks(lambda n, b: dve.tensor_scalar(rv[1][0:n, b], rv[1][0:n, b], 1e-16, None, ALU.add))
            blocks(lambda n, b: dve.reciprocal(rv[1][0:n, b], rv[1][0:n, b]))
            blocks(lambda n, b: dve.tensor_tensor(rv[5][0:n, b], rv[5][0:n, b], rv[1][0:n, b], ALU.mult))
            blocks(lambda n, b: dve.tensor_tensor(rv[6][0:n, b], rv[6][0:n, b], rv[1][0:n, b], ALU.mult))
            to_cols_dve(wE)
            to_cols_dve(wS)
            link(dve, "dve", dve.tensor_tensor(wS[:], wS[:], isrep[:], ALU.mult))

        def soft_pe():
            to_rows_pe(a_s)
            to_rows_pe(a_d)
            to_rows_pe(a_o)
            scan_pe(rv[3], False)
            scan_pe(rv[4], False)
            scan_pe(rv[1], True)
            scan_pe(rv[2], False)
            scan_pe(rv[1], True)
            scan_pe(rv[2], False)
            to_cols_pe(rv[5])
            to_cols_pe(rv[6])

        def soft_act():
            act = nc.scalar
            act.wait_ge(sem("logits"), 1)
            for v in (rv[5], rv[6]):
                for b, (_, n) in enumerate(RB):
                    ins = act.activation(v[0:n, b], v[0:n, b], ACT.Exp)
            ins.then_inc(sem("exps"), 1)

        def norm1_dve():
            dve = nc.vector
            L = lambda ins: link(dve, "dve", ins)
            t = tmp[1][0:D]
            for k, st in enumerate((stN, stE)):
                for m in range(2):
                    L(dve.tensor_reduce(t[:, 2 * k + m:2 * k + m + 1], st[:, m], AX_X, ALU.add))
            norm_dve(1, t[:, 0:1], t[:, 1:2], N, G_N, BE_N, A_N, S_N)
            norm_dve(2, t[:, 2:3], t[:, 3:4], E, G_E, BE_E, A_E, S_E)
            L(dve.tensor_scalar(WM3[:], WM[:, 2], col[:, A_E:A_E + 1], None, ALU.mult))
            dve.tensor_scalar(AN[:], cent[:], col[:, A_N:A_N + 1], None, ALU.mult).then_inc(sem("norm1"), 1)
            dve.wait_ge(sem("norm1_pe"), 1)
            L(dve.tensor_copy(col[:, C_N:C_N + 1], ps[0:D, DB, 0:1]))
            L(dve.tensor_tensor(mb2[0:1], mb2[0:1], ps[0:1, DB + 1, 0:D], ALU.add))

        def norm1_pe():
            pe = nc.tensor
            pe.wait_ge(sem("norm1"), 1)
            pe.matmul(ps[0:D, DB, 0:1], cent[:], col[:, S_N:S_N + 1], start=True, stop=True)
            pe.matmul(ps[0:1, DB + 1, 0:D], col[:, S_E:S_E + 1], WM[:, 2], start=True, stop=True).then_inc(sem("norm1_pe"), 1)

        def norm2_dve():
            dve = nc.vector
            L = lambda ins: link(dve, "dve", ins)
            t = tmp[1][0:D]
            dve.wait_ge(sem("msum"), 1)
            L(dve.tensor_copy(t[:, 0:2], ps[0:D, DB, 0:2]))
            norm_dve(3, t[:, 0:1], t[:, 1:2], E, G_M, BE_M, A_M, S_M)
            L(dve.tensor_scalar(AM[:], cent[:], col[:, A_M:A_M + 1], None, ALU.mult))
            L(dve.tensor_copy(t[:, 4:5], col[:, S_M:S_M + 1]))
            dve.tensor_copy(t[:, 5:6], col[:, S_N:S_N + 1]).then_inc(sem("norm2"), 1)
            dve.wait_ge(sem("norm2_pe"), 1)
            L(dve.tensor_copy(sh2[:], ps[0:2, DB + 1, 0:D]))
            L(dve.reciprocal(tmp[2][:], deg[:]))
            L(dve.tensor_copy(wE[:], tmp[2][:]))

        def norm2_pe():
            pe = nc.tensor
            for m in range(2):
                for t in range(TG):
                    ins = pe.matmul(ps[0:D, DB, m:m + 1], acc[:, m, t], ones[:, 0:1], start=(t == 0), stop=(t == TG - 1))
            ins.then_inc(sem("msum"), 1)
            pe.wait_ge(sem("norm2"), 1)
            pe.matmul(ps[0:2, DB + 1, 0:D], tmp[1][0:D, 4:6], cent[:], start=True, stop=True).then_inc(sem("norm2_pe"), 1)

        block = ctx.enter_context(nc.Block())

        @block.sync
        def _(sp):
            prepare_sp()
            barrier(sp, "sp")
            barrier(sp, "sp")
            index_sp()
            copy_sp(PQ["copy"])
            barrier(sp, "sp")
            chain_sp(DQ["source"])
            barrier(sp, "sp")
            chain_sp(DQ["dense"])
            barrier(sp, "sp")
            for name in ("conv1", "conv2", "conv3"):
                conv_sp(PQ[name])
                barrier(sp, "sp")
            att_sp(PQ["att"])
            barrier(sp, "sp")
            barrier(sp, "sp")
            conv_sp(PQ["gat"])
            barrier(sp, "sp")
            mlp_sp(PQ["mlp"])
            barrier(sp, "sp")
            emlp_sp(PQ["emlp"])
            barrier(sp, "sp")
            barrier(sp, "sp")
            msg_sp(PQ["msg"])
            barrier(sp, "sp")
            barrier(sp, "sp")
            join_sp(PQ["join"])
            barrier(sp, "sp")
            end_sp(DQ["source3"])
            barrier(sp, "sp")
            conv_sp(PQ["hop1"])
            barrier(sp, "sp")
            conv_sp(PQ["hop2"])
            barrier(sp, "sp")
            end_sp(DQ["final"])
            barrier(sp, "sp")
            put_sp(PQ["put"])

        @block.gpsimd
        def _(pool):
            for name in list(PQ["put"]["base"]):
                if start_of(name):
                    pool.sem_inc(S(name), START)
            for name in list(DQ["final"]["base"]):
                pool.sem_inc(R(name), START)
            barrier(pool, "pool")
            tab_put_pool(PQ["tab_put"])
            barrier(pool, "pool")
            tab_get_pool(PQ["tab_get"])
            gather_pool(PQ["copy"], (ringG, ringS), (a["x"], a["x"]))
            barrier(pool, "pool")
            barrier(pool, "pool")
            barrier(pool, "pool")
            barrier(pool, "pool")
            for name in ("conv2", "conv3"):
                gather_pool(PQ[name], (ringG,), (PQ[name]["table"],))
                barrier(pool, "pool")
            gather_pool(PQ["att"], (ringG,), (T[3],))
            for _ in range(5):
                barrier(pool, "pool")
            barrier(pool, "pool")
            gather_pool(PQ["msg"], (ringG, ringS), (T[4], T[4]))
            for _ in range(4):
                barrier(pool, "pool")
            for name in ("hop1", "hop2"):
                gather_pool(PQ[name], (ringG,), (PQ[name]["table"],))
                barrier(pool, "pool")
            barrier(pool, "pool")
            put_pool(PQ["put"])

        @block.scalar
        def _(act):
            barrier(act, "act")
            barrier(act, "act")
            index_act()
            barrier(act, "act")
            chain_act(DQ["source"])
            barrier(act, "act")
            chain_act(DQ["dense"])
            barrier(act, "act")
            for name in ("conv1", "conv2", "conv3"):
                conv_act(PQ[name])
                barrier(act, "act")
            barrier(act, "act")
            soft_act()
            barrier(act, "act")
            conv_act(PQ["gat"])
            barrier(act, "act")
            mlp_act(PQ["mlp"])
            barrier(act, "act")
            emlp_act(PQ["emlp"])
            barrier(act, "act")
            norm_act(1)
            norm_act(2)
            barrier(act, "act")
            msg_act(PQ["msg"])
            barrier(act, "act")
            norm_act(3)
            barrier(act, "act")
            conv_act(PQ["join"])
            barrier(act, "act")
            end_act(DQ["source3"])
            barrier(act, "act")
            conv_act(PQ["hop1"])
            barrier(act, "act")
            conv_act(PQ["hop2"])
            barrier(act, "act")
            end_act(DQ["final"])
            barrier(act, "act")

        @block.vector
        def _(dve):
            prepare_dve()
            barrier(dve, "dve_")
            tab_put_dve(PQ["tab_put"])
            barrier(dve, "dve_")
            tab_get_dve(PQ["tab_get"])
            index_dve()
            copy_dve(PQ["copy"])
            barrier(dve, "dve_")
            chain_dve(DQ["source"])
            barrier(dve, "dve_")
            chain_dve(DQ["dense"])
            barrier(dve, "dve_")
            for name in ("conv1", "conv2", "conv3"):
                conv_dve(PQ[name])
                barrier(dve, "dve_")
            att_dve(PQ["att"])
            barrier(dve, "dve_")
            soft_dve()
            barrier(dve, "dve_")
            conv_dve(PQ["gat"])
            barrier(dve, "dve_")
            mlp_dve(PQ["mlp"])
            barrier(dve, "dve_")
            barrier(dve, "dve_")
            norm1_dve()
            barrier(dve, "dve_")
            msg_dve(PQ["msg"])
            barrier(dve, "dve_")
            norm2_dve()
            barrier(dve, "dve_")
            join_dve(PQ["join"])
            barrier(dve, "dve_")
            end_dve(DQ["source3"])
            barrier(dve, "dve_")
            conv_dve(PQ["hop1"])
            barrier(dve, "dve_")
            conv_dve(PQ["hop2"])
            barrier(dve, "dve_")
            end_dve(DQ["final"])
            barrier(dve, "dve_")
            copy_dve(PQ["put"])

        @block.tensor
        def _(pe):
            prepare_pe()
            barrier(pe, "pe")
            barrier(pe, "pe")
            barrier(pe, "pe")
            chain_pe(DQ["source"])
            barrier(pe, "pe")
            chain_pe(DQ["dense"])
            barrier(pe, "pe")
            for name in ("conv1", "conv2", "conv3"):
                conv_pe(PQ[name])
                barrier(pe, "pe")
            barrier(pe, "pe")
            soft_pe()
            barrier(pe, "pe")
            conv_pe(PQ["gat"])
            barrier(pe, "pe")
            mlp_pe(PQ["mlp"])
            barrier(pe, "pe")
            emlp_pe(PQ["emlp"])
            barrier(pe, "pe")
            norm1_pe()
            barrier(pe, "pe")
            msg_pe(PQ["msg"])
            barrier(pe, "pe")
            norm2_pe()
            barrier(pe, "pe")
            join_pe(PQ["join"])
            barrier(pe, "pe")
            end_pe(DQ["source3"])
            barrier(pe, "pe")
            conv_pe(PQ["hop1"])
            barrier(pe, "pe")
            conv_pe(PQ["hop2"])
            barrier(pe, "pe")
            end_pe(DQ["final"])
            barrier(pe, "pe")


def kernel(**inputs):
    import numpy as np
    import concourse.bacc as bacc
    from concourse.bass_utils import run_bass_kernel_spmd

    arrays = {k: np.ascontiguousarray(v) for k, v in inputs.items() if k not in ("src", "dst", "edge_attr_4")}
    src, dst, attr = (np.asarray(inputs[k]) for k in ("src", "dst", "edge_attr_4"))
    pad = EP - E
    lines = np.concatenate([np.full(1, -1, dst.dtype), dst, np.full(pad, N, dst.dtype), np.full(1, -1, dst.dtype)])
    arrays["dst_line"] = lines
    arrays["dst_cols"] = np.ascontiguousarray(lines[1:1 + EP].reshape(ET, P).T)
    arrays["src_cols"] = np.ascontiguousarray(np.concatenate([src, np.zeros(pad, src.dtype)]).reshape(ET, P).T)
    auxe = np.zeros((2 + DE, EP), attr.dtype)
    auxe[0, :E] = 1
    auxe[1, E:] = 1
    auxe[2:, :E] = attr.T
    arrays["auxe"] = auxe
    eye = np.eye(P, dtype=np.float32)
    arrays["ident"] = eye
    arrays["eye_row"] = np.ascontiguousarray(np.eye(D + 1, D, dtype=np.float32))
    arrays["cent"] = (np.eye(D) - 1.0 / D).astype(np.float32)
    arrays["avg"] = np.full((D, D), 1.0 / D, np.float32)
    slots = np.arange(EP, dtype=np.float32)
    arrays["own_cols"] = np.ascontiguousarray(slots.reshape(ET, P).T)
    own_rows = np.zeros((P, 2, P), np.float32)
    own_rows[:, 0] = slots.reshape(ET, P)[:P]
    own_rows[:ET - P, 1] = slots.reshape(ET, P)[P:]
    arrays["own_rows"] = own_rows
    nc = bacc.Bacc("TRN2", target_bir_lowering=False, num_devices=1)
    args = {}
    feed = {}
    for name, v in arrays.items():
        feed[f"in_{name}"] = v
        args[name] = nc.dram_tensor(f"in_{name}", v.shape, mybir.dt.from_np(v.dtype), kind="ExternalInput").ap()
    args["out"] = nc.dram_tensor("out_x", (N, D), F32, kind="ExternalOutput").ap()
    build(nc, args)
    r = run_bass_kernel_spmd(nc, [feed], core_ids=[0])
    return r.results[0]["out_x"]
```

```python
from contextlib import ExitStack

import concourse.bass as bass
from concourse import mybir

ALU = mybir.AluOpType
ACT = mybir.ActivationFunctionType
F32 = mybir.dt.float32
U8 = mybir.dt.uint8
I32 = mybir.dt.int32
AX_X = mybir.AxisListType.X
ds = bass.ds

P = 128
N, D = 100000, 96
E, DE = 25000, 4
ET = -(-E // P)
EP = ET * P
TG = 4
GW = TG * P
NJ = 7
NI = ET // (TG * NJ)
NG = NI * NJ
TI = TG * NJ
HALF = 4
CH = 4
CR = 4
DENSE1 = 2 * NI + 1
CHAIN_GAPS, END_GAPS = 7, 2
NSUB = 125
TURN = CH * CR * NSUB
STURN = CH * CR * P
ND = N // TURN
NL = -(-EP // STURN)
LR = NL * STURN
BIG = 1.0e30
EPS = 1e-5
SLOPE = 0.2
ENGINES = 5
START = 1
RB = [(0, P), (P, ET - P)]
assert ET == TI * NI and N == ND * TURN
(B_1, B_2, B_N, G_N, BE_N, G_E, BE_E, G_M, BE_M, A_N, S_N, A_E, S_E, A_M, S_M,
 NCOL) = range(16)


def build(nc, a):
    with ExitStack() as ctx:
        def sb(name, shape, dt=F32):
            return ctx.enter_context(nc.sbuf_tensor(name, shape, dt))

        def dram(name, shape, dt=F32):
            return nc.dram_tensor(name, shape, dt, kind="Internal").ap()

        sems = {}

        def sem(name):
            if name not in sems:
                sems[name] = ctx.enter_context(nc.semaphore(name))
            return sems[name]

        XS = dram("XS", (LR, D))
        XD = dram("XD", (EP, D))
        T = [None] + [dram(f"T{k}", (EP + LR, D)) for k in (1, 2, 3, 4, 5)]
        TN = dram("TN", (EP + P, D))
        GX = dram("GX", (EP, D))
        FR = dram("FR", (EP, D))
        TAB = dram("TAB", (N, 2))
        ACTV = dram("ACTV", (ND, TURN))
        X2T = dram("X2T", (D, N))
        X2L = dram("X2L", (D, LR))
        NDT = dram("NDT", (NG, D, 2, GW))
        AGG = dram("AGG", (NG, D, GW))
        LID = dram("LID", (EP,), U8)
        LINE = dram("LINE", (3, EP))
        CONT = dram("CONT", (ET,))

        ps = ctx.enter_context(nc.psum_tensor("ps", [P, 8, 512], F32))
        ZB, OB, DB = 0, 2, 4

        ident = sb("ident", [P, P])
        cent = sb("cent", [D, P])
        W = {k: sb(f"W{k}", [D + 1, P]) for k in "123GI"}
        WN = sb("WN", [D + 1, D])
        WE = sb("WE", [DE + 2, D])
        WM = sb("WM", [D, 3, P])
        WM3 = sb("WM3", [D, P])
        W3C = sb("W3C", [D + 1, P])
        AN = sb("AN", [D + 1, P])
        AM = sb("AM", [D, P])
        col = sb("col", [D, NCOL])
        wt = sb("wt", [D, 2, D + 1])
        att = sb("att", [D, 2])
        attB = sb("attB", [D, 2, P])
        uv = sb("uv", [P, 2, D])
        epsc = sb("epsc", [P, 2])
        ones = sb("ones", [P, P])
        zero = sb("zero", [P, 800])
        onesr = sb("onesr", [P, 2, P])
        nb2 = sb("nb2", [2, D])
        mb2 = sb("mb2", [2, P])
        sh2 = sb("sh2", [2, P])

        src_i = sb("src_i", [P, ET], I32)
        dst_i = sb("dst_i", [P, ET], I32)
        own = sb("own", [P, ET])
        lid = sb("lid", [P, ET])
        deg = sb("deg", [P, ET])
        isrep = sb("isrep", [P, ET])
        repf = sb("repf", [P, ET])
        wE = sb("wE", [P, ET])
        wS = sb("wS", [P, ET])
        one = sb("one", [P, ET])
        tmp = [sb(f"tmp{k}", [P, ET]) for k in range(4)]
        gs_i = sb("gs_i", [P, ET + TI], I32)
        gd_i = sb("gd_i", [P, ET + TI], I32)
        gi_i = sb("gi_i", [P, ET + TI], I32)
        gr_i = sb("gr_i", [P, ET + TI], I32)
        gn_i = sb("gn_i", [P, ET + TI], I32)
        go_i = sb("go_i", [P, ET + TI], I32)
        tabs = sb("tabs", [P, ET + TI, 2])
        stg = sb("stg", [P, 2, TI], I32)
        tabg = sb("tabg", [P, TI, 2])
        a_s = sb("a_s", [P, ET])
        a_d = sb("a_d", [P, ET])
        a_o = sb("a_o", [P, ET])
        dl_i = sb("dl_i", [P, 2, 3, P], I32)
        dl = sb("dl", [P, 2, 3, P])
        keepF = sb("keepF", [P, 2, P])
        keepB = sb("keepB", [P, 2, P])
        penF = sb("penF", [P, 2, P])
        penB = sb("penB", [P, 2, P])
        rv = [sb(f"rv{k}", [P, 2, P]) for k in range(8)]
        rcol = sb("rcol", [P, 2, 8])
        krow = sb("krow", [1, 4, ET])
        crow = sb("crow", [1, ET + 2])
        ownr = sb("ownr", [P, 2, P])
        lid_b = sb("lid_b", [P, 2, P], U8)
        lidB = sb("lidB", [P, EP], U8)
        contB = sb("contB", [P, ET])

        ringG = sb("ringG", [P, NJ, TG, D])
        ringS = sb("ringS", [P, NJ, TG, D])
        ringO = sb("ringO", [P, NJ, TG, D])
        Sm = sb("Sm", [P, 2, TG, P])
        Dg = sb("Dg", [P, 2, TG, P])
        cm = sb("cm", [D, TG, P])
        zT = sb("zT", [D + 1, 2, GW])
        yb = sb("yb", [P, 2, TG, D])
        st6 = sb("st6", [P, 2, TG, 6])
        mv = sb("mv", [P, 2, TG, 2])
        sdv = sb("sdv", [P, 2, TG])
        acc = sb("acc", [P, 2, TG, D])

        wx = sb("wx", [D, STURN])
        wh = sb("wh", [D + 1, STURN])
        wc = sb("wc", [P, STURN])
        wq = sb("wq", [P, STURN])
        w1 = sb("w1", [D + 1, STURN])
        w2 = sb("w2", [D + 1, STURN])
        xin = ringG[:].rearrange("p j t f -> p (j t f)")[:, 0:CH * GW]
        rows = ringS[:].rearrange("p j t f -> p (j t f)")[:, 0:CH * GW]
        dss = sb("dss", [P, CH, CR])
        dsd = sb("dsd", [P, CH, CR])
        drs = sb("drs", [P, CH, CR])
        dst6 = sb("dst6", [P, CH, CR, 6])
        dmv = sb("dmv", [P, CH, CR, 2])
        stN = sb("stN", [D, 2, ND * CH + NG])
        stE = sb("stE", [D, 2, NG])

        resR = sb("resR", [P, 2, TG, D])
        aux = sb("aux", [DE + 2, NJ, GW])

        bar = sem("all_engines")
        bars = {}

        def barrier(eng, key):
            bars[key] = bars.get(key, 0) + 1
            eng.drain().then_inc(bar, 1)
            eng.wait_ge(bar, ENGINES * bars[key])

        chains = {}

        def link(eng, key, ins):
            chains[key] = chains.get(key, 0) + 1
            ins.then_inc(sem(f"{key}_chain"), 1)
            eng.wait_ge(sem(f"{key}_chain"), chains[key])

        def spread(beside, i, turn, group):
            if beside is None:
                for j in range(NJ):
                    group(j)
                return
            p, first, m = beside["dense"], beside["first"], beside["turns"]
            gaps = m * p["gaps"]
            for k in range(m):
                def between(step, k=k):
                    for j in range(NJ):
                        if j * gaps // NJ == k * p["gaps"] + step:
                            group(j)
                turn(p, i * m + first + k, between)

        rows_bank = ps[:, OB].rearrange("p (t f) -> p t f", t=TG)[:, :, 0:D]
        PASSES = {}
        order = []

        def start_of(w):
            return 0 if w in {f"g{j}" for j in range(NJ)} else START

        def add_pass(name, signals="", credit=0, staged=0, slots=(0, 0, 0, 0, 0), **k):
            uses = {w: NG for w in signals.split()}
            if "z" in uses:
                uses["z"] = TG * NG
            if "seg" in uses:
                uses["seg"] += credit
            uses["staged"] = staged
            for c, n in zip("gmsro", slots):
                for j in range(NJ):
                    uses[f"{c}{j}"] = 16 * n * NI
            names = sorted(set(uses) | {"S", "D", "seg", "mask", "z", "cv", "th", "y", "st", "mv", "sq", "rc", "out", "u"})
            k["uses"] = uses
            k["base"] = {w: start_of(w) + sum(PASSES[q]["uses"].get(w, 0) for q in order) for w in names}
            k.setdefault("ngather", 1)
            k.setdefault("own", False)
            k.setdefault("tail", None)
            k.setdefault("beside", None)
            ends = k["beside"] and k["beside"]["dense"]["gaps"] == END_GAPS
            k["dense_sp"], k["dense_pe"], k["dense_act"], k["dense_dve"] = (
                (end_sp_turn, end_pe_turn, end_act_turn, end_dve_turn) if ends else
                (chain_sp_turn, chain_pe_turn, chain_act_turn, chain_dve_turn))
            PASSES[name] = k
            order.append(name)

        def S(name):
            return sem("e_" + name)

        def at(p, name, v):
            return v + p["base"][name]

        def before(i, j):
            return i * NJ + max(j - 1, 0)

        def table_rows(t, g, row0=0):
            return t[row0:row0 + EP].rearrange("(g t p) f -> g p t f", t=TG, p=P)[g]

        def load_group(p, sp, i, j):
            g = i * NJ + j
            if p.get("m"):
                sp.dma_start(ringG[:, j], table_rows(p["m"], g)).then_inc(S(f"m{j}"), 16)
            if p.get("s"):
                sp.dma_start(ringS[:, j], table_rows(p["s"], g)).then_inc(S(f"s{j}"), 16)

        def res_of(p, j):
            return resR[:, j % 2] if p.get("r") else ringS[:, j]

        def conv_sp(p):
            def store(i, j):
                sp.wait_ge(S("out"), at(p, "out", i * NJ + j + 1))
                sp.nop(nofuse=True)
                sp.dma_start(table_rows(p["out"], i * NJ + j), ringO[:, j]).then_inc(S(f"o{j}"), 16)

            def load_res(i, j):
                if p.get("r"):
                    sp.wait_ge(S("y"), at(p, "y", before(i, j)))
                    sp.nop(nofuse=True)
                    sp.dma_start(resR[:, j % 2], table_rows(p["r"], i * NJ + j)).then_inc(S(f"r{j}"), 16)

            sp = nc.sync
            for j in range(NJ):
                load_group(p, sp, 0, j)

            def turn(i, last):
                def group(j):
                    if j + 1 < NJ:
                        load_res(i, j + 1)
                    store(i, j)
                    if not last:
                        load_group(p, sp, i + 1, j)
                load_res(i, 0)
                spread(p["beside"], i, p["dense_sp"], group)
            with sp.Fori(0, NI - 1) as i:
                turn(i, False)
            turn(NI - 1, True)
            for j in range(NJ):
                sp.wait_ge(S(f"o{j}"), at(p, f"o{j}", 16 * NI))

        def gather_pool(p, rings, tables):
            pool = nc.gpsimd
            with pool.Fori(0, NI) as i:
                for j in range(NJ):
                    pool.wait_ge(S("staged"), at(p, "staged", 2 * i + (1 if j < HALF else 2)))
                    pool.nop(nofuse=True)
                    if p["kind"] in ("copy", "att"):
                        pool.wait_ge(S(f"o{j}"), at(p, f"o{j}", i * (16 * p["ngather"])))
                        pool.nop(nofuse=True)
                    else:
                        pool.wait_ge(S("seg"), at(p, "seg", i * NJ + j + 1))
                        pool.nop(nofuse=True)
                    for k, (ring, table) in enumerate(zip(rings, tables)):
                        for t in range(TG):
                            pool.indirect_dma_start(
                                ring[:, j, t, :], None, table,
                                bass.IndirectOffsetOnAxis(ap=stg[:, k, TG * j + t:TG * j + t + 1], axis=0)).then_inc(S(f"g{j}"), 16)

        def stage(p, i, half):
            lo, hi = (0, HALF * TG) if half == 0 else (HALF * TG, TI)
            idx = p["gather"]
            for k, g in enumerate(idx):
                ins = nc.vector.tensor_copy(stg[:, k, lo:hi], g[:, ds(i * TI + lo, hi - lo)])
            ins.then_inc(S("staged"), 1)

        def stage_after(p, i, half):
            js = range(HALF) if half == 0 else range(HALF, NJ)
            for j in js:
                nc.vector.wait_ge(S(f"g{j}"), at(p, f"g{j}", (i + 1) * (16 * TG * p.get("ngather", 1))))
            stage(p, i + 1, half)

        def build_S(p, i, j, w):
            dve = nc.vector
            dve.wait_ge(S("seg"), at(p, "seg", before(i, j) + NJ))
            for t in range(TG):
                tile = (i * NJ + j) * TG + t
                ins = dve.tensor_scalar(Sm[:, j % 2, t], lidB[:, ds(tile * P, P)], lid[:, ds(tile, 1)],
                                        w[:, ds(tile, 1)], ALU.is_equal, ALU.mult)
            ins.then_inc(S("S"), 1)

        def add_carry(p, i, j):
            dve = nc.vector
            g = i * NJ + j
            dve.wait_ge(S("z"), at(p, "z", g * TG))
            dve.tensor_tensor(
                cm[:], lidB[0:D, ds(g * GW, GW)].rearrange("p (t e) -> p t e", t=TG),
                contB[0:D, ds(g * TG, TG)].unsqueeze(2).to_broadcast([D, TG, P]), ALU.is_equal).then_inc(S("mask"), 1)
            dve.wait_ge(S("mask"), at(p, "mask", g + 1))
            dve.wait_ge(S("seg"), at(p, "seg", g + 1 + NJ))
            dve.wait_ge(S("cv"), at(p, "cv", before(i, j)))
            b = j % 2
            for t in range(TG):
                if t:
                    dve.wait_ge(S("z"), at(p, "z", g * TG + t))
                before_ = zT[0:D, b, t * P - 1:t * P] if t else zT[0:D, (b + 1) % 2 if j else 0, GW - 1:GW]
                dve.scalar_tensor_tensor(
                    out=zT[0:D, b, t * P:(t + 1) * P], in0=cm[:, t], scalar=before_,
                    in1=ps[0:D, ZB + b, t * P:(t + 1) * P], op0=ALU.mult, op1=ALU.add).then_inc(S("z"), 1)

        def ln_sum(p, i, j):
            dve = nc.vector
            b, g = j % 2, i * NJ + j
            o = rows_bank
            if p["tail"] == "tanh":
                dve.wait_ge(S("th"), at(p, "th", g + 1))
            else:
                dve.wait_ge(S("cv"), at(p, "cv", g + 1))
            if p.get("r"):
                dve.wait_ge(S(f"r{j}"), at(p, f"r{j}", (i + 1) * 16))
            if p.get("s"):
                dve.wait_ge(S(f"s{j}"), at(p, f"s{j}", (i + 1) * 16))
            if p["tail"] == "tanh":
                dve.tensor_tensor(yb[:, b], yb[:, b], res_of(p, j), ALU.add).then_inc(S("y"), 1)
            elif p["tail"] == "ln":
                dve.tensor_tensor(yb[:, b], o, res_of(p, j), ALU.add).then_inc(S("y"), 1)
            elif p["tail"] == "copy":
                dve.tensor_copy(yb[:, b], o).then_inc(S("y"), 1)
            else:
                dve.scalar_tensor_tensor(out=ringS[:, j], in0=resR[:, b], scalar=0.5,
                                                in1=ringS[:, j], op0=ALU.mult, op1=ALU.add).then_inc(S("u"), 1)
                dve.wait_ge(S("u"), at(p, "u", g + 1))
                dve.scalar_tensor_tensor(out=yb[:, b], in0=o, scalar=0.5, in1=ringS[:, j],
                                                op0=ALU.mult, op1=ALU.add).then_inc(S("y"), 1)
            dve.wait_ge(S("y"), at(p, "y", g + 1))
            for t in range(TG):
                ins = dve.bn_stats(st6[:, b, t], yb[:, b, t])
            ins.then_inc(S("st"), 1)
            dve.wait_ge(S("st"), at(p, "st", g + 1))
            dve.nop(nofuse=True)
            for t in range(TG):
                ins = dve.bn_aggr(mv[:, b, t], st6[:, b, t])
            ins.then_inc(S("mv"), 1)

        def ln_scale(p, i, j):
            dve = nc.vector
            b, g = j % 2, i * NJ + j
            dve.wait_ge(S("sq"), at(p, "sq", g + 1))
            dve.reciprocal(sdv[:, b], sdv[:, b]).then_inc(S("rc"), 1)
            dve.wait_ge(S("rc"), at(p, "rc", g + 1))
            dve.wait_ge(S(f"o{j}"), at(p, f"o{j}", i * 16))
            for t in range(TG):
                ins = dve.tensor_scalar(ringO[:, j, t], yb[:, b, t], mv[:, b, t, 0:1], sdv[:, b, t:t + 1],
                                        ALU.subtract, ALU.mult)
            ins.then_inc(S("out"), 1)

        def conv_dve(p):
            dve = nc.vector
            link(dve, "dve", dve.memset(zT[0:D], 0.0))
            if p.get("gather"):
                stage(p, 0, 0)
                stage(p, 0, 1)
            ln = p["tail"] != "relu" and p["tail"] != "plain"
            with dve.Fori(0, NI) as i:
                def group(j):
                    if j + 1 < NJ:
                        build_S(p, i, j + 1, p["w"])
                    add_carry(p, i, j)
                    if p.get("gather") and j == HALF:
                        stage_after(p, i, 0)
                    if ln and j:
                        ln_scale(p, i, j - 1)
                    if ln:
                        ln_sum(p, i, j)
                build_S(p, i, 0, p["w"])
                spread(p["beside"], i, p["dense_dve"], group)
                if p.get("gather"):
                    stage_after(p, i, 1)
                if ln:
                    ln_scale(p, i, NJ - 1)

        def conv_pe(p):
            pe = nc.tensor
            pe.sem_inc(S("seg"), NJ)
            rhs = p["W"]

            def seg(i, j):
                g, b = i * NJ + j, j % 2
                pe.wait_ge(S("S"), at(p, "S", g + 1))
                if p.get("m"):
                    pe.wait_ge(S(f"m{j}"), at(p, f"m{j}", (i + 1) * 16))
                else:
                    pe.wait_ge(S(f"g{j}"), at(p, f"g{j}", (i + 1) * (16 * TG)))
                if p["own"]:
                    pe.wait_ge(S(f"s{j}"), at(p, f"s{j}", (i + 1) * 16))
                    pe.wait_ge(S("D"), at(p, "D", g + 1))
                pe.wait_ge(S("z"), at(p, "z", before(i, j) * TG))
                for t in range(TG):
                    o = ps[0:D, ZB + b, t * P:(t + 1) * P]
                    ins = pe.matmul(o, ringG[:, j, t], Sm[:, b, t], start=True, stop=not p["own"])
                    if p["own"]:
                        ins = pe.matmul(o, ringS[:, j, t], Dg[:, b, t], start=False, stop=True)
                ins.then_inc(S("seg"), 1)

            def rows_(i, j):
                g, b = i * NJ + j, j % 2
                pe.wait_ge(S("z"), at(p, "z", (g + 1) * TG))
                pe.wait_ge(S("out" if p["tail"] in ("relu", "plain") else "th" if p["tail"] == "tanh" else "y"), at(p, "out" if p["tail"] in ("relu", "plain") else "th" if p["tail"] == "tanh" else "y", g))
                for t in range(TG):
                    ins = pe.matmul(ps[:, OB, t * P:(t + 1) * P], zT[:, b, t * P:(t + 1) * P], rhs[:],
                                    start=True, stop=True)
                ins.then_inc(S("cv"), 1)

            with pe.Fori(0, NI) as i:
                def group(j):
                    if j + 1 < NJ:
                        seg(i, j + 1)
                    rows_(i, j)
                seg(i, 0)
                spread(p["beside"], i, p["dense_pe"], group)

        def conv_act(p):
            act = nc.scalar
            o = rows_bank

            def diag(i, j):
                act.wait_ge(S("seg"), at(p, "seg", before(i, j) + NJ))
                for t in range(TG):
                    tile = (i * NJ + j) * TG + t
                    ins = act.activation(Dg[:, j % 2, t], ident[:], ACT.Copy, scale=wS[:, ds(tile, 1)])
                ins.then_inc(S("D"), 1)

            def tail(i, j):
                g, b = i * NJ + j, j % 2
                if p["tail"] in ("relu", "plain"):
                    act.wait_ge(S("cv"), at(p, "cv", g + 1))
                    act.wait_ge(S(f"o{j}"), at(p, f"o{j}", i * 16))
                    act.activation(ringO[:, j], o,
                                          ACT.Relu if p["tail"] == "relu" else ACT.Copy).then_inc(S("out"), 1)
                elif p["tail"] == "tanh":
                    act.wait_ge(S("cv"), at(p, "cv", g + 1))
                    act.wait_ge(S("out"), at(p, "out", before(i, j)))
                    act.activation(yb[:, b], o, ACT.Tanh).then_inc(S("th"), 1)

            def root(i, j):
                act.wait_ge(S("mv"), at(p, "mv", i * NJ + j + 1))
                act.activation(sdv[:, j % 2], mv[:, j % 2, :, 1], ACT.Sqrt, bias=epsc[:, 0:1]).then_inc(S("sq"), 1)

            ln = p["tail"] not in ("relu", "plain")
            with act.Fori(0, NI) as i:
                def group(j):
                    if p["own"] and j + 1 < NJ:
                        diag(i, j + 1)
                    tail(i, j)
                    if ln:
                        root(i, j)
                if p["own"]:
                    diag(i, 0)
                spread(p["beside"], i, p["dense_act"], group)

        nscan = {"dve": 0, "pe": 0}
        nmove = {"dve": 0, "pe": 0}

        def scan_dve(outv, data, keep, keep_row, fwd, summed=True):
            dve = nc.vector
            k = nscan["dve"] = nscan["dve"] + 1
            op0, op1 = (ALU.mult, ALU.add) if summed else (ALU.add, ALU.max)
            init = 0.0 if summed else -BIG
            f = (lambda ap: ap) if fwd else (lambda ap: ap[:, ::-1])
            for b, (_, n) in enumerate(RB):
                ins = dve.tensor_tensor_scan(f(outv[0:n, b]), f(keep[0:n, b]), f(data[0:n, b]), init, op0, op1)
            ins.then_inc(sem("scan_tile"), 1)
            dve.wait_ge(sem("scan_last"), k)
            link(dve, "dve", dve.memset(crow[:], init))
            to = crow[0:1, 1:ET + 1]
            dve.tensor_tensor_scan(f(to), f(keep_row), f(ps[0:1, ZB, 0:ET]), init, op0, op1).then_inc(sem("scan_row"), 1)
            dve.wait_ge(sem("scan_carry"), k)
            for b, (_, n) in enumerate(RB):
                link(dve, "dve", dve.tensor_copy(rcol[0:n, b, 0:1], ps[0:n, ZB + 1, 8 * b:8 * b + 1]))
            for b, (_, n) in enumerate(RB):
                link(dve, "dve", dve.tensor_tensor_scan(f(outv[0:n, b]), f(keep[0:n, b]), f(data[0:n, b]),
                                                        rcol[0:n, b, 0:1], op0, op1))

        def scan_pe(outv, fwd):
            pe = nc.tensor
            k = nscan["pe"] = nscan["pe"] + 1
            pe.wait_ge(sem("scan_tile"), k)
            c = P - 1 if fwd else 0
            for b, (t0, n) in enumerate(RB):
                ins = pe.transpose(ps[0:1, ZB, t0:t0 + n], outv[0:n, b, c:c + 1], ident[0:n, 0:n])
            ins.then_inc(sem("scan_last"), 1)
            pe.wait_ge(sem("scan_row"), k)
            off = 0 if fwd else 2
            for b, (t0, n) in enumerate(RB):
                ins = pe.matmul(ps[0:n, ZB + 1, 8 * b:8 * b + 1], crow[0:1, off + t0:off + t0 + n],
                                ones[0:1, 0:1], start=True, stop=True)
            ins.then_inc(sem("scan_carry"), 1)

        def to_cols_dve(dst):
            dve = nc.vector
            k = nmove["dve"] = nmove["dve"] + 1
            dve.sem_inc(sem("move_ready"), 1)
            dve.wait_ge(sem("move_done"), k)
            link(dve, "dve", dve.tensor_copy(dst[:, 0:ET], ps[:, OB, 0:ET]))

        def to_cols_pe(srcv):
            pe = nc.tensor
            k = nmove["pe"] = nmove["pe"] + 1
            pe.wait_ge(sem("move_ready"), k)
            for b, (t0, n) in enumerate(RB):
                ins = pe.transpose(ps[:, OB, t0:t0 + n], srcv[0:n, b], ident[0:n, 0:n])
            ins.then_inc(sem("move_done"), 1)

        def to_rows_dve(dst):
            dve = nc.vector
            k = nmove["dve"] = nmove["dve"] + 1
            dve.sem_inc(sem("move_ready"), 1)
            dve.wait_ge(sem("move_done"), k)
            for b, (_, n) in enumerate(RB):
                link(dve, "dve", dve.tensor_copy(dst[0:n, b], ps[0:n, OB, b * P:(b + 1) * P]))

        def to_rows_pe(srcv):
            pe = nc.tensor
            k = nmove["pe"] = nmove["pe"] + 1
            pe.wait_ge(sem("move_ready"), k)
            for b, (t0, n) in enumerate(RB):
                ins = pe.transpose(ps[0:n, OB, b * P:(b + 1) * P], srcv[:, t0:t0 + n], ident[:])
            ins.then_inc(sem("move_done"), 1)

        def blocks(fn):
            for b, (_, n) in enumerate(RB):
                link(nc.vector, "dve", fn(n, b))


        def copy_sp(p):
            sp = nc.sync
            with sp.Fori(0, NI) as i:
                def group(j):
                    sp.wait_ge(S(f"g{j}"), at(p, f"g{j}", (i + 1) * (16 * TG * p["ngather"])))
                    sp.nop(nofuse=True)
                    for ring, t in zip((ringG, ringS), p["to"]):
                        sp.dma_start(table_rows(t, i * NJ + j), ring[:, j]).then_inc(S(f"o{j}"), 16)
                spread(p["beside"], i, p["dense_sp"], group)
            for j in range(NJ):
                sp.wait_ge(S(f"o{j}"), at(p, f"o{j}", 16 * NI * p["ngather"]))

        def copy_dve(p):
            stage(p, 0, 0)
            stage(p, 0, 1)
            with nc.vector.Fori(0, NI) as i:
                def group(j):
                    if j == HALF:
                        stage_after(p, i, 0)
                spread(p["beside"], i, p["dense_dve"], group)
                stage_after(p, i, 1)

        def copy_pe(p):
            with nc.tensor.Fori(0, NI) as i:
                spread(p["beside"], i, p["dense_pe"], nothing)

        def copy_act(p):
            with nc.scalar.Fori(0, NI) as i:
                spread(p["beside"], i, p["dense_act"], nothing)

        def att_sp(p):
            sp = nc.sync
            for j in range(NJ):
                load_group(p, sp, 0, j)

            def turn(i, last):
                def group(j):
                    sp.wait_ge(S("out"), at(p, "out", i * NJ + j + 1))
                    sp.nop(nofuse=True)
                    sp.dma_start(table_rows(GX, i * NJ + j), ringG[:, j]).then_inc(S(f"o{j}"), 16)
                    if not last:
                        load_group(p, sp, i + 1, j)
                spread(p["beside"], i, p["dense_sp"], group)
            with sp.Fori(0, NI - 1) as i:
                turn(i, False)
            turn(NI - 1, True)
            for j in range(NJ):
                sp.wait_ge(S(f"o{j}"), at(p, f"o{j}", 16 * NI))

        def att_dve(p):
            dve = nc.vector
            stage(p, 0, 0)
            stage(p, 0, 1)
            with dve.Fori(0, NI) as i:
                def group(j):
                    g = i * NJ + j
                    dve.wait_ge(S(f"g{j}"), at(p, f"g{j}", (i + 1) * (16 * TG)))
                    dve.wait_ge(S(f"s{j}"), at(p, f"s{j}", (i + 1) * 16))
                    dve.wait_ge(S("out"), at(p, "out", g))
                    for k, (ring, v) in enumerate(((ringG, 0), (ringS, 0), (ringS, 1))):
                        ins = dve.tensor_tensor(att3[:, k], ring[:, j], uv[:, v:v + 1].to_broadcast([P, TG, D]), ALU.mult)
                    ins.then_inc(S("y"), 1)
                    dve.wait_ge(S("y"), at(p, "y", g + 1))
                    for k, dst in enumerate((a_s, a_o, a_d)):
                        ins = dve.tensor_reduce(dst[:, ds(g * TG, TG)], att3[:, k], AX_X, ALU.add)
                    ins.then_inc(S("out"), 1)
                    if j == HALF:
                        stage_after(p, i, 0)
                spread(p["beside"], i, p["dense_dve"], group)
                stage_after(p, i, 1)

        att3 = ringO[:, 0:3]

        def mlp_sp(p):
            sp = nc.sync

            def load(i, j):
                g = i * NJ + j
                sp.dma_start(aux[0:2, j], LINE[1:3].rearrange("r (g e) -> g r e", e=GW)[g]).then_inc(S(f"m{j}"), 16)
            for j in range(NJ):
                load_group(dict(p, m=None), sp, 0, j)
                load(0, j)

            def turn(i, last):
                for j in range(NJ):
                    sp.wait_ge(S("out"), at(p, "out", i * NJ + j + 1))
                    sp.nop(nofuse=True)
                    sp.dma_start(NDT[i * NJ + j], ndt(j % 2)).then_inc(S(f"o{j}"), 16)
                    if not last:
                        load_group(dict(p, m=None), sp, i + 1, j)
                        load(i + 1, j)
            with sp.Fori(0, NI - 1) as i:
                turn(i, False)
            turn(NI - 1, True)
            for j in range(NJ):
                sp.wait_ge(S(f"o{j}"), at(p, f"o{j}", 16 * NI))

        def ndt(b):
            return (wc, wq)[b][0:D, 0:2 * GW].rearrange("p (k e) -> p k e", k=2)

        def mlp_pe(p):
            pe = nc.tensor
            with pe.Fori(0, NI) as i:
                for j in range(NJ):
                    g = i * NJ + j
                    pe.wait_ge(S(f"s{j}"), at(p, f"s{j}", (i + 1) * 16))
                    pe.wait_ge(S(f"m{j}"), at(p, f"m{j}", (i + 1) * 16))
                    pe.wait_ge(S("y"), at(p, "y", g))
                    for t in range(TG):
                        ins = pe.transpose(ps[0:D, DB, t * P:(t + 1) * P], ringS[:, j, t], ident[:])
                    ins.then_inc(S("seg"), 1)
                    pe.wait_ge(S("y"), at(p, "y", g + 1))
                    pe.wait_ge(S("th"), at(p, "th", g))
                    pe.matmul(ps[0:D, DB + 1, 0:GW], WN[0:D], ndt(j % 2)[:, 0], start=True, stop=False)
                    pe.matmul(ps[0:D, DB + 1, 0:GW], nb2[:], aux[0:2, j], start=False, stop=True).then_inc(S("cv"), 1)

        def mlp_dve(p):
            dve = nc.vector
            with dve.Fori(0, NI) as i:
                for j in range(NJ):
                    g = i * NJ + j
                    dve.wait_ge(S("seg"), at(p, "seg", g + 1))
                    if j > 1:
                        dve.wait_ge(S(f"o{j - 2}"), at(p, f"o{j - 2}", (i + 1) * 16))
                    else:
                        dve.wait_ge(S(f"o{NJ - 1 - j}"), at(p, f"o{NJ - 1 - j}", i * 16))
                        if j:
                            dve.wait_ge(S(f"o{NJ - 1}"), at(p, f"o{NJ - 1}", i * 16))
                    dve.tensor_copy(ndt(j % 2)[:, 0], ps[0:D, DB, 0:GW]).then_inc(S("y"), 1)

        def mlp_act(p):
            act = nc.scalar
            with act.Fori(0, NI) as i:
                for j in range(NJ):
                    g = i * NJ + j
                    act.wait_ge(S("cv"), at(p, "cv", g + 1))
                    h = ndt(j % 2)[:, 1]
                    act.wait_ge(S("out"), at(p, "out", g))
                    act.activation(h, ps[0:D, DB + 1, 0:GW], ACT.Relu,
                                          accum_out=stN[:, 0, ds(g + ND * CH, 1)]).then_inc(S("th"), 1)
                    act.wait_ge(S("th"), at(p, "th", g + 1))
                    act.activation(wh[0:D, 0:GW], h, ACT.Square,
                                          accum_out=stN[:, 1, ds(g + ND * CH, 1)]).then_inc(S("out"), 1)

        def emlp_sp(p):
            sp = nc.sync

            def load(i, j):
                sp.dma_start(aux[:, j], a["auxe"].rearrange("r (g e) -> g r e", e=GW)[i * NJ + j]).then_inc(S(f"m{j}"), 16)
            for j in range(NJ):
                load(0, j)
            with sp.Fori(0, NI - 1) as i:
                for j in range(NJ):
                    sp.wait_ge(S("cv"), at(p, "cv", i * NJ + j + 1))
                    sp.nop(nofuse=True)
                    load(i + 1, j)

        def emlp_pe(p):
            pe = nc.tensor
            with pe.Fori(0, NI) as i:
                for j in range(NJ):
                    g = i * NJ + j
                    pe.wait_ge(S(f"m{j}"), at(p, f"m{j}", (i + 1) * 16))
                    pe.wait_ge(S("th"), at(p, "th", before(i, j)))
                    pe.matmul(ps[0:D, DB + j % 2, 0:GW], WE[:], aux[:, j], start=True, stop=True).then_inc(S("cv"), 1)

        def emlp_act(p):
            act = nc.scalar
            with act.Fori(0, NI) as i:
                for j in range(NJ):
                    g = i * NJ + j
                    act.wait_ge(S("cv"), at(p, "cv", g + 1))
                    act.wait_ge(S("out"), at(p, "out", g))
                    act.activation(wh[0:D, 0:GW], ps[0:D, DB + j % 2, 0:GW], ACT.Relu,
                                          accum_out=stE[:, 0, ds(g, 1)]).then_inc(S("th"), 1)
                    act.wait_ge(S("th"), at(p, "th", g + 1))
                    act.activation(wh[0:D, 0:GW], wh[0:D, 0:GW], ACT.Square,
                                          accum_out=stE[:, 1, ds(g, 1)]).then_inc(S("out"), 1)

        xsT, xdT, heT = wc[0:D, 0:GW], wc[0:D, GW:2 * GW], wc[0:D, 2 * GW:3 * GW]

        def msg_sp(p):
            sp = nc.sync

            def load(i, j):
                sp.dma_start(aux[:, j], a["auxe"].rearrange("r (g e) -> g r e", e=GW)[i * NJ + j]).then_inc(S(f"m{j}"), 16)
            for j in range(NJ):
                load(0, j)

            def turn(i, last):
                for j in range(NJ):
                    g = i * NJ + j
                    sp.wait_ge(S("z"), at(p, "z", (g + 1) * TG))
                    sp.nop(nofuse=True)
                    sp.dma_start(AGG[g], zT[0:D, j % 2]).then_inc(S(f"o{j}"), 16)
                    if not last:
                        load(i + 1, j)
            with sp.Fori(0, NI - 1) as i:
                turn(i, False)
            turn(NI - 1, True)
            for j in range(NJ):
                sp.wait_ge(S(f"o{j}"), at(p, f"o{j}", 16 * NI))

        def msg_pe(p):
            pe = nc.tensor
            pe.sem_inc(S("seg"), NJ)

            def turned(i, j):
                g = i * NJ + j
                pe.wait_ge(S(f"g{j}"), at(p, f"g{j}", (i + 1) * (16 * TG * 2)))
                pe.wait_ge(S(f"m{j}"), at(p, f"m{j}", (i + 1) * 16))
                pe.wait_ge(S("y"), at(p, "y", g))
                pe.wait_ge(S("th"), at(p, "th", g))
                for t in range(TG):
                    pe.transpose(ps[0:D, DB, t * P:(t + 1) * P], ringG[:, j, t], ident[:])
                for t in range(TG):
                    pe.transpose(ps[0:D, DB + 1, t * P:(t + 1) * P], ringS[:, j, t], ident[:])
                pe.matmul(ps[0:D, DB + 2, 0:GW], WE[:], aux[:, j], start=True, stop=True).then_inc(S("D"), 1)

            def message(i, j):
                g = i * NJ + j
                pe.wait_ge(S("y"), at(p, "y", g + 1))
                pe.wait_ge(S("th"), at(p, "th", g + 1))
                pe.wait_ge(S("u"), at(p, "u", g))
                for t in range(TG):
                    o = ps[:, OB, t * P:(t + 1) * P]
                    e = slice(t * P, (t + 1) * P)
                    pe.matmul(o, xsT[:, e], WM[:, 0], start=True, stop=False)
                    pe.matmul(o, xdT[:, e], WM[:, 1], start=False, stop=False)
                    pe.matmul(o, heT[:, e], WM3[:], start=False, stop=False)
                    ins = pe.matmul(o, aux[0:2, j, e], mb2[:], start=False, stop=True)
                ins.then_inc(S("cv"), 1)

            def seg(i, j):
                g, b = i * NJ + j, j % 2
                pe.wait_ge(S("S"), at(p, "S", g + 1))
                pe.wait_ge(S("u"), at(p, "u", g + 1))
                pe.wait_ge(S("z"), at(p, "z", before(i, j) * TG))
                for t in range(TG):
                    ins = pe.matmul(ps[0:D, ZB + b, t * P:(t + 1) * P], ringO[:, j, t], Sm[:, b, t],
                                    start=True, stop=True)
                ins.then_inc(S("seg"), 1)

            with pe.Fori(0, NI) as i:
                for j in range(NJ):
                    turned(i, j)
                    message(i, j)
                    seg(i, j)

        def msg_act(p):
            act = nc.scalar
            with act.Fori(0, NI) as i:
                for j in range(NJ):
                    g = i * NJ + j
                    act.wait_ge(S("D"), at(p, "D", g + 1))
                    act.wait_ge(S("cv"), at(p, "cv", g))
                    act.activation(xdT, ps[0:D, DB + 1, 0:GW], ACT.Copy)
                    act.activation(heT, ps[0:D, DB + 2, 0:GW], ACT.Relu).then_inc(S("th"), 1)
                    act.wait_ge(S("cv"), at(p, "cv", g + 1))
                    act.wait_ge(S("seg"), at(p, "seg", g + 1))
                    act.wait_ge(S("out"), at(p, "out", g))
                    act.activation(ringO[:, j], rows_bank, ACT.Relu).then_inc(S("u"), 1)
                    act.wait_ge(S("u"), at(p, "u", g + 1))
                    act.activation(yb[:, 0].rearrange("p t f -> p (t f)"),
                                          ringO[:, j].rearrange("p t f -> p (t f)"), ACT.Square).then_inc(S("sq"), 1)

        def msg_dve(p):
            dve = nc.vector
            link(dve, "dve", dve.memset(zT[0:D], 0.0))
            link(dve, "dve", dve.memset(acc[:], 0.0))
            stage(p, 0, 0)
            stage(p, 0, 1)
            with dve.Fori(0, NI) as i:
                for j in range(NJ):
                    g = i * NJ + j
                    build_S(p, i, j, one)
                    dve.wait_ge(S("D"), at(p, "D", g + 1))
                    dve.wait_ge(S("cv"), at(p, "cv", g))
                    dve.tensor_copy(xsT, ps[0:D, DB, 0:GW]).then_inc(S("y"), 1)
                    dve.wait_ge(S("u"), at(p, "u", g + 1))
                    dve.wait_ge(S("out"), at(p, "out", g))
                    dve.tensor_tensor(acc[:, 0], acc[:, 0], ringO[:, j], ALU.add)
                    dve.wait_ge(S("sq"), at(p, "sq", g + 1))
                    dve.tensor_tensor(acc[:, 1], acc[:, 1], yb[:, 0], ALU.add).then_inc(S("out"), 1)
                    if j > 1:
                        dve.wait_ge(S(f"o{j - 2}"), at(p, f"o{j - 2}", (i + 1) * 16))
                    else:
                        dve.wait_ge(S(f"o{NJ - 1 - j}"), at(p, f"o{NJ - 1 - j}", i * 16))
                        if j:
                            dve.wait_ge(S(f"o{NJ - 1}"), at(p, f"o{NJ - 1}", i * 16))
                    add_carry(dict(p, nocv=True), i, j)
                    if j == HALF:
                        stage_after(p, i, 0)
                stage_after(p, i, 1)

        def join_buf(b):
            return (wc, wq)[b][0:D, 0:3 * GW].rearrange("p (k e) -> p k e", k=3)

        def join_sp(p):
            sp = nc.sync

            def load(i, j):
                g = i * NJ + j
                sp.wait_ge(S("cv"), at(p, "cv", before(i, j)))
                sp.nop(nofuse=True)
                sp.dma_start(join_buf(j % 2)[:, 0:2], NDT[g]).then_inc(S(f"m{j}"), 16)
                sp.dma_start(join_buf(j % 2)[:, 2], AGG[g]).then_inc(S(f"r{j}"), 16)
                sp.dma_start(aux[0:2, j], LINE[0:2].rearrange("r (g e) -> g r e", e=GW)[g]).then_inc(S(f"s{j}"), 16)
            with sp.Fori(0, NI) as i:
                load(i, 0)
                for j in range(NJ):
                    if j + 1 < NJ:
                        load(i, j + 1)
                    sp.wait_ge(S("out"), at(p, "out", i * NJ + j + 1))
                    sp.nop(nofuse=True)
                    sp.dma_start(table_rows(T[5], i * NJ + j), ringO[:, j]).then_inc(S(f"o{j}"), 16)
            for j in range(NJ):
                sp.wait_ge(S(f"o{j}"), at(p, f"o{j}", 16 * NI))

        def join_pe(p):
            pe = nc.tensor
            with pe.Fori(0, NI) as i:
                for j in range(NJ):
                    g = i * NJ + j
                    for r in "mrs":
                        pe.wait_ge(S(f"{r}{j}"), at(p, f"{r}{j}", (i + 1) * 16))
                    pe.wait_ge(S("y"), at(p, "y", g))
                    for t in range(TG):
                        o = ps[:, OB, t * P:(t + 1) * P]
                        e = slice(t * P, (t + 1) * P)
                        pe.matmul(o, join_buf(j % 2)[:, 0, e], cent[:], start=True, stop=False)
                        pe.matmul(o, join_buf(j % 2)[:, 1, e], AN[0:D], start=False, stop=False)
                        pe.matmul(o, join_buf(j % 2)[:, 2, e], AM[:], start=False, stop=False)
                        ins = pe.matmul(o, aux[0:2, j, e], sh2[:], start=False, stop=True)
                    ins.then_inc(S("cv"), 1)

        def join_dve(p):
            with nc.vector.Fori(0, NI) as i:
                for j in range(NJ):
                    ln_sum(p, i, j)
                    ln_scale(p, i, j)

        def put_sp(p):
            sp = nc.sync
            for j in range(NJ):
                load_group(p, sp, 0, j)
            with sp.Fori(0, NI - 1) as i:
                for j in range(NJ):
                    sp.wait_ge(S(f"g{j}"), at(p, f"g{j}", (i + 1) * (16 * TG)))
                    sp.nop(nofuse=True)
                    load_group(p, sp, i + 1, j)

        def put_pool(p):
            pool = nc.gpsimd
            with pool.Fori(0, NI) as i:
                for j in range(NJ):
                    pool.wait_ge(S("staged"), at(p, "staged", 2 * i + (1 if j < HALF else 2)))
                    pool.nop(nofuse=True)
                    pool.wait_ge(S(f"s{j}"), at(p, f"s{j}", (i + 1) * 16))
                    pool.nop(nofuse=True)
                    for t in range(TG):
                        pool.indirect_dma_start(
                            a["out"], bass.IndirectOffsetOnAxis(ap=stg[:, 0, TG * j + t:TG * j + t + 1], axis=0),
                            ringS[:, j, t, :], None, bounds_check=N - 1, oob_is_err=False).then_inc(S(f"g{j}"), 16)
            for j in range(NJ):
                pool.wait_ge(S(f"g{j}"), at(p, f"g{j}", 16 * TG * NI))

        def tab_put_dve(p):
            dve = nc.vector
            dve.tensor_copy(tabg[:], tabs[:, 0:TI, :])
            dve.tensor_copy(stg[:, 0], go_i[:, 0:TI]).then_inc(S("staged"), 1)
            with dve.Fori(0, NI - 1) as i:
                for j in range(NJ):
                    dve.wait_ge(S(f"g{j}"), at(p, f"g{j}", (i + 1) * (16 * TG)))
                dve.tensor_copy(tabg[:], tabs[:, ds((i + 1) * TI, TI), :])
                dve.tensor_copy(stg[:, 0], go_i[:, ds((i + 1) * TI, TI)]).then_inc(S("staged"), 1)

        def tab_put_pool(p):
            pool = nc.gpsimd
            with pool.Fori(0, NI) as i:
                pool.wait_ge(S("staged"), at(p, "staged", i + 1))
                pool.nop(nofuse=True)
                for j in range(NJ):
                    for t in range(j * TG, (j + 1) * TG):
                        pool.indirect_dma_start(
                            TAB, bass.IndirectOffsetOnAxis(ap=stg[:, 0, t:t + 1], axis=0), tabg[:, t, :], None,
                            bounds_check=N - 1, oob_is_err=False).then_inc(S(f"g{j}"), 16)
            for j in range(NJ):
                pool.wait_ge(S(f"g{j}"), at(p, f"g{j}", 16 * TG * NI))

        def tab_get_dve(p):
            dve = nc.vector
            dve.tensor_copy(stg[:, 0], gs_i[:, 0:TI]).then_inc(S("staged"), 1)
            with dve.Fori(0, NI) as i:
                for j in range(NJ):
                    dve.wait_ge(S(f"g{j}"), at(p, f"g{j}", (i + 1) * (16 * TG)))
                dve.tensor_copy(tabs[:, ds(i * TI, TI), :], tabg[:])
                dve.tensor_copy(stg[:, 0], gs_i[:, ds((i + 1) * TI, TI)]).then_inc(S("staged"), 1)
            link(dve, "dve", dve.drain())

        def tab_get_pool(p):
            pool = nc.gpsimd
            with pool.Fori(0, NI) as i:
                pool.wait_ge(S("staged"), at(p, "staged", i + 1))
                pool.nop(nofuse=True)
                for j in range(NJ):
                    for t in range(j * TG, (j + 1) * TG):
                        pool.indirect_dma_start(
                            tabg[:, t, :], None, TAB,
                            bass.IndirectOffsetOnAxis(ap=stg[:, 0, t:t + 1], axis=0)).then_inc(S(f"g{j}"), 16)

        DENSE, dorder = {}, []

        def add_dense(name, signals, **k):
            n = CH * k["turns"]
            uses = {w: n for w in signals.split()}
            for w in ("tp", "ev"):
                if w in uses:
                    uses[w] = 2 * n
            uses[k["last"]] += CH
            for c in range(CH):
                for w, m in k["slots"].items():
                    uses[f"{w}{c}"] = 16 * m * k["turns"]
            k.setdefault("t0", 0)
            names = sorted(set(uses) | {f"{w}{c}" for w in DENSE_DMA.split() for c in range(CH)} | set(CHAIN.split()))
            k["uses"] = uses
            k["base"] = {w: START + sum(DENSE[q]["uses"].get(w, 0) for q in dorder) for w in names}
            DENSE[name] = k
            dorder.append(name)

        def R(name):
            return sem("d_" + name)

        def dat(p, name, v):
            return v + p["base"][name] + (CH if name == p["last"] else 0)

        def block_rows(t, p, i, c, row0=0):
            n = p["all"] * p["turn"]
            return t[row0:row0 + n].rearrange("(i c q r) f -> i c q (r f)", c=CH, q=p["sub"], r=CR)[i + p["t0"], c]

        def cols(buf, p, c, rows_=D):
            w = p["turn"] // CH
            return buf[0:rows_, c * w:(c + 1) * w]

        def part(buf, p, c, q, rows_=D):
            if p["natural"]:
                w = p["turn"] // CH
                return buf[0:rows_, c * w + q:(c + 1) * w:CR]
            return buf[0:rows_, c * p["turn"] // CH + q * p["sub"]:c * p["turn"] // CH + (q + 1) * p["sub"]]

        def rowbuf(buf, p, c):
            return buf[0:p["sub"], c * GW:c * GW + CR * D].rearrange("p (q f) -> p q f", q=CR)

        def flat(buf, p, c):
            return buf[0:p["sub"], c * GW:c * GW + CR * D]

        def bank(p, c):
            return ps[0:D, DB + c, 0:CR * p["sub"]]

        def bank_rows(p, c):
            return ps[0:p["sub"], DB + c].rearrange("p (q f) -> p q f", q=CR)[:, :, 0:D]

        def small(buf, p, c):
            return buf[0:p["sub"], c]

        def nothing(step):
            pass

        def is_last(p, i):
            return isinstance(i, int) and i == p["turns"] - 1

        def columns(t, p, i, c):
            w = p["turn"] // CH
            return t[:, ds((i + p["t0"]) * p["turn"] + c * w, w)]

        def load_chain(p, i, c):
            if p["rows_in"]:
                nc.sync.dma_start(flat(xin, p, c), block_rows(p["x"], p, i, c)).then_inc(R(f"ld{c}"), 16)
            else:
                nc.sync.dma_start(cols(wx, p, c), columns(p["x"], p, i, c)).then_inc(R(f"ld{c}"), 16)

        def load_mask(p, i, c):
            w = p["turn"] // CH
            nc.sync.dma_start(w2[D:D + 1, c * w:(c + 1) * w],
                              ACTV[ds(i + p["t0"], 1), c * w:(c + 1) * w]).then_inc(R(f"mk{c}"), 16)

        def chain_sp_start(p):
            for c in range(CH):
                load_chain(p, 0, c)
                if not p["rows_in"]:
                    load_mask(p, 0, c)

        def chain_sp_turn(p, i, between):
            sp = nc.sync
            last = is_last(p, i)
            for step in range(3):
                between(step)
            if p["rows_in"]:
                for c in range(CH):
                    sp.wait_ge(R("tr"), dat(p, "tr", i * CH + c + 1))
                    sp.nop(nofuse=True)
                    if not last:
                        load_chain(p, i + 1, c)
                for s in range(2):
                    for c in range(CH):
                        sp.wait_ge(R("ev"), dat(p, "ev", i * (2 * CH) + s * CH + c + 1))
                        sp.nop(nofuse=True)
                        sp.dma_start(block_rows(T[s + 1], p, i, c, EP), flat(rows, p, c)).then_inc(R(f"ro{c}"), 16)
                for c in range(CH):
                    sp.wait_ge(R("x1"), dat(p, "x1", i * CH + c + 1))
                    sp.nop(nofuse=True)
                    sp.dma_start(block_rows(T[3], p, i, c, EP), flat(wc, p, c)).then_inc(R(f"rp{c}"), 16)
                for c in range(CH):
                    sp.wait_ge(R("x2"), dat(p, "x2", i * CH + c + 1))
                    sp.nop(nofuse=True)
                    sp.dma_start(block_rows(T[4], p, i, c, EP), flat(wq, p, c)).then_inc(R(f"rq{c}"), 16)
            elif not last:
                for c in range(CH):
                    sp.wait_ge(R("p3"), dat(p, "p3", i * CH + c + 1))
                    sp.nop(nofuse=True)
                    load_chain(p, i + 1, c)
            between(3)
            between(4)
            for c in range(CH):
                sp.wait_ge(R("c2"), dat(p, "c2", i * CH + c + 1))
                sp.nop(nofuse=True)
                sp.dma_start(columns(p["to"], p, i, c), cols(w2, p, c)).then_inc(R(f"o{c}"), 16)
            between(5)
            if not p["rows_in"] and not last:
                for c in range(CH):
                    sp.wait_ge(R("pn"), dat(p, "pn", i * CH + c + 1))
                    sp.nop(nofuse=True)
                    load_mask(p, i + 1, c)
            between(6)

        def chain_sp(p, first=0):
            sp = nc.sync
            if first == 0:
                chain_sp_start(p)
            if p["turns"] - 1 > first:
                with sp.Fori(first, p["turns"] - 1) as i:
                    chain_sp_turn(p, i, nothing)
            if first < p["turns"]:
                chain_sp_turn(p, p["turns"] - 1, nothing)
            for c in range(CH):
                sp.wait_ge(R(f"o{c}"), dat(p, f"o{c}", 16 * p["turns"]))
                if p["rows_in"]:
                    sp.wait_ge(R(f"ro{c}"), dat(p, f"ro{c}", 32 * p["turns"]))
                    sp.wait_ge(R(f"rp{c}"), dat(p, f"rp{c}", 16 * p["turns"]))
                    sp.wait_ge(R(f"rq{c}"), dat(p, f"rq{c}", 16 * p["turns"]))

        def dense_pe_start(p):
            nc.tensor.sem_inc(R(p["last"]), CH)

        def chain_pe_turn(p, i, between):
            pe = nc.tensor
            n = p["sub"]

            def put_rows(s, c, i):
                e = i * (2 * CH) + s * CH + c
                k = (s * CH + c) % 2
                pe.wait_ge(R("ev"), dat(p, "ev", e if (s * CH + c) == 0 else e - 1))
                for q in range(CR):
                    ins = pe.transpose(ps[0:n, ZB + k, q * D:(q + 1) * D], part(wh, p, c, q), ident[0:D, 0:D])
                ins.then_inc(R("tp"), 1)

            if p["rows_in"]:
                for c in range(CH):
                    pe.wait_ge(R(f"ld{c}"), dat(p, f"ld{c}", (i + 1) * 16))
                    pe.wait_ge(R(p["last"]), dat(p, p["last"], i * CH + c + 1 - CH))
                    for q in range(CR):
                        ins = pe.transpose(ps[0:D, DB + c, q * n:(q + 1) * n],
                                           rowbuf(xin, p, c)[:, q], ident[0:n, 0:n])
                    ins.then_inc(R("tr"), 1)
            for c in range(CH):
                if p["rows_in"]:
                    pe.wait_ge(R("x0"), dat(p, "x0", i * CH + c + 1))
                else:
                    pe.wait_ge(R(f"ld{c}"), dat(p, f"ld{c}", (i + 1) * 16))
                    pe.wait_ge(R(p["last"]), dat(p, p["last"], i * CH + c + 1 - CH))
                pe.matmul(bank(p, c), W["1"][0:D, 0:D], cols(wx, p, c), start=True, stop=True).then_inc(R("p1"), 1)
            between(0)
            for c in range(CH):
                pe.wait_ge(R("h1"), dat(p, "h1", i * CH + c + 1))
                if p["rows_in"]:
                    put_rows(0, c, i)
                pe.matmul(bank(p, c), W["2"][0:D, 0:D], cols(wh, p, c), start=True, stop=True).then_inc(R("p2"), 1)
            between(1)
            for c in range(CH):
                pe.wait_ge(R("h2"), dat(p, "h2", i * CH + c + 1))
                if p["rows_in"]:
                    put_rows(1, c, i)
                for q in range(CR):
                    o = ps[0:n, DB + c, q * P:(q + 1) * P]
                    pe.matmul(o, part(wx, p, c, q), cent[:], start=True, stop=False)
                    ins = pe.matmul(o, part(wh, p, c, q, D + 1), W3C[:], start=False, stop=True)
                ins.then_inc(R("p3"), 1)
            between(2)
            for c in range(CH):
                pe.wait_ge(R("x1"), dat(p, "x1", i * CH + c + 1))
                for q in range(CR):
                    ins = pe.transpose(ps[0:D, DB + c, q * n:(q + 1) * n], rowbuf(wc, p, c)[:, q], ident[0:n, 0:n])
                ins.then_inc(R("t1"), 1)
            between(3)
            for c in range(CH):
                pe.wait_ge(R("e1"), dat(p, "e1", i * CH + c + 1))
                for q in range(CR):
                    ins = pe.matmul(ps[0:n, DB + c, q * P:(q + 1) * P],
                                    w1[:, c * CR * n + q * n:c * CR * n + (q + 1) * n], W["G"][:],
                                    start=True, stop=True)
                ins.then_inc(R("pg"), 1)
            between(4)
            for c in range(CH):
                pe.wait_ge(R("x2"), dat(p, "x2", i * CH + c + 1))
                for q in range(CR):
                    ins = pe.transpose(ps[0:D, DB + c, q * n:(q + 1) * n], rowbuf(wq, p, c)[:, q], ident[0:n, 0:n])
                ins.then_inc(R("t2"), 1)
            between(5)
            if not p["rows_in"]:
                for c in range(CH):
                    pe.wait_ge(R("c2"), dat(p, "c2", i * CH + c + 1))
                    pe.wait_ge(R(f"mk{c}"), dat(p, f"mk{c}", (i + 1) * 16))
                    pe.matmul(bank(p, c), WN[:], cols(w2, p, c, D + 1), start=True, stop=True).then_inc(R("pn"), 1)
            between(6)

        def chain_pe(p, first=0):
            if first == 0:
                dense_pe_start(p)
            with nc.tensor.Fori(first, p["turns"]) as i:
                chain_pe_turn(p, i, nothing)

        def chain_act_turn(p, i, between):
            act = nc.scalar

            def evict(s, i):
                for c in range(CH):
                    act.wait_ge(R("tp"), dat(p, "tp", i * (2 * CH) + s * CH + c + 1))
                    act.wait_ge(R(f"ro{c}"), dat(p, f"ro{c}", i * 32 + 16 * s))
                    act.activation(flat(rows, p, c), ps[0:p["sub"], ZB + c % 2, 0:CR * D], ACT.Copy).then_inc(R("ev"), 1)

            for c in range(CH):
                act.wait_ge(R("p1"), dat(p, "p1", i * CH + c + 1))
                if not p["rows_in"]:
                    act.wait_ge(R("qn"), dat(p, "qn", i * CH))
                act.activation(cols(wh, p, c), bank(p, c), ACT.Relu, bias=col[:, B_1:B_1 + 1]).then_inc(R("h1"), 1)
            between(0)
            if p["rows_in"]:
                evict(0, i)
                evict(1, i)
            between(1)
            for c in range(CH):
                act.wait_ge(R("p3"), dat(p, "p3", i * CH + c + 1))
                if p["rows_in"]:
                    act.wait_ge(R(f"rq{c}"), dat(p, f"rq{c}", i * 16))
                act.activation(rowbuf(wq, p, c), bank_rows(p, c), ACT.Square).then_inc(R("q1"), 1)
            for c in range(CH):
                act.wait_ge(R("s1"), dat(p, "s1", i * CH + c + 1))
                act.activation(small(dsd, p, c), small(dss, p, c), ACT.Sqrt, bias=epsc[0:p["sub"], 0:1],
                               scale=1.0 / D).then_inc(R("d1"), 1)
            between(2)
            for c in range(CH):
                act.wait_ge(R("t1"), dat(p, "t1", i * CH + c + 1))
                w = CR * p["sub"]
                act.activation(w1[0:D, c * w:(c + 1) * w], bank(p, c), ACT.Copy).then_inc(R("e1"), 1)
            between(3)
            for c in range(CH):
                act.wait_ge(R("pg"), dat(p, "pg", i * CH + c + 1))
                act.activation(rowbuf(wq, p, c), bank_rows(p, c), ACT.Tanh).then_inc(R("th"), 1)
            for c in range(CH):
                act.wait_ge(R("mv"), dat(p, "mv", i * CH + c + 1))
                act.activation(small(dsd, p, c), dmv[0:p["sub"], c, :, 1], ACT.Sqrt,
                               bias=epsc[0:p["sub"], 0:1]).then_inc(R("d2"), 1)
            between(4)
            between(5)
            if not p["rows_in"]:
                for c in range(CH):
                    g = (i + p["t0"]) * CH + c
                    act.wait_ge(R("pn"), dat(p, "pn", i * CH + c + 1))
                    act.activation(cols(wh, p, c), bank(p, c), ACT.Relu, bias=col[:, B_N:B_N + 1],
                                   accum_out=stN[:, 0, ds(g, 1)]).then_inc(R("rn"), 1)
                for c in range(CH):
                    g = (i + p["t0"]) * CH + c
                    act.wait_ge(R("rn"), dat(p, "rn", i * CH + c + 1))
                    act.activation(cols(wh, p, c), cols(wh, p, c), ACT.Square,
                                   accum_out=stN[:, 1, ds(g, 1)]).then_inc(R("qn"), 1)
            between(6)

        def chain_act(p, first=0):
            with nc.scalar.Fori(first, p["turns"]) as i:
                chain_act_turn(p, i, nothing)

        def over_row(ap, p):
            return ap.unsqueeze(2).to_broadcast([p["sub"], CR, D])

        def chain_dve_turn(p, i, between):
            dve = nc.vector
            if p["rows_in"]:
                for c in range(CH):
                    dve.wait_ge(R("tr"), dat(p, "tr", i * CH + c + 1))
                    dve.tensor_copy(cols(wx, p, c), bank(p, c)).then_inc(R("x0"), 1)
            between(0)
            for c in range(CH):
                dve.wait_ge(R("p2"), dat(p, "p2", i * CH + c + 1))
                dve.tensor_scalar(cols(wh, p, c), bank(p, c), col[:, B_2:B_2 + 1], 0.0, ALU.add, ALU.max).then_inc(R("h2"), 1)
            between(1)
            for c in range(CH):
                dve.wait_ge(R("q1"), dat(p, "q1", i * CH + c + 1))
                dve.tensor_reduce(small(dss, p, c), rowbuf(wq, p, c), AX_X, ALU.add).then_inc(R("s1"), 1)
            for c in range(CH):
                dve.wait_ge(R("d1"), dat(p, "d1", i * CH + c + 1))
                dve.reciprocal(small(drs, p, c), small(dsd, p, c)).then_inc(R("r1"), 1)
                dve.wait_ge(R("r1"), dat(p, "r1", i * CH + c + 1))
                if p["rows_in"]:
                    dve.wait_ge(R(f"rp{c}"), dat(p, f"rp{c}", i * 16))
                dve.tensor_tensor(rowbuf(wc, p, c), bank_rows(p, c), over_row(small(drs, p, c), p),
                                  ALU.mult).then_inc(R("x1"), 1)
            between(2)
            between(3)
            for c in range(CH):
                dve.wait_ge(R("th"), dat(p, "th", i * CH + c + 1))
                dve.tensor_tensor(rowbuf(wq, p, c), rowbuf(wq, p, c), rowbuf(wc, p, c), ALU.add).then_inc(R("y"), 1)
                dve.wait_ge(R("y"), dat(p, "y", i * CH + c + 1))
                for q in range(CR):
                    ins = dve.bn_stats(dst6[0:p["sub"], c, q], rowbuf(wq, p, c)[:, q])
                ins.then_inc(R("st"), 1)
                dve.wait_ge(R("st"), dat(p, "st", i * CH + c + 1))
                dve.nop(nofuse=True)
                for q in range(CR):
                    ins = dve.bn_aggr(dmv[0:p["sub"], c, q], dst6[0:p["sub"], c, q])
                ins.then_inc(R("mv"), 1)
            for c in range(CH):
                dve.wait_ge(R("d2"), dat(p, "d2", i * CH + c + 1))
                dve.reciprocal(small(drs, p, c), small(dsd, p, c)).then_inc(R("r2"), 1)
                dve.wait_ge(R("r2"), dat(p, "r2", i * CH + c + 1))
                for q in range(CR):
                    ins = dve.tensor_scalar(rowbuf(wq, p, c)[:, q], rowbuf(wq, p, c)[:, q],
                                            dmv[0:p["sub"], c, q, 0:1], drs[0:p["sub"], c, q:q + 1],
                                            ALU.subtract, ALU.mult)
                ins.then_inc(R("x2"), 1)
            between(4)
            for c in range(CH):
                dve.wait_ge(R("t2"), dat(p, "t2", i * CH + c + 1))
                dve.wait_ge(R(f"o{c}"), dat(p, f"o{c}", i * 16))
                dve.tensor_copy(cols(w2, p, c), bank(p, c)).then_inc(R("c2"), 1)
            between(5)
            between(6)

        def chain_dve(p, first=0):
            with nc.vector.Fori(first, p["turns"]) as i:
                chain_dve_turn(p, i, nothing)

        def load_end(p, i, c):
            nc.sync.dma_start(cols(w2, p, c), columns(p["x"], p, i, c)).then_inc(R(f"ld{c}"), 16)

        def end_sp_start(p):
            for c in range(CH):
                load_end(p, 0, c)

        def end_sp_turn(p, i, between):
            sp = nc.sync
            between(0)
            for c in range(CH):
                sp.wait_ge(R("p3"), dat(p, "p3", i * CH + c + 1))
                sp.nop(nofuse=True)
                if not is_last(p, i):
                    load_end(p, i + 1, c)
            for c in range(CH):
                sp.wait_ge(R("y"), dat(p, "y", i * CH + c + 1))
                sp.nop(nofuse=True)
                sp.dma_start(block_rows(p["to"], p, i, c, p["row0"]), flat(wc, p, c)).then_inc(R(f"ro{c}"), 16)
            between(1)

        def end_sp(p, first=0):
            sp = nc.sync
            if first == 0:
                end_sp_start(p)
            if p["turns"] - 1 > first:
                with sp.Fori(first, p["turns"] - 1) as i:
                    end_sp_turn(p, i, nothing)
            end_sp_turn(p, p["turns"] - 1, nothing)
            for c in range(CH):
                sp.wait_ge(R(f"ro{c}"), dat(p, f"ro{c}", 16 * p["turns"]))

        def end_pe_turn(p, i, between):
            pe = nc.tensor
            for c in range(CH):
                pe.wait_ge(R(f"ld{c}"), dat(p, f"ld{c}", (i + 1) * 16))
                pe.wait_ge(R("y"), dat(p, "y", i * CH + c + 1 - CH))
                pe.matmul(bank(p, c), WN[0:D], cols(w2, p, c), start=True, stop=True).then_inc(R("pn"), 1)
            between(0)
            for c in range(CH):
                pe.wait_ge(R("rn"), dat(p, "rn", i * CH + c + 1))
                for q in range(CR):
                    o = ps[0:p["sub"], DB + c, q * P:(q + 1) * P]
                    pe.matmul(o, part(w2, p, c, q), cent[:], start=True, stop=False)
                    ins = pe.matmul(o, part(wh, p, c, q, D + 1), AN[:], start=False, stop=True)
                ins.then_inc(R("p3"), 1)
            between(1)

        def end_pe(p, first=0):
            if first == 0:
                dense_pe_start(p)
            with nc.tensor.Fori(first, p["turns"]) as i:
                end_pe_turn(p, i, nothing)

        def end_act_turn(p, i, between):
            act = nc.scalar
            sc, bi = (1.0, 0) if p["row0"] else (1.0 + EPS, 1)
            for c in range(CH):
                act.wait_ge(R("pn"), dat(p, "pn", i * CH + c + 1))
                act.activation(cols(wh, p, c), bank(p, c), ACT.Relu, bias=col[:, B_N:B_N + 1]).then_inc(R("rn"), 1)
            between(0)
            for c in range(CH):
                act.wait_ge(R("p3"), dat(p, "p3", i * CH + c + 1))
                act.activation(rowbuf(wq, p, c), bank_rows(p, c), ACT.Square).then_inc(R("q1"), 1)
            for c in range(CH):
                act.wait_ge(R("s1"), dat(p, "s1", i * CH + c + 1))
                act.activation(small(dsd, p, c), small(dss, p, c), ACT.Sqrt, bias=epsc[0:p["sub"], bi:bi + 1],
                               scale=sc / D).then_inc(R("d1"), 1)
            between(1)

        def end_act(p, first=0):
            with nc.scalar.Fori(first, p["turns"]) as i:
                end_act_turn(p, i, nothing)

        def end_dve_turn(p, i, between):
            dve = nc.vector
            between(0)
            for c in range(CH):
                dve.wait_ge(R("q1"), dat(p, "q1", i * CH + c + 1))
                dve.tensor_reduce(small(dss, p, c), rowbuf(wq, p, c), AX_X, ALU.add).then_inc(R("s1"), 1)
            for c in range(CH):
                dve.wait_ge(R("d1"), dat(p, "d1", i * CH + c + 1))
                dve.reciprocal(small(drs, p, c), small(dsd, p, c)).then_inc(R("r1"), 1)
                dve.wait_ge(R("r1"), dat(p, "r1", i * CH + c + 1))
                dve.wait_ge(R(f"ro{c}"), dat(p, f"ro{c}", i * 16))
                dve.tensor_tensor(rowbuf(wc, p, c), bank_rows(p, c), over_row(small(drs, p, c), p),
                                  ALU.mult).then_inc(R("y"), 1)
            between(1)

        def end_dve(p, first=0):
            with nc.vector.Fori(first, p["turns"]) as i:
                end_dve_turn(p, i, nothing)

        def norm_dve(k, s, q, count, g, b, ac, sc):
            dve = nc.vector
            t = tmp[0][0:D]
            link(dve, "dve", dve.tensor_scalar(t[:, 0:1], s, 1.0 / count, None, ALU.mult))
            link(dve, "dve", dve.tensor_scalar(t[:, 1:2], q, 1.0 / count, None, ALU.mult))
            link(dve, "dve", dve.tensor_tensor(t[:, 2:3], t[:, 0:1], t[:, 0:1], ALU.mult))
            dve.tensor_tensor(t[:, 3:4], t[:, 1:2], t[:, 2:3], ALU.subtract).then_inc(sem("norm_var"), 1)
            dve.wait_ge(sem("norm_root"), k)
            link(dve, "dve", dve.reciprocal(t[:, 5:6], t[:, 4:5]))
            link(dve, "dve", dve.tensor_tensor(col[:, ac:ac + 1], col[:, g:g + 1], t[:, 5:6], ALU.mult))
            link(dve, "dve", dve.tensor_tensor(t[:, 6:7], t[:, 0:1], col[:, ac:ac + 1], ALU.mult))
            link(dve, "dve", dve.tensor_tensor(col[:, sc:sc + 1], col[:, b:b + 1], t[:, 6:7], ALU.subtract))

        def norm_act(k):
            act = nc.scalar
            act.wait_ge(sem("norm_var"), k)
            act.activation(tmp[0][0:D, 4:5], tmp[0][0:D, 3:4], ACT.Sqrt, bias=epsc[0:D, 0:1]).then_inc(sem("norm_root"), 1)

        CHAIN = "tr x0 p1 h1 p2 h2 p3 q1 s1 d1 r1 x1 t1 e1 pg th y st mv d2 r2 x2 t2 c2 pn rn qn tp ev"
        DENSE_DMA = "ld mk o ro rp rq"
        chain_sig = "p1 h1 p2 h2 p3 q1 s1 d1 r1 x1 t1 e1 pg th y st mv d2 r2 x2 t2 c2"
        end_sig = "pn rn p3 q1 s1 d1 r1 y"
        side = dict(turns=NL, all=NL, turn=STURN, sub=P, natural=False)
        nodes = dict(all=ND, turn=TURN, sub=NSUB, natural=False, x=a["xT"], to=X2T, rows_in=False, last="rn",
                     slots=dict(ld=1, o=1, mk=1), gaps=CHAIN_GAPS)
        add_dense("dense1", chain_sig + " pn rn qn", turns=DENSE1, **nodes)
        add_dense("source", chain_sig + " tr x0 tp ev", x=XS, to=X2L, rows_in=True, last="c2",
                  slots=dict(ld=1, o=1, ro=2, rp=1, rq=1), gaps=CHAIN_GAPS, **side)
        add_dense("dense2", chain_sig + " pn rn qn", turns=ND - DENSE1, t0=DENSE1, **nodes)
        add_dense("source3", end_sig, x=X2L, to=T[5], row0=EP, last="y", slots=dict(ld=1, ro=1), gaps=END_GAPS,
                  **side)
        add_dense("final", end_sig, x=X2T, to=a["out"], row0=0, last="y", slots=dict(ld=1, ro=1), gaps=END_GAPS,
                  turns=ND, all=ND, turn=TURN, sub=NSUB, natural=True)
        PQ, DQ = PASSES, DENSE

        def beside(name, first, m):
            return dict(dense=DQ[name], first=first, turns=m)
        ln_sig = "S seg mask z cv out y st mv sq rc "
        GS = 2 + 2 * NI
        add_pass("tab_put", kind="tab", staged=NI, slots=(TG, 0, 0, 0, 0))
        add_pass("tab_get", kind="tab", staged=NI + 1, slots=(TG, 0, 0, 0, 0))
        add_pass("copy", kind="copy", gather=(gs_i, gd_i), ngather=2, to=(XS, XD), staged=GS,
                 slots=(2 * TG, 0, 0, 0, 2), beside=beside("dense1", 0, 2))
        add_pass("conv1", "S D seg mask z cv out", NJ, slots=(0, 1, 1, 0, 1), kind="conv", m=XS, s=XD, own=True,
                 w=wE, W=W["1"], tail="relu", out=T[1], beside=beside("dense2", 0 * NI, 1))
        add_pass("conv2", "S D seg mask z cv out", NJ, GS, slots=(TG, 0, 1, 0, 1), kind="conv", gather=(gi_i,),
                 table=T[1], s=T[1], own=True, w=wE, W=W["2"], tail="relu", out=T[2], beside=beside("dense2", 1 * NI, 1))
        add_pass("conv3", ln_sig + "D", NJ, GS, slots=(TG, 0, 1, 1, 1), kind="conv", gather=(gi_i,),
                 table=T[2], s=T[2], r=XD, own=True, w=wE, W=W["3"], tail="ln", out=T[3], beside=beside("dense2", 2 * NI, 1))
        add_pass("att", "y out", 0, GS, slots=(TG, 0, 1, 0, 1), kind="att", gather=(gi_i,), s=T[3], beside=beside("dense2", 3 * NI, 1))
        add_pass("gat", ln_sig + "D th", NJ, slots=(0, 1, 1, 0, 1), kind="conv", m=GX, s=T[3], own=True,
                 w=wE, W=W["G"], tail="tanh", out=T[4], beside=beside("dense2", 4 * NI, 1))
        add_pass("mlp", "seg y cv th out", slots=(0, 1, 1, 0, 1), kind="mlp", s=T[4])
        add_pass("emlp", "cv th out", slots=(0, 1, 0, 0, 0), kind="emlp")
        add_pass("msg", "S D seg mask z cv y th u sq out", NJ, GS, slots=(2 * TG, 1, 0, 0, 1), kind="msg",
                 gather=(gi_i, gr_i), ngather=2)
        add_pass("join", "cv y st mv sq rc out", slots=(0, 1, 1, 1, 1), kind="join", tail="copy")
        add_pass("hop1", "S seg mask z cv out", NJ, GS, slots=(TG, 0, 0, 0, 1), kind="conv", gather=(gi_i,),
                 table=T[5], w=wE, W=W["I"], tail="plain", out=TN, beside=beside("final", 0, 4))
        add_pass("hop2", ln_sig + "u", NJ, GS, slots=(TG, 0, 1, 1, 1), kind="conv", gather=(gn_i,),
                 table=TN, s=T[5], r=TN, w=wE, W=W["I"], tail="half", out=FR, beside=beside("final", 4 * NI, 3))
        add_pass("put", staged=GS, slots=(TG, 0, 1, 0, 0), kind="put", gather=(go_i,), s=FR)
        loaded = sem("loaded")
        n_loads = [0]

        def prepare_sp():
            sp = nc.sync
            sp.wait_ge(sem("cleared"), 1)

            def ld(dst, src):
                n_loads[0] += 1
                sp.dma_start(dst, src).then_inc(loaded, 16)
            r = lambda v: a[v].rearrange("(o f) -> o f", o=1)
            c = lambda v: a[v].rearrange("(f o) -> f o", o=1)
            ld(ident[:], a["ident"])
            ld(cent[:], a["cent"])
            for k, wn, bn in (("1", "L0_gnn_W1", "L0_gnn_b1"), ("2", "L0_gnn_W2", "L0_gnn_b2"),
                              ("3", "L0_gnn_W3", "L0_gnn_b3"), ("G", "L1_gnn_W", "L1_gnn_bias")):
                ld(W[k][0:D, 0:D], a[wn])
                ld(W[k][D:D + 1, 0:D], r(bn))
            ld(W["I"][:, 0:D], a["eye_row"])
            ld(WN[0:D], a["L2_gnn_W_node"])
            ld(WE[2:2 + DE], a["L2_gnn_W_edge"])
            ld(WE[0:1], r("L2_gnn_b_edge"))
            ld(WM[:, :, 0:D], a["L2_gnn_W_msg"].rearrange("(k f) n -> f k n", k=3))
            ld(nb2[0:1], r("L2_gnn_b_node"))
            ld(mb2[0:1, 0:D], r("L2_gnn_b_msg"))
            for k, v in ((B_1, "L0_gnn_b1"), (B_2, "L0_gnn_b2"), 
                         (B_N, "L2_gnn_b_node"), (G_N, "L2_gnn_g_node"),
                         (BE_N, "L2_gnn_beta_node"), (G_E, "L2_gnn_g_edge"), (BE_E, "L2_gnn_beta_edge"),
                         (G_M, "L2_gnn_g_msg"), (BE_M, "L2_gnn_beta_msg")):
                ld(col[:, k:k + 1], c(v))
            ld(att[:, 0:1], c("L1_gnn_att_src"))
            ld(att[:, 1:2], c("L1_gnn_att_dst"))
            ld(src_i[:], a["src_cols"])
            ld(dst_i[:], a["dst_cols"])
            ld(own[:], a["own_cols"])
            ld(ownr[:], a["own_rows"])
            for b, (t0, n) in enumerate(RB):
                for k in range(3):
                    ld(dl_i[0:n, b, k], a["dst_line"][k + t0 * P:k + (t0 + n) * P].rearrange("(t e) -> t e", e=P))
            for h in (0, 1):
                r0, nr = EP + h * (LR - EP) // 2, (LR - EP) // 2
                ld(XS[r0:r0 + nr].rearrange("(p a) f -> p (a f)", p=P), zero[:, 0:nr // P * D])
            for h in range(2):
                ld(TAB[h * N // 2:(h + 1) * N // 2].rearrange("(p a) f -> p (a f)", p=125), zero[0:125, 0:800])
            ld(TN[EP:EP + P], zero[:, 0:D])
            sp.wait_ge(loaded, 16 * n_loads[0])
            sp.sem_inc(sem("ready"), 1)
            sp.wait_ge(sem("lines"), 1)
            m = 0
            for b, (t0, n) in enumerate(RB):
                v = lambda t: t[t0 * P:(t0 + n) * P].rearrange("(t e) -> t e", e=P)
                for dst, src in ((v(LID), lid_b[0:n, b]), (v(LINE[0]), rv[5][0:n, b]), (v(LINE[1]), onesr[0:n, b]),
                                 (v(LINE[2]), rv[2][0:n, b]),
                                 (CONT[t0:t0 + n].rearrange("(t o) -> t o", o=1), rcol[0:n, b, 6:7])):
                    sp.dma_start(dst, src).then_inc(sem("lined"), 16)
                    m += 16
            sp.wait_ge(sem("lined"), m)
            sp.dma_start(lidB[:], LID.rearrange("(o e) -> o e", o=1).to_broadcast([P, EP])).then_inc(sem("lined"), 16)
            sp.dma_start(contB[:], CONT.rearrange("(o e) -> o e", o=1).to_broadcast([P, ET])).then_inc(sem("lined"), 16)
            sp.wait_ge(sem("lined"), m + 32)

        def prepare_dve():
            dve = nc.vector
            for t, v in ((ones, 1.0), (onesr, 1.0), (one, 1.0), (zero, 0.0), (WE, 0.0), (nb2, -BIG), (mb2, -BIG),
                         (zT, 1.0), (gs_i, 0), (gd_i, 0), (gi_i, 0), (gr_i, 0), (gn_i, 0), (go_i, N), (tabs, 0.0)):
                link(dve, "dve", dve.memset(t[:], v))
            link(dve, "dve", dve.memset(WN[D:D + 1], -BIG))
            for t in list(W.values()) + [W3C, AN, AM, WM, WM3, sh2]:
                link(dve, "dve", dve.memset(t[:], 0.0))
            link(dve, "dve", dve.memset(wh[D:D + 1], 1.0))
            link(dve, "dve", dve.memset(w1[D:D + 1], 1.0))
            link(dve, "dve", dve.memset(epsc[:, 0:1], EPS))
            link(dve, "dve", dve.memset(epsc[:, 1:2], EPS * EPS))
            dve.sem_inc(sem("cleared"), 1)
            dve.wait_ge(sem("ready"), 1)
            L = lambda ins: link(dve, "dve", ins)
            dve.wait_ge(sem("w_pe"), 1)
            L(dve.tensor_copy(wt[:, 0], ps[0:D, DB, 0:D + 1]))
            L(dve.tensor_copy(wt[:, 1, 0:D], ps[0:D, DB, P:P + D]))
            L(dve.tensor_scalar(attB[:, 0], ones[0:D], att[:, 0:1], None, ALU.mult))
            dve.tensor_scalar(attB[:, 1], ones[0:D], att[:, 1:2], None, ALU.mult).then_inc(sem("w_dve"), 1)
            dve.wait_ge(sem("w_pe"), 2)
            L(dve.tensor_copy(W3C[:, 0:D], ps[0:D + 1, DB + 1, 0:D]))
            for k in range(2):
                L(dve.tensor_copy(uv[:, k], ps[:, DB + 2, k * P:k * P + D]))
            L(dve.tensor_copy(gs_i[:, 0:ET], src_i[:]))
            L(dve.tensor_copy(tmp[1][:], dst_i[:]))
            L(dve.tensor_scalar(gd_i[:, 0:ET], tmp[1][:], float(N - 1), None, ALU.min))
            blocks(lambda n, b: dve.tensor_copy(dl[0:n, b], dl_i[0:n, b]))
            blocks(lambda n, b: dve.tensor_tensor(keepF[0:n, b], dl[0:n, b, 1], dl[0:n, b, 0], ALU.is_equal))
            blocks(lambda n, b: dve.tensor_tensor(keepB[0:n, b], dl[0:n, b, 1], dl[0:n, b, 2], ALU.is_equal))
            blocks(lambda n, b: dve.tensor_scalar(penF[0:n, b], keepF[0:n, b], 1.0, BIG, ALU.subtract, ALU.mult))
            blocks(lambda n, b: dve.tensor_scalar(penB[0:n, b], keepB[0:n, b], 1.0, BIG, ALU.subtract, ALU.mult))
            for k, v in enumerate((keepF, keepB, penF, penB)):
                blocks(lambda n, b: dve.tensor_reduce(rcol[0:n, b, 1 + k:2 + k], v[0:n, b], AX_X, ALU.min))
            dve.sem_inc(sem("keep_cols"), 1)
            dve.wait_ge(sem("keep_rows"), 1)
            for k in range(4):
                L(dve.tensor_copy(krow[0:1, k], ps[0:1, DB + k, 0:ET]))
            blocks(lambda n, b: dve.tensor_scalar(rv[0][0:n, b], keepF[0:n, b], -1.0, 1.0, ALU.mult, ALU.add))
            blocks(lambda n, b: dve.memset(rv[0][0:n, b, 0:1], 0.0))
            blocks(lambda n, b: dve.tensor_tensor_scan(rv[1][0:n, b], onesr[0:n, b], rv[0][0:n, b], 0.0, ALU.mult, ALU.add))
            blocks(lambda n, b: dve.tensor_copy(lid_b[0:n, b], rv[1][0:n, b]))
            blocks(lambda n, b: dve.tensor_scalar(rcol[0:n, b, 6:7], keepF[0:n, b, 0:1], 1.0, None, ALU.subtract))
            to_cols_dve(lid)
            scan_dve(rv[3], onesr, keepF, krow[0:1, 0], True)
            scan_dve(rv[4], onesr, keepB, krow[0:1, 1], False)
            blocks(lambda n, b: dve.scalar_tensor_tensor(out=rv[5][0:n, b], in0=rv[3][0:n, b], scalar=-1.0,
                                                         in1=rv[4][0:n, b], op0=ALU.add, op1=ALU.add))
            blocks(lambda n, b: dve.scalar_tensor_tensor(out=rv[6][0:n, b], in0=rv[4][0:n, b], scalar=-1.0,
                                                         in1=ownr[0:n, b], op0=ALU.add, op1=ALU.add))
            blocks(lambda n, b: dve.tensor_scalar(rv[0][0:n, b], keepB[0:n, b], -1.0, 1.0, ALU.mult, ALU.add))
            blocks(lambda n, b: dve.scalar_tensor_tensor(out=rv[7][0:n, b], in0=dl[0:n, b, 1], scalar=float(N),
                                                         in1=rv[0][0:n, b], op0=ALU.is_lt, op1=ALU.mult))
            blocks(lambda n, b: dve.tensor_scalar(rv[2][0:n, b], rv[7][0:n, b], -1.0, 1.0, ALU.mult, ALU.add))
            dve.sem_inc(sem("lines"), 1)
            to_cols_dve(deg)
            to_cols_dve(repf)
            to_cols_dve(isrep)
            L(dve.tensor_copy(gr_i[:, 0:ET], repf[:]))
            L(dve.tensor_scalar(tmp[1][:], tmp[1][:], float(N), None, ALU.subtract))
            L(dve.tensor_tensor(tmp[1][:], tmp[1][:], isrep[:], ALU.mult))
            L(dve.tensor_scalar(go_i[:, 0:ET], tmp[1][:], float(N), None, ALU.add))
            L(dve.tensor_copy(tabs[:, 0:ET, 0], repf[:]))
            L(dve.tensor_copy(tabs[:, 0:ET, 1], deg[:]))

        def prepare_pe():
            pe = nc.tensor
            pe.wait_ge(sem("ready"), 1)
            pe.transpose(ps[0:D, DB, 0:D + 1], W["3"][:, 0:D], ident[0:D + 1, 0:D + 1])
            pe.transpose(ps[0:D, DB, P:P + D], W["G"][0:D, 0:D], ident[0:D, 0:D]).then_inc(sem("w_pe"), 1)
            pe.wait_ge(sem("w_dve"), 1)
            pe.matmul(ps[0:D + 1, DB + 1, 0:P], wt[:, 0], cent[:], start=True, stop=True)
            for k in range(2):
                ins = pe.matmul(ps[:, DB + 2, k * P:k * P + D], attB[:, k], wt[:, 1, 0:D], start=True, stop=True)
            ins.then_inc(sem("w_pe"), 1)
            pe.wait_ge(sem("keep_cols"), 1)
            for k in range(4):
                for b, (t0, n) in enumerate(RB):
                    ins = pe.transpose(ps[0:1, DB + k, t0:t0 + n], rcol[0:n, b, 1 + k:2 + k], ident[0:n, 0:n])
            ins.then_inc(sem("keep_rows"), 1)
            to_cols_pe(rv[1])
            scan_pe(rv[3], True)
            scan_pe(rv[4], False)
            to_cols_pe(rv[5])
            to_cols_pe(rv[6])
            to_cols_pe(rv[7])

        def index_dve():
            dve = nc.vector
            L = lambda ins: link(dve, "dve", ins)
            s_, d_, A, B = tabs[:, 0:ET, 0], tabs[:, 0:ET, 1], tmp[2][:], tmp[3][:]
            L(dve.tensor_scalar(A, d_, 0.0, None, ALU.is_gt))
            L(dve.tensor_tensor(B, s_, own[:], ALU.subtract))
            L(dve.tensor_scalar(B, B, float(EP), None, ALU.subtract))
            L(dve.tensor_tensor(B, B, A, ALU.mult))
            L(dve.tensor_tensor(B, B, own[:], ALU.add))
            L(dve.tensor_scalar(gi_i[:, 0:ET], B, float(EP), None, ALU.add))
            L(dve.tensor_scalar(B, s_, float(EP), None, ALU.subtract))
            L(dve.tensor_tensor(B, B, A, ALU.mult))
            L(dve.tensor_scalar(gn_i[:, 0:ET], B, float(EP), None, ALU.add))
            L(dve.tensor_scalar(A, d_, 1.0, None, ALU.add))
            dve.tensor_scalar(B, deg[:], 1.0, None, ALU.add).then_inc(sem("deg1"), 1)
            dve.wait_ge(sem("deg_root"), 1)
            L(dve.reciprocal(A, A))
            L(dve.reciprocal(B, B))
            L(dve.tensor_tensor(wE[:], A, B, ALU.mult))
            L(dve.tensor_tensor(B, B, B, ALU.mult))
            L(dve.tensor_tensor(wS[:], B, isrep[:], ALU.mult))
            half = TURN // 2
            dve.wait_ge(sem("tab_in"), 32)
            for h, t in enumerate((wx, wh)):
                src = t[0:ND, 0:2 * half].rearrange("i (n two) -> i n two", two=2)[:, :, 1]
                dst = wc[0:ND, h * half:(h + 1) * half]
                L(dve.tensor_scalar(dst, src, 0.0, None, ALU.is_gt))
            dve.sem_inc(sem("active"), 1)

        def index_act():
            act = nc.scalar
            act.wait_ge(sem("deg1"), 1)
            act.activation(tmp[2][:], tmp[2][:], ACT.Sqrt)
            act.activation(tmp[3][:], tmp[3][:], ACT.Sqrt).then_inc(sem("deg_root"), 1)

        def index_sp():
            sp = nc.sync
            half = TURN // 2
            for h, t in enumerate((wx, wh)):
                sp.dma_start(t[0:ND, 0:2 * half],
                             TAB.rearrange("(i h n) two -> i h (n two)", h=2, n=half)[:, h]).then_inc(sem("tab_in"), 16)
            sp.wait_ge(sem("active"), 1)
            sp.dma_start(ACTV, wc[0:ND, 0:TURN]).then_inc(sem("active_out"), 16)
            sp.wait_ge(sem("active_out"), 16)

        def soft_dve():
            dve = nc.vector
            asr, adr, aor = rv[0], rv[1], rv[2]
            to_rows_dve(asr)
            to_rows_dve(adr)
            to_rows_dve(aor)
            blocks(lambda n, b: dve.tensor_scalar(rv[7][0:n, b], keepB[0:n, b], -1.0, 1.0, ALU.mult, ALU.add))
            blocks(lambda n, b: dve.tensor_tensor(adr[0:n, b], adr[0:n, b], rv[7][0:n, b], ALU.mult))
            blocks(lambda n, b: dve.tensor_tensor(aor[0:n, b], aor[0:n, b], rv[7][0:n, b], ALU.mult))
            scan_dve(rv[3], adr, keepB, krow[0:1, 1], False)
            scan_dve(rv[4], aor, keepB, krow[0:1, 1], False)
            for x in (asr, rv[4]):
                blocks(lambda n, b: dve.tensor_tensor(x[0:n, b], x[0:n, b], rv[3][0:n, b], ALU.add))
                blocks(lambda n, b: dve.scalar_tensor_tensor(out=x[0:n, b], in0=x[0:n, b], scalar=SLOPE, in1=x[0:n, b],
                                                             op0=ALU.mult, op1=ALU.max))
            scan_dve(rv[1], asr, penF, krow[0:1, 2], True, summed=False)
            scan_dve(rv[2], asr, penB, krow[0:1, 3], False, summed=False)
            blocks(lambda n, b: dve.tensor_tensor(rv[1][0:n, b], rv[1][0:n, b], rv[2][0:n, b], ALU.max))
            blocks(lambda n, b: dve.tensor_tensor(rv[1][0:n, b], rv[1][0:n, b], rv[4][0:n, b], ALU.max))
            blocks(lambda n, b: dve.tensor_tensor(rv[5][0:n, b], asr[0:n, b], rv[1][0:n, b], ALU.subtract))
            blocks(lambda n, b: dve.tensor_tensor(rv[6][0:n, b], rv[4][0:n, b], rv[1][0:n, b], ALU.subtract))
            dve.sem_inc(sem("logits"), 1)
            dve.wait_ge(sem("exps"), 1)
            scan_dve(rv[1], rv[5], keepF, krow[0:1, 0], True)
            scan_dve(rv[2], rv[5], keepB, krow[0:1, 1], False)
            blocks(lambda n, b: dve.tensor_tensor(rv[1][0:n, b], rv[1][0:n, b], rv[5][0:n, b], ALU.subtract))
            blocks(lambda n, b: dve.tensor_tensor(rv[1][0:n, b], rv[1][0:n, b], rv[2][0:n, b], ALU.add))
            blocks(lambda n, b: dve.tensor_tensor(rv[1][0:n, b], rv[1][0:n, b], rv[6][0:n, b], ALU.add))
            blocks(lambda n, b: dve.tensor_scalar(rv[1][0:n, b], rv[1][0:n, b], 1e-16, None, ALU.add))
            blocks(lambda n, b: dve.reciprocal(rv[1][0:n, b], rv[1][0:n, b]))
            blocks(lambda n, b: dve.tensor_tensor(rv[5][0:n, b], rv[5][0:n, b], rv[1][0:n, b], ALU.mult))
            blocks(lambda n, b: dve.tensor_tensor(rv[6][0:n, b], rv[6][0:n, b], rv[1][0:n, b], ALU.mult))
            to_cols_dve(wE)
            to_cols_dve(wS)
            link(dve, "dve", dve.tensor_tensor(wS[:], wS[:], isrep[:], ALU.mult))

        def soft_pe():
            to_rows_pe(a_s)
            to_rows_pe(a_d)
            to_rows_pe(a_o)
            scan_pe(rv[3], False)
            scan_pe(rv[4], False)
            scan_pe(rv[1], True)
            scan_pe(rv[2], False)
            scan_pe(rv[1], True)
            scan_pe(rv[2], False)
            to_cols_pe(rv[5])
            to_cols_pe(rv[6])

        def soft_act():
            act = nc.scalar
            act.wait_ge(sem("logits"), 1)
            for v in (rv[5], rv[6]):
                for b, (_, n) in enumerate(RB):
                    ins = act.activation(v[0:n, b], v[0:n, b], ACT.Exp)
            ins.then_inc(sem("exps"), 1)

        def norm1_dve():
            dve = nc.vector
            L = lambda ins: link(dve, "dve", ins)
            t = tmp[1][0:D]
            for k, st in enumerate((stN, stE)):
                for m in range(2):
                    L(dve.tensor_reduce(t[:, 2 * k + m:2 * k + m + 1], st[:, m], AX_X, ALU.add))
            norm_dve(1, t[:, 0:1], t[:, 1:2], N, G_N, BE_N, A_N, S_N)
            norm_dve(2, t[:, 2:3], t[:, 3:4], E, G_E, BE_E, A_E, S_E)
            L(dve.tensor_scalar(WM3[:], WM[:, 2], col[:, A_E:A_E + 1], None, ALU.mult))
            L(dve.tensor_scalar(wt[:, 0, 0:D], ident[0:D, 0:D], col[:, A_N:A_N + 1], None, ALU.mult))
            dve.tensor_copy(wt[:, 0, D:D + 1], col[:, S_N:S_N + 1]).then_inc(sem("norm1"), 1)
            dve.wait_ge(sem("norm1_pe"), 1)
            L(dve.tensor_copy(AN[:, 0:D], ps[0:D + 1, DB, 0:D]))
            L(dve.tensor_tensor(mb2[0:1, 0:D], mb2[0:1, 0:D], ps[0:1, DB + 1, 0:D], ALU.add))

        def norm1_pe():
            pe = nc.tensor
            pe.wait_ge(sem("norm1"), 1)
            pe.matmul(ps[0:D + 1, DB, 0:P], wt[:, 0], cent[:], start=True, stop=True)
            pe.matmul(ps[0:1, DB + 1, 0:P], col[:, S_E:S_E + 1], WM[:, 2], start=True, stop=True).then_inc(sem("norm1_pe"), 1)

        def norm2_dve():
            dve = nc.vector
            L = lambda ins: link(dve, "dve", ins)
            t = tmp[1][0:D]
            dve.wait_ge(sem("msum"), 1)
            L(dve.tensor_copy(t[:, 0:2], ps[0:D, DB, 0:2]))
            norm_dve(3, t[:, 0:1], t[:, 1:2], E, G_M, BE_M, A_M, S_M)
            L(dve.tensor_scalar(AM[:], cent[:], col[:, A_M:A_M + 1], None, ALU.mult))
            L(dve.tensor_copy(t[:, 4:5], col[:, S_M:S_M + 1]))
            dve.tensor_copy(t[:, 5:6], col[:, S_N:S_N + 1]).then_inc(sem("norm2"), 1)
            dve.wait_ge(sem("norm2_pe"), 1)
            L(dve.tensor_copy(sh2[:, 0:D], ps[0:2, DB + 1, 0:D]))
            L(dve.reciprocal(tmp[2][:], deg[:]))
            L(dve.tensor_copy(wE[:], tmp[2][:]))

        def norm2_pe():
            pe = nc.tensor
            for m in range(2):
                for t in range(TG):
                    ins = pe.matmul(ps[0:D, DB, m:m + 1], acc[:, m, t], ones[:, 0:1], start=(t == 0), stop=(t == TG - 1))
            ins.then_inc(sem("msum"), 1)
            pe.wait_ge(sem("norm2"), 1)
            pe.matmul(ps[0:2, DB + 1, 0:P], tmp[1][0:D, 4:6], cent[:], start=True, stop=True).then_inc(sem("norm2_pe"), 1)

        block = ctx.enter_context(nc.Block())

        @block.sync
        def _(sp):
            prepare_sp()
            barrier(sp, "sp")
            barrier(sp, "sp")
            index_sp()
            barrier(sp, "sp")
            chain_sp_start(DQ["dense1"])
            copy_sp(PQ["copy"])
            chain_sp(DQ["dense1"], 2 * NI)
            barrier(sp, "sp")
            chain_sp(DQ["source"])
            barrier(sp, "sp")
            chain_sp_start(DQ["dense2"])
            for name in ("conv1", "conv2", "conv3"):
                conv_sp(PQ[name])
                barrier(sp, "sp")
            att_sp(PQ["att"])
            barrier(sp, "sp")
            barrier(sp, "sp")
            conv_sp(PQ["gat"])
            chain_sp(DQ["dense2"], 5 * NI)
            barrier(sp, "sp")
            mlp_sp(PQ["mlp"])
            barrier(sp, "sp")
            emlp_sp(PQ["emlp"])
            barrier(sp, "sp")
            barrier(sp, "sp")
            msg_sp(PQ["msg"])
            barrier(sp, "sp")
            barrier(sp, "sp")
            join_sp(PQ["join"])
            barrier(sp, "sp")
            end_sp(DQ["source3"])
            barrier(sp, "sp")
            end_sp_start(DQ["final"])
            conv_sp(PQ["hop1"])
            barrier(sp, "sp")
            conv_sp(PQ["hop2"])
            end_sp(DQ["final"], 7 * NI)
            barrier(sp, "sp")
            put_sp(PQ["put"])

        @block.gpsimd
        def _(pool):
            for name in list(PQ["put"]["base"]):
                if start_of(name):
                    pool.sem_inc(S(name), START)
            for name in list(DQ["final"]["base"]):
                pool.sem_inc(R(name), START)
            barrier(pool, "pool")
            tab_put_pool(PQ["tab_put"])
            barrier(pool, "pool")
            tab_get_pool(PQ["tab_get"])
            barrier(pool, "pool")
            gather_pool(PQ["copy"], (ringG, ringS), (a["x"], a["x"]))
            barrier(pool, "pool")
            barrier(pool, "pool")
            barrier(pool, "pool")
            for name in ("conv2", "conv3"):
                gather_pool(PQ[name], (ringG,), (PQ[name]["table"],))
                barrier(pool, "pool")
            gather_pool(PQ["att"], (ringG,), (T[3],))
            for _ in range(5):
                barrier(pool, "pool")
            barrier(pool, "pool")
            gather_pool(PQ["msg"], (ringG, ringS), (T[4], T[4]))
            for _ in range(4):
                barrier(pool, "pool")
            for name in ("hop1", "hop2"):
                gather_pool(PQ[name], (ringG,), (PQ[name]["table"],))
                barrier(pool, "pool")
            put_pool(PQ["put"])

        @block.scalar
        def _(act):
            barrier(act, "act")
            barrier(act, "act")
            index_act()
            barrier(act, "act")
            copy_act(PQ["copy"])
            chain_act(DQ["dense1"], 2 * NI)
            barrier(act, "act")
            chain_act(DQ["source"])
            barrier(act, "act")
            for name in ("conv1", "conv2", "conv3"):
                conv_act(PQ[name])
                barrier(act, "act")
            copy_act(PQ["att"])
            barrier(act, "act")
            soft_act()
            barrier(act, "act")
            conv_act(PQ["gat"])
            barrier(act, "act")
            mlp_act(PQ["mlp"])
            barrier(act, "act")
            emlp_act(PQ["emlp"])
            barrier(act, "act")
            norm_act(1)
            norm_act(2)
            barrier(act, "act")
            msg_act(PQ["msg"])
            barrier(act, "act")
            norm_act(3)
            barrier(act, "act")
            conv_act(PQ["join"])
            barrier(act, "act")
            end_act(DQ["source3"])
            barrier(act, "act")
            conv_act(PQ["hop1"])
            barrier(act, "act")
            conv_act(PQ["hop2"])
            end_act(DQ["final"], 7 * NI)
            barrier(act, "act")

        @block.vector
        def _(dve):
            prepare_dve()
            barrier(dve, "dve_")
            tab_put_dve(PQ["tab_put"])
            barrier(dve, "dve_")
            tab_get_dve(PQ["tab_get"])
            index_dve()
            barrier(dve, "dve_")
            copy_dve(PQ["copy"])
            chain_dve(DQ["dense1"], 2 * NI)
            barrier(dve, "dve_")
            chain_dve(DQ["source"])
            barrier(dve, "dve_")
            for name in ("conv1", "conv2", "conv3"):
                conv_dve(PQ[name])
                barrier(dve, "dve_")
            att_dve(PQ["att"])
            barrier(dve, "dve_")
            soft_dve()
            barrier(dve, "dve_")
            conv_dve(PQ["gat"])
            barrier(dve, "dve_")
            mlp_dve(PQ["mlp"])
            barrier(dve, "dve_")
            barrier(dve, "dve_")
            norm1_dve()
            barrier(dve, "dve_")
            msg_dve(PQ["msg"])
            barrier(dve, "dve_")
            norm2_dve()
            barrier(dve, "dve_")
            join_dve(PQ["join"])
            barrier(dve, "dve_")
            end_dve(DQ["source3"])
            barrier(dve, "dve_")
            conv_dve(PQ["hop1"])
            barrier(dve, "dve_")
            conv_dve(PQ["hop2"])
            end_dve(DQ["final"], 7 * NI)
            barrier(dve, "dve_")
            copy_dve(PQ["put"])

        @block.tensor
        def _(pe):
            prepare_pe()
            barrier(pe, "pe")
            barrier(pe, "pe")
            barrier(pe, "pe")
            dense_pe_start(DQ["dense1"])
            copy_pe(PQ["copy"])
            chain_pe(DQ["dense1"], 2 * NI)
            barrier(pe, "pe")
            chain_pe(DQ["source"])
            barrier(pe, "pe")
            dense_pe_start(DQ["dense2"])
            for name in ("conv1", "conv2", "conv3"):
                conv_pe(PQ[name])
                barrier(pe, "pe")
            copy_pe(PQ["att"])
            barrier(pe, "pe")
            soft_pe()
            barrier(pe, "pe")
            conv_pe(PQ["gat"])
            barrier(pe, "pe")
            mlp_pe(PQ["mlp"])
            barrier(pe, "pe")
            emlp_pe(PQ["emlp"])
            barrier(pe, "pe")
            norm1_pe()
            barrier(pe, "pe")
            msg_pe(PQ["msg"])
            barrier(pe, "pe")
            norm2_pe()
            barrier(pe, "pe")
            join_pe(PQ["join"])
            barrier(pe, "pe")
            end_pe(DQ["source3"])
            barrier(pe, "pe")
            dense_pe_start(DQ["final"])
            conv_pe(PQ["hop1"])
            barrier(pe, "pe")
            conv_pe(PQ["hop2"])
            end_pe(DQ["final"], 7 * NI)
            barrier(pe, "pe")


def kernel(**inputs):
    import numpy as np
    import concourse.bacc as bacc
    from concourse.bass_utils import run_bass_kernel_spmd

    arrays = {k: np.ascontiguousarray(v) for k, v in inputs.items() if k not in ("src", "dst", "edge_attr_4")}
    src, dst, attr = (np.asarray(inputs[k]) for k in ("src", "dst", "edge_attr_4"))
    pad = EP - E
    lines = np.concatenate([np.full(1, -1, dst.dtype), dst, np.full(pad, N, dst.dtype), np.full(1, -1, dst.dtype)])
    arrays["dst_line"] = lines
    arrays["dst_cols"] = np.ascontiguousarray(lines[1:1 + EP].reshape(ET, P).T)
    arrays["src_cols"] = np.ascontiguousarray(np.concatenate([src, np.zeros(pad, src.dtype)]).reshape(ET, P).T)
    auxe = np.zeros((2 + DE, EP), attr.dtype)
    auxe[0, :E] = 1
    auxe[1, E:] = 1
    auxe[2:, :E] = attr.T
    arrays["auxe"] = auxe
    eye = np.eye(P, dtype=np.float32)
    arrays["ident"] = eye
    arrays["eye_row"] = np.ascontiguousarray(np.eye(D + 1, D, dtype=np.float32))
    arrays["cent"] = np.zeros((D, P), np.float32)
    arrays["cent"][:, :D] = np.eye(D) - 1.0 / D
    arrays["xT"] = np.ascontiguousarray(arrays["x"].T)
    slots = np.arange(EP, dtype=np.float32)
    arrays["own_cols"] = np.ascontiguousarray(slots.reshape(ET, P).T)
    own_rows = np.zeros((P, 2, P), np.float32)
    own_rows[:, 0] = slots.reshape(ET, P)[:P]
    own_rows[:ET - P, 1] = slots.reshape(ET, P)[P:]
    arrays["own_rows"] = own_rows
    nc = bacc.Bacc("TRN2", target_bir_lowering=False, num_devices=1)
    args = {}
    feed = {}
    for name, v in arrays.items():
        feed[f"in_{name}"] = v
        args[name] = nc.dram_tensor(f"in_{name}", v.shape, mybir.dt.from_np(v.dtype), kind="ExternalInput").ap()
    args["out"] = nc.dram_tensor("out_x", (N, D), F32, kind="ExternalOutput").ap()
    build(nc, args)
    r = run_bass_kernel_spmd(nc, [feed], core_ids=[0])
    return r.results[0]["out_x"]
```

```python
from contextlib import ExitStack

import concourse.bass as bass
from concourse import mybir

ALU = mybir.AluOpType
ACT = mybir.ActivationFunctionType
F32 = mybir.dt.float32
U8 = mybir.dt.uint8
I32 = mybir.dt.int32
AX_X = mybir.AxisListType.X
ds = bass.ds

P = 128
N, D = 100000, 96
E, DE = 25000, 4
ET = -(-E // P)
EP = ET * P
TG = 4
GW = TG * P
NJ = 7
NI = ET // (TG * NJ)
NG = NI * NJ
TI = TG * NJ
HALF = 4
CH = 4
CR = 4
DENSE1 = 3 * NI + 2
CHAIN_GAPS, END_GAPS = 11, 2
NSUB = 125
TURN = CH * CR * NSUB
STURN = CH * CR * P
ND = N // TURN
NL = -(-EP // STURN)
LR = NL * STURN
BIG = 1.0e30
EPS = 1e-5
SLOPE = 0.2
ENGINES = 5
START = 1
RB = [(0, P), (P, ET - P)]
assert ET == TI * NI and N == ND * TURN
(B_1, B_2, B_N, G_N, BE_N, G_E, BE_E, G_M, BE_M, A_N, S_N, A_E, S_E, A_M, S_M,
 NCOL) = range(16)


def build(nc, a):
    with ExitStack() as ctx:
        def sb(name, shape, dt=F32):
            return ctx.enter_context(nc.sbuf_tensor(name, shape, dt))

        def dram(name, shape, dt=F32):
            return nc.dram_tensor(name, shape, dt, kind="Internal").ap()

        sems = {}

        def sem(name):
            if name not in sems:
                sems[name] = ctx.enter_context(nc.semaphore(name))
            return sems[name]

        XS = dram("XS", (LR, D))
        XD = dram("XD", (EP, D))
        T = [None] + [dram(f"T{k}", (EP + LR, D)) for k in (1, 2, 3, 4, 5)]
        TN = dram("TN", (EP + P, D))
        GX = dram("GX", (EP, D))
        TAB = dram("TAB", (N, 2))
        ACTV = dram("ACTV", (ND, TURN))
        X2T = dram("X2T", (D, N))
        X2L = dram("X2L", (D, LR))
        NDT = dram("NDT", (NG, D, 2, GW))
        AGG = dram("AGG", (NG, D, GW))
        LID = dram("LID", (EP,), U8)
        LINE = dram("LINE", (3, EP))
        CONT = dram("CONT", (ET,))

        ps = ctx.enter_context(nc.psum_tensor("ps", [P, 8, 512], F32))
        ZB, OB, DB = 0, 2, 4

        ident = sb("ident", [P, P])
        cent = sb("cent", [D, P])
        W = {k: sb(f"W{k}", [D + 1, P]) for k in "123GI"}
        WN = sb("WN", [D + 1, D])
        WE = sb("WE", [DE + 2, D + 2])
        WM = sb("WM", [D, 3, P])
        WM3 = sb("WM3", [D + 2, P])
        W3C = sb("W3C", [D + 1, P])
        AN = sb("AN", [D + 1, P])
        AM = sb("AM", [D + 2, P])
        col = sb("col", [D, NCOL])
        wt = sb("wt", [D, 2, D + 2])
        att = sb("att", [D, 2])
        attB = sb("attB", [D, 2, P])
        uv = sb("uv", [P, 2, D])
        epsc = sb("epsc", [P, 2])
        ones = sb("ones", [P, P])
        zero = sb("zero", [P, 800])
        onesr = sb("onesr", [P, 2, P])
        mb2 = sb("mb2", [D + 2, P])

        src_i = sb("src_i", [P, ET], I32)
        dst_i = sb("dst_i", [P, ET], I32)
        own = sb("own", [P, ET])
        lid = sb("lid", [P, ET])
        deg = sb("deg", [P, ET])
        isrep = sb("isrep", [P, ET])
        repf = sb("repf", [P, ET])
        wE = sb("wE", [P, ET])
        wS = sb("wS", [P, ET])
        one = sb("one", [P, ET])
        tmp = [sb(f"tmp{k}", [P, ET]) for k in range(4)]
        gs_i = sb("gs_i", [P, ET + TI], I32)
        gd_i = sb("gd_i", [P, ET + TI], I32)
        gi_i = sb("gi_i", [P, ET + TI], I32)
        gr_i = sb("gr_i", [P, ET + TI], I32)
        gn_i = sb("gn_i", [P, ET + TI], I32)
        go_i = sb("go_i", [P, ET + TI], I32)
        tabs = sb("tabs", [P, ET + TI, 2])
        stg = sb("stg", [P, 2, TI], I32)
        tabg = sb("tabg", [P, TI, 2])
        a_s = sb("a_s", [P, ET])
        a_d = sb("a_d", [P, ET])
        a_o = sb("a_o", [P, ET])
        dl_i = sb("dl_i", [P, 2, 3, P], I32)
        dl = sb("dl", [P, 2, 3, P])
        keepF = sb("keepF", [P, 2, P])
        keepB = sb("keepB", [P, 2, P])
        penF = sb("penF", [P, 2, P])
        penB = sb("penB", [P, 2, P])
        rv = [sb(f"rv{k}", [P, 2, P]) for k in range(8)]
        rcol = sb("rcol", [P, 2, 8])
        krow = sb("krow", [1, 4, ET])
        crow = sb("crow", [1, ET + 2])
        ownr = sb("ownr", [P, 2, P])
        lid_b = sb("lid_b", [P, 2, P], U8)
        lidB = sb("lidB", [P, EP], U8)
        contB = sb("contB", [P, ET])

        ringG = sb("ringG", [P, NJ, TG, D])
        ringS = sb("ringS", [P, NJ, TG, D])
        ringO = sb("ringO", [P, NJ, TG, D])
        Sm = sb("Sm", [P, 2, TG, P])
        Dg = sb("Dg", [P, 2, TG, P])
        cm = sb("cm", [D, TG, P])
        zT = sb("zT", [D + 1, 2, GW])
        yb = sb("yb", [P, 2, TG, D])
        st6 = sb("st6", [P, 2, TG, 6])
        mv = sb("mv", [P, 2, TG, 2])
        sdv = sb("sdv", [P, 2, TG])
        acc = sb("acc", [P, 2, TG, D])

        wx = sb("wx", [D, STURN])
        wh = sb("wh", [D + 1, STURN])
        wc = sb("wc", [P, STURN])
        wq = sb("wq", [P, STURN])
        w1 = sb("w1", [D + 1, STURN])
        w2 = sb("w2", [D + 1, STURN])
        xin = ringG[:].rearrange("p j t f -> p (j t f)")[:, 0:CH * GW]
        rows = ringS[:].rearrange("p j t f -> p (j t f)")[:, 0:CH * GW]
        dss = sb("dss", [P, CH, CR])
        dsd = sb("dsd", [P, CH, CR])
        drs = sb("drs", [P, CH, CR])
        dst6 = sb("dst6", [P, CH, CR, 6])
        dmv = sb("dmv", [P, CH, CR, 2])
        stN = sb("stN", [D, 2, ND * CH + NG])
        stE = sb("stE", [D, 2, NG])

        resR = sb("resR", [P, 2, TG, D])
        aux = sb("aux", [DE + 2, NJ, GW])

        bar = sem("all_engines")
        bars = {}

        def barrier(eng, key):
            bars[key] = bars.get(key, 0) + 1
            eng.drain().then_inc(bar, 1)
            eng.wait_ge(bar, ENGINES * bars[key])

        chains = {}

        def link(eng, key, ins):
            chains[key] = chains.get(key, 0) + 1
            ins.then_inc(sem(f"{key}_chain"), 1)
            eng.wait_ge(sem(f"{key}_chain"), chains[key])

        def spread(beside, i, turn, group):
            if beside is None:
                for j in range(NJ):
                    group(j)
                return
            p, first, m = beside["dense"], beside["first"], beside["turns"]
            gaps = m * p["gaps"]
            for k in range(m):
                def between(step, k=k):
                    for j in range(NJ):
                        if j * gaps // NJ == k * p["gaps"] + step:
                            group(j)
                turn(p, i * m + first + k, between)

        def rows_bank(j):
            return ps[:, OB + j % 2].rearrange("p (t f) -> p t f", t=TG)[:, :, 0:D]

        PASSES = {}
        order = []

        def start_of(w):
            return 0 if w in {f"{c}{j}" for j in range(NJ) for c in "gw"} else START

        def add_pass(name, signals="", credit=0, staged=0, slots=(0, 0, 0, 0, 0), **k):
            uses = {w: NG for w in signals.split()}
            if "z" in uses:
                uses["z"] = TG * NG
            if "seg" in uses:
                uses["seg"] += credit
            uses["staged"] = staged
            for c, n in zip("gmsrow", slots + (0,) * (6 - len(slots))):
                for j in range(NJ):
                    uses[f"{c}{j}"] = 16 * n * NI
            names = sorted(set(uses) | {"S", "D", "seg", "mask", "z", "cv", "th", "y", "st", "mv", "sq", "rc", "out", "u"})
            k["uses"] = uses
            k["base"] = {w: start_of(w) + sum(PASSES[q]["uses"].get(w, 0) for q in order) for w in names}
            k.setdefault("ngather", 1)
            k.setdefault("scatter", None)
            k.setdefault("own", False)
            k.setdefault("tail", None)
            k.setdefault("beside", None)
            ends = k["beside"] and k["beside"]["dense"]["gaps"] == END_GAPS
            k["dense_sp"], k["dense_pe"], k["dense_act"], k["dense_dve"] = (
                (end_sp_turn, end_pe_turn, end_act_turn, end_dve_turn) if ends else
                (chain_sp_turn, chain_pe_turn, chain_act_turn, chain_dve_turn))
            PASSES[name] = k
            order.append(name)

        def S(name):
            return sem("e_" + name)

        def at(p, name, v):
            return v + p["base"][name]

        def before(i, j):
            return i * NJ + max(j - 1, 0)

        def table_rows(t, g, row0=0):
            return t[row0:row0 + EP].rearrange("(g t p) f -> g p t f", t=TG, p=P)[g]

        def load_group(p, sp, i, j):
            g = i * NJ + j
            if p.get("m"):
                sp.dma_start(ringG[:, j], table_rows(p["m"], g)).then_inc(S(f"m{j}"), 16)
            if p.get("s"):
                sp.dma_start(ringS[:, j], table_rows(p["s"], g)).then_inc(S(f"s{j}"), 16)

        def res_of(p, j):
            return resR[:, j % 2] if p.get("r") else ringS[:, j]

        def conv_sp(p):
            def store(i, j):
                sp.wait_ge(S("out"), at(p, "out", i * NJ + j + 1))
                sp.nop(nofuse=True)
                if p["scatter"] is not None:
                    return
                sp.dma_start(table_rows(p["out"], i * NJ + j), ringO[:, j]).then_inc(S(f"o{j}"), 16)

            def load_res(i, j):
                if p.get("r"):
                    sp.wait_ge(S("y"), at(p, "y", before(i, j)))
                    sp.nop(nofuse=True)
                    sp.dma_start(resR[:, j % 2], table_rows(p["r"], i * NJ + j)).then_inc(S(f"r{j}"), 16)

            sp = nc.sync
            behind = 0 if p["tail"] in ("relu", "plain") else 2
            for j in range(NJ):
                load_group(p, sp, 0, j)

            def turn(i, last):
                def leave(j):
                    store(i, j)
                    if not last:
                        load_group(p, sp, i + 1, j)

                def group(j):
                    if j + 1 < NJ:
                        load_res(i, j + 1)
                    if j >= behind:
                        leave(j - behind)
                load_res(i, 0)
                spread(p["beside"], i, p["dense_sp"], group)
                for j in range(NJ - behind, NJ):
                    leave(j)
            with sp.Fori(0, NI - 1) as i:
                turn(i, False)
            turn(NI - 1, True)
            if p["scatter"] is None:
                for j in range(NJ):
                    sp.wait_ge(S(f"o{j}"), at(p, f"o{j}", 16 * NI))

        def gather_pool(p, rings, tables):
            pool = nc.gpsimd
            with pool.Fori(0, NI) as i:
                for j in range(NJ):
                    pool.wait_ge(S("staged"), at(p, "staged", 2 * i + (1 if j < HALF else 2)))
                    pool.nop(nofuse=True)
                    if p["kind"] in ("copy", "att"):
                        pool.wait_ge(S(f"o{j}"), at(p, f"o{j}", i * (16 * p["ngather"])))
                        pool.nop(nofuse=True)
                    else:
                        pool.wait_ge(S("seg"), at(p, "seg", i * NJ + j + 1))
                        pool.nop(nofuse=True)
                    for k, (ring, table) in enumerate(zip(rings, tables)):
                        for t in range(TG):
                            pool.indirect_dma_start(
                                ring[:, j, t, :], None, table,
                                bass.IndirectOffsetOnAxis(ap=stg[:, k, TG * j + t:TG * j + t + 1], axis=0)).then_inc(S(f"g{j}"), 16)

        def stage(p, i, half):
            lo, hi = (0, HALF * TG) if half == 0 else (HALF * TG, TI)
            idx = p["gather"]
            for k, g in enumerate(idx):
                ins = nc.vector.tensor_copy(stg[:, k, lo:hi], g[:, ds(i * TI + lo, hi - lo)])
            if p["scatter"] is not None and not (isinstance(i, int) and i == 0):
                ins = nc.vector.tensor_copy(stg[:, 1, lo:hi], p["scatter"][:, ds((i - 1) * TI + lo, hi - lo)])
            ins.then_inc(S("staged"), 1)

        def stage_after(p, i, half):
            js = range(HALF) if half == 0 else range(HALF, NJ)
            for j in js:
                nc.vector.wait_ge(S(f"g{j}"), at(p, f"g{j}", (i + 1) * (16 * TG * p.get("ngather", 1))))
                if p["scatter"] is not None:
                    nc.vector.wait_ge(S(f"o{j}"), at(p, f"o{j}", i * 16))
            stage(p, i + 1, half)

        def build_S(p, i, j, w):
            dve = nc.vector
            dve.wait_ge(S("seg"), at(p, "seg", before(i, j) + NJ))
            for t in range(TG):
                tile = (i * NJ + j) * TG + t
                ins = dve.tensor_scalar(Sm[:, j % 2, t], lidB[:, ds(tile * P, P)], lid[:, ds(tile, 1)],
                                        w[:, ds(tile, 1)], ALU.is_equal, ALU.mult)
            ins.then_inc(S("S"), 1)

        def add_carry(p, i, j):
            dve = nc.vector
            g = i * NJ + j
            dve.wait_ge(S("z"), at(p, "z", g * TG))
            dve.tensor_tensor(
                cm[:], lidB[0:D, ds(g * GW, GW)].rearrange("p (t e) -> p t e", t=TG),
                contB[0:D, ds(g * TG, TG)].unsqueeze(2).to_broadcast([D, TG, P]), ALU.is_equal).then_inc(S("mask"), 1)
            dve.wait_ge(S("mask"), at(p, "mask", g + 1))
            dve.wait_ge(S("seg"), at(p, "seg", g + 1 + NJ))
            dve.wait_ge(S("cv"), at(p, "cv", before(i, j)))
            b = j % 2
            for t in range(TG):
                if t:
                    dve.wait_ge(S("z"), at(p, "z", g * TG + t))
                before_ = zT[0:D, b, t * P - 1:t * P] if t else zT[0:D, (b + 1) % 2 if j else 0, GW - 1:GW]
                dve.scalar_tensor_tensor(
                    out=zT[0:D, b, t * P:(t + 1) * P], in0=cm[:, t], scalar=before_,
                    in1=ps[0:D, ZB + b, t * P:(t + 1) * P], op0=ALU.mult, op1=ALU.add).then_inc(S("z"), 1)

        def ln_sum(p, i, j):
            dve = nc.vector
            b, g = j % 2, i * NJ + j
            o = rows_bank(j)
            dve.wait_ge(S("out"), at(p, "out", before(i, j)))
            if p["tail"] == "tanh":
                dve.wait_ge(S("th"), at(p, "th", g + 1))
            else:
                dve.wait_ge(S("cv"), at(p, "cv", g + 1))
            if p.get("r"):
                dve.wait_ge(S(f"r{j}"), at(p, f"r{j}", (i + 1) * 16))
            if p.get("s"):
                dve.wait_ge(S(f"s{j}"), at(p, f"s{j}", (i + 1) * 16))
            if p["tail"] == "tanh":
                dve.tensor_tensor(yb[:, b], yb[:, b], res_of(p, j), ALU.add).then_inc(S("y"), 1)
            elif p["tail"] == "ln":
                dve.tensor_tensor(yb[:, b], o, res_of(p, j), ALU.add).then_inc(S("y"), 1)
            elif p["tail"] == "copy":
                dve.tensor_copy(yb[:, b], o).then_inc(S("y"), 1)
            else:
                dve.scalar_tensor_tensor(out=ringS[:, j], in0=resR[:, b], scalar=0.5,
                                                in1=ringS[:, j], op0=ALU.mult, op1=ALU.add).then_inc(S("u"), 1)
                dve.wait_ge(S("u"), at(p, "u", g + 1))
                dve.scalar_tensor_tensor(out=yb[:, b], in0=o, scalar=0.5, in1=ringS[:, j],
                                                op0=ALU.mult, op1=ALU.add).then_inc(S("y"), 1)
            dve.wait_ge(S("y"), at(p, "y", g + 1))
            for t in range(TG):
                ins = dve.bn_stats(st6[:, b, t], yb[:, b, t])
            ins.then_inc(S("st"), 1)
            dve.wait_ge(S("st"), at(p, "st", g + 1))
            dve.nop(nofuse=True)
            for t in range(TG):
                ins = dve.bn_aggr(mv[:, b, t], st6[:, b, t])
            ins.then_inc(S("mv"), 1)

        def ln_scale(p, i, j):
            dve = nc.vector
            b, g = j % 2, i * NJ + j
            dve.wait_ge(S("sq"), at(p, "sq", g + 1))
            dve.reciprocal(sdv[:, b], sdv[:, b]).then_inc(S("rc"), 1)
            dve.wait_ge(S("rc"), at(p, "rc", g + 1))
            dve.wait_ge(S(f"o{j}"), at(p, f"o{j}", i * 16))
            for t in range(TG):
                ins = dve.tensor_scalar(ringO[:, j, t], yb[:, b, t], mv[:, b, t, 0:1], sdv[:, b, t:t + 1],
                                        ALU.subtract, ALU.mult)
            ins.then_inc(S("out"), 1)

        def conv_dve(p):
            dve = nc.vector
            link(dve, "dve", dve.memset(zT[0:D], 0.0))
            if p.get("gather"):
                stage(p, 0, 0)
                stage(p, 0, 1)
            ln = p["tail"] != "relu" and p["tail"] != "plain"
            with dve.Fori(0, NI) as i:
                def group(j):
                    add_carry(p, i, j)
                    if p.get("gather") and j == HALF:
                        stage_after(p, i, 0)
                    if ln and j:
                        ln_sum(p, i, j - 1)
                    if ln and j > 1:
                        ln_scale(p, i, j - 2)
                    if j + 2 < NJ:
                        build_S(p, i, j + 2, p["w"])
                build_S(p, i, 0, p["w"])
                build_S(p, i, 1, p["w"])
                spread(p["beside"], i, p["dense_dve"], group)
                if p.get("gather"):
                    stage_after(p, i, 1)
                if ln:
                    ln_sum(p, i, NJ - 1)
                    ln_scale(p, i, NJ - 2)
                    ln_scale(p, i, NJ - 1)

        def conv_pe(p):
            pe = nc.tensor
            pe.sem_inc(S("seg"), NJ)
            rhs = p["W"]

            def seg(i, j):
                g, b = i * NJ + j, j % 2
                pe.wait_ge(S("S"), at(p, "S", g + 1))
                if p.get("m"):
                    pe.wait_ge(S(f"m{j}"), at(p, f"m{j}", (i + 1) * 16))
                else:
                    pe.wait_ge(S(f"g{j}"), at(p, f"g{j}", (i + 1) * (16 * TG)))
                if p["own"]:
                    pe.wait_ge(S(f"s{j}"), at(p, f"s{j}", (i + 1) * 16))
                    pe.wait_ge(S("D"), at(p, "D", g + 1))
                pe.wait_ge(S("z"), at(p, "z", before(i, j) * TG))
                for t in range(TG):
                    o = ps[0:D, ZB + b, t * P:(t + 1) * P]
                    ins = pe.matmul(o, ringG[:, j, t], Sm[:, b, t], start=True, stop=not p["own"])
                    if p["own"]:
                        ins = pe.matmul(o, ringS[:, j, t], Dg[:, b, t], start=False, stop=True)
                ins.then_inc(S("seg"), 1)

            bank_read = {"relu": "out", "plain": "out", "tanh": "th"}.get(p["tail"], "y")

            def rows_(i, j):
                g, b = i * NJ + j, j % 2
                pe.wait_ge(S("z"), at(p, "z", (g + 1) * TG))
                pe.wait_ge(S(bank_read), at(p, bank_read, before(i, j)))
                for t in range(TG):
                    ins = pe.matmul(ps[:, OB + b, t * P:(t + 1) * P], zT[:, b, t * P:(t + 1) * P], rhs[:],
                                    start=True, stop=True)
                ins.then_inc(S("cv"), 1)

            with pe.Fori(0, NI) as i:
                def group(j):
                    if j + 1 < NJ:
                        seg(i, j + 1)
                    rows_(i, j)
                seg(i, 0)
                spread(p["beside"], i, p["dense_pe"], group)

        def conv_act(p):
            act = nc.scalar

            def diag(i, j):
                act.wait_ge(S("seg"), at(p, "seg", before(i, j) + NJ))
                for t in range(TG):
                    tile = (i * NJ + j) * TG + t
                    ins = act.activation(Dg[:, j % 2, t], ident[:], ACT.Copy, scale=wS[:, ds(tile, 1)])
                ins.then_inc(S("D"), 1)

            def tail(i, j):
                g, b = i * NJ + j, j % 2
                if p["tail"] in ("relu", "plain"):
                    act.wait_ge(S("cv"), at(p, "cv", g + 1))
                    act.wait_ge(S(f"o{j}"), at(p, f"o{j}", i * 16))
                    act.activation(ringO[:, j], rows_bank(j),
                                   ACT.Relu if p["tail"] == "relu" else ACT.Copy).then_inc(S("out"), 1)
                elif p["tail"] == "tanh":
                    act.wait_ge(S("cv"), at(p, "cv", g + 1))
                    act.wait_ge(S("out"), at(p, "out", before(i, j)))
                    act.activation(yb[:, b], rows_bank(j), ACT.Tanh).then_inc(S("th"), 1)

            def root(i, j):
                act.wait_ge(S("mv"), at(p, "mv", i * NJ + j + 1))
                act.activation(sdv[:, j % 2], mv[:, j % 2, :, 1], ACT.Sqrt, bias=epsc[:, 0:1]).then_inc(S("sq"), 1)

            ln = p["tail"] not in ("relu", "plain")
            with act.Fori(0, NI) as i:
                def group(j):
                    tail(i, j)
                    if ln and j:
                        root(i, j - 1)
                    if p["own"] and j + 2 < NJ:
                        diag(i, j + 2)
                if p["own"]:
                    diag(i, 0)
                    diag(i, 1)
                spread(p["beside"], i, p["dense_act"], group)
                if ln:
                    root(i, NJ - 1)

        nscan = {"dve": 0, "pe": 0}
        nmove = {"dve": 0, "pe": 0}

        def scan_dve(outv, data, keep, keep_row, fwd, summed=True):
            dve = nc.vector
            k = nscan["dve"] = nscan["dve"] + 1
            op0, op1 = (ALU.mult, ALU.add) if summed else (ALU.add, ALU.max)
            init = 0.0 if summed else -BIG
            f = (lambda ap: ap) if fwd else (lambda ap: ap[:, ::-1])
            for b, (_, n) in enumerate(RB):
                ins = dve.tensor_tensor_scan(f(outv[0:n, b]), f(keep[0:n, b]), f(data[0:n, b]), init, op0, op1)
            ins.then_inc(sem("scan_tile"), 1)
            dve.wait_ge(sem("scan_last"), k)
            link(dve, "dve", dve.memset(crow[:], init))
            to = crow[0:1, 1:ET + 1]
            dve.tensor_tensor_scan(f(to), f(keep_row), f(ps[0:1, ZB, 0:ET]), init, op0, op1).then_inc(sem("scan_row"), 1)
            dve.wait_ge(sem("scan_carry"), k)
            for b, (_, n) in enumerate(RB):
                link(dve, "dve", dve.tensor_copy(rcol[0:n, b, 0:1], ps[0:n, ZB + 1, 8 * b:8 * b + 1]))
            for b, (_, n) in enumerate(RB):
                link(dve, "dve", dve.tensor_tensor_scan(f(outv[0:n, b]), f(keep[0:n, b]), f(data[0:n, b]),
                                                        rcol[0:n, b, 0:1], op0, op1))

        def scan_pe(outv, fwd):
            pe = nc.tensor
            k = nscan["pe"] = nscan["pe"] + 1
            pe.wait_ge(sem("scan_tile"), k)
            c = P - 1 if fwd else 0
            for b, (t0, n) in enumerate(RB):
                ins = pe.transpose(ps[0:1, ZB, t0:t0 + n], outv[0:n, b, c:c + 1], ident[0:n, 0:n])
            ins.then_inc(sem("scan_last"), 1)
            pe.wait_ge(sem("scan_row"), k)
            off = 0 if fwd else 2
            for b, (t0, n) in enumerate(RB):
                ins = pe.matmul(ps[0:n, ZB + 1, 8 * b:8 * b + 1], crow[0:1, off + t0:off + t0 + n],
                                ones[0:1, 0:1], start=True, stop=True)
            ins.then_inc(sem("scan_carry"), 1)

        def to_cols_dve(dst):
            dve = nc.vector
            k = nmove["dve"] = nmove["dve"] + 1
            dve.sem_inc(sem("move_ready"), 1)
            dve.wait_ge(sem("move_done"), k)
            link(dve, "dve", dve.tensor_copy(dst[:, 0:ET], ps[:, OB, 0:ET]))

        def to_cols_pe(srcv):
            pe = nc.tensor
            k = nmove["pe"] = nmove["pe"] + 1
            pe.wait_ge(sem("move_ready"), k)
            for b, (t0, n) in enumerate(RB):
                ins = pe.transpose(ps[:, OB, t0:t0 + n], srcv[0:n, b], ident[0:n, 0:n])
            ins.then_inc(sem("move_done"), 1)

        def to_rows_dve(dst):
            dve = nc.vector
            k = nmove["dve"] = nmove["dve"] + 1
            dve.sem_inc(sem("move_ready"), 1)
            dve.wait_ge(sem("move_done"), k)
            for b, (_, n) in enumerate(RB):
                link(dve, "dve", dve.tensor_copy(dst[0:n, b], ps[0:n, OB, b * P:(b + 1) * P]))

        def to_rows_pe(srcv):
            pe = nc.tensor
            k = nmove["pe"] = nmove["pe"] + 1
            pe.wait_ge(sem("move_ready"), k)
            for b, (t0, n) in enumerate(RB):
                ins = pe.transpose(ps[0:n, OB, b * P:(b + 1) * P], srcv[:, t0:t0 + n], ident[:])
            ins.then_inc(sem("move_done"), 1)

        def blocks(fn):
            for b, (_, n) in enumerate(RB):
                link(nc.vector, "dve", fn(n, b))


        def copy_sp(p):
            sp = nc.sync
            with sp.Fori(0, NI) as i:
                def group(j):
                    sp.wait_ge(S(f"g{j}"), at(p, f"g{j}", (i + 1) * (16 * TG * p["ngather"])))
                    sp.nop(nofuse=True)
                    for ring, t in zip((ringG, ringS), p["to"]):
                        sp.dma_start(table_rows(t, i * NJ + j), ring[:, j]).then_inc(S(f"o{j}"), 16)
                spread(p["beside"], i, p["dense_sp"], group)
            for j in range(NJ):
                sp.wait_ge(S(f"o{j}"), at(p, f"o{j}", 16 * NI * p["ngather"]))

        def copy_dve(p):
            stage(p, 0, 0)
            stage(p, 0, 1)
            with nc.vector.Fori(0, NI) as i:
                def group(j):
                    if j == HALF:
                        stage_after(p, i, 0)
                spread(p["beside"], i, p["dense_dve"], group)
                stage_after(p, i, 1)

        def copy_pe(p):
            with nc.tensor.Fori(0, NI) as i:
                spread(p["beside"], i, p["dense_pe"], nothing)

        def copy_act(p):
            with nc.scalar.Fori(0, NI) as i:
                spread(p["beside"], i, p["dense_act"], nothing)

        def att_sp(p):
            sp = nc.sync
            for j in range(NJ):
                load_group(p, sp, 0, j)

            def turn(i, last):
                def group(j):
                    sp.wait_ge(S("out"), at(p, "out", i * NJ + j + 1))
                    sp.nop(nofuse=True)
                    sp.dma_start(table_rows(GX, i * NJ + j), ringG[:, j]).then_inc(S(f"o{j}"), 16)
                    if not last:
                        load_group(p, sp, i + 1, j)
                spread(p["beside"], i, p["dense_sp"], group)
            with sp.Fori(0, NI - 1) as i:
                turn(i, False)
            turn(NI - 1, True)
            for j in range(NJ):
                sp.wait_ge(S(f"o{j}"), at(p, f"o{j}", 16 * NI))

        def att_dve(p):
            dve = nc.vector
            stage(p, 0, 0)
            stage(p, 0, 1)
            with dve.Fori(0, NI) as i:
                def group(j):
                    g = i * NJ + j
                    dve.wait_ge(S(f"g{j}"), at(p, f"g{j}", (i + 1) * (16 * TG)))
                    dve.wait_ge(S(f"s{j}"), at(p, f"s{j}", (i + 1) * 16))
                    dve.wait_ge(S("out"), at(p, "out", g))
                    for k, (ring, v) in enumerate(((ringG, 0), (ringS, 0), (ringS, 1))):
                        ins = dve.tensor_tensor(att3[:, k], ring[:, j], uv[:, v:v + 1].to_broadcast([P, TG, D]), ALU.mult)
                    ins.then_inc(S("y"), 1)
                    dve.wait_ge(S("y"), at(p, "y", g + 1))
                    for k, dst in enumerate((a_s, a_o, a_d)):
                        ins = dve.tensor_reduce(dst[:, ds(g * TG, TG)], att3[:, k], AX_X, ALU.add)
                    ins.then_inc(S("out"), 1)
                    if j == HALF:
                        stage_after(p, i, 0)
                spread(p["beside"], i, p["dense_dve"], group)
                stage_after(p, i, 1)

        att3 = ringO[:, 0:3]

        def mlp_sp(p):
            sp = nc.sync

            def load_mask_row(i, j):
                sp.wait_ge(S("cv"), at(p, "cv", i * NJ + max(j + 1 - NB, 0)))
                sp.nop(nofuse=True)
                sp.dma_start(x2_rows(j, slice(D, D + 1)),
                             LINE[2:3].rearrange("r (g e) -> g r e", e=GW)[i * NJ + j]).then_inc(S(f"m{j}"), 16)
            for j in range(NJ):
                load_group(dict(p, m=None), sp, 0, j)

            def turn(i, last):
                load_mask_row(i, 0)
                load_mask_row(i, 1)
                for j in range(NJ):
                    if j + 2 < NJ:
                        load_mask_row(i, j + 2)
                    sp.wait_ge(S("out"), at(p, "out", i * NJ + j + 1))
                    sp.nop(nofuse=True)
                    sp.dma_start(NDT[i * NJ + j], ndt(j % NB)).then_inc(S(f"o{j}"), 16)
                    if not last:
                        load_group(dict(p, m=None), sp, i + 1, j)
            with sp.Fori(0, NI - 1) as i:
                turn(i, False)
            turn(NI - 1, True)
            for j in range(NJ):
                sp.wait_ge(S(f"o{j}"), at(p, f"o{j}", 16 * NI))

        NB = 4

        def ndt(b):
            return (wc, wq)[b % 2][0:D, b // 2 * 2 * GW:(b // 2 + 1) * 2 * GW].rearrange("p (k e) -> p k e", k=2)

        def x2_rows(j, rows_):
            k = j % NB // 2 * 2 * GW
            return (wc, wq)[j % 2][rows_, k:k + GW]

        def mlp_pe(p):
            pe = nc.tensor

            def turned(i, j):
                pe.wait_ge(S(f"s{j}"), at(p, f"s{j}", (i + 1) * 16))
                pe.wait_ge(S("y"), at(p, "y", before(i, j)))
                for t in range(TG):
                    ins = pe.transpose(ps[0:D, DB + j % 2, t * P:(t + 1) * P], ringS[:, j, t], ident[:])
                ins.then_inc(S("seg"), 1)

            def product(i, j):
                pe.wait_ge(S("y"), at(p, "y", i * NJ + j + 1))
                pe.wait_ge(S(f"m{j}"), at(p, f"m{j}", (i + 1) * 16))
                pe.wait_ge(S("th"), at(p, "th", before(i, j)))
                pe.matmul(ps[0:D, DB + 2 + j % 2, 0:GW], WN[:], x2_rows(j, slice(0, D + 1)),
                          start=True, stop=True).then_inc(S("cv"), 1)

            with pe.Fori(0, NI) as i:
                turned(i, 0)
                for j in range(NJ):
                    if j + 1 < NJ:
                        turned(i, j + 1)
                    product(i, j)

        def mlp_dve(p):
            dve = nc.vector
            with dve.Fori(0, NI) as i:
                for j in range(NJ):
                    g = i * NJ + j
                    dve.wait_ge(S("seg"), at(p, "seg", g + 1))
                    if j >= NB:
                        dve.wait_ge(S(f"o{j - NB}"), at(p, f"o{j - NB}", (i + 1) * 16))
                    else:
                        k = j + NB if j + NB < NJ else j
                        dve.wait_ge(S(f"o{k}"), at(p, f"o{k}", i * 16))
                    dve.tensor_copy(ndt(j % NB)[:, 0], ps[0:D, DB + j % 2, 0:GW]).then_inc(S("y"), 1)

        def mlp_act(p):
            act = nc.scalar
            with act.Fori(0, NI) as i:
                for j in range(NJ):
                    g = i * NJ + j
                    act.wait_ge(S("cv"), at(p, "cv", g + 1))
                    h = ndt(j % NB)[:, 1]
                    act.wait_ge(S("out"), at(p, "out", g))
                    act.activation(h, ps[0:D, DB + 2 + j % 2, 0:GW], ACT.Relu, bias=col[:, B_N:B_N + 1],
                                          accum_out=stN[:, 0, ds(g + ND * CH, 1)]).then_inc(S("th"), 1)
                    act.wait_ge(S("th"), at(p, "th", g + 1))
                    act.activation(wh[0:D, 0:GW], h, ACT.Square,
                                          accum_out=stN[:, 1, ds(g + ND * CH, 1)]).then_inc(S("out"), 1)

        def emlp_sp(p):
            sp = nc.sync

            def load(i, j):
                sp.dma_start(aux[:, j], a["auxe"].rearrange("r (g e) -> g r e", e=GW)[i * NJ + j]).then_inc(S(f"m{j}"), 16)
            for j in range(NJ):
                load(0, j)
            with sp.Fori(0, NI - 1) as i:
                for j in range(NJ):
                    sp.wait_ge(S("cv"), at(p, "cv", i * NJ + j + 1))
                    sp.nop(nofuse=True)
                    load(i + 1, j)

        def emlp_pe(p):
            pe = nc.tensor
            with pe.Fori(0, NI) as i:
                for j in range(NJ):
                    g = i * NJ + j
                    pe.wait_ge(S(f"m{j}"), at(p, f"m{j}", (i + 1) * 16))
                    pe.wait_ge(S("th"), at(p, "th", before(i, j)))
                    pe.matmul(ps[0:D, DB + j % 2, 0:GW], WE[:, 0:D], aux[:, j], start=True, stop=True).then_inc(S("cv"), 1)

        def emlp_act(p):
            act = nc.scalar
            with act.Fori(0, NI) as i:
                for j in range(NJ):
                    g = i * NJ + j
                    act.wait_ge(S("cv"), at(p, "cv", g + 1))
                    act.wait_ge(S("out"), at(p, "out", g))
                    act.activation(wh[0:D, 0:GW], ps[0:D, DB + j % 2, 0:GW], ACT.Relu,
                                          accum_out=stE[:, 0, ds(g, 1)]).then_inc(S("th"), 1)
                    act.wait_ge(S("th"), at(p, "th", g + 1))
                    act.activation(wh[0:D, 0:GW], wh[0:D, 0:GW], ACT.Square,
                                          accum_out=stE[:, 1, ds(g, 1)]).then_inc(S("out"), 1)

        xsT, xdT, heT = wc[0:D, 0:GW], wc[0:D, GW:2 * GW], wc[0:D + 2, 2 * GW:3 * GW]

        def msg_sp(p):
            sp = nc.sync

            def load(i, j):
                sp.dma_start(aux[:, j], a["auxe"].rearrange("r (g e) -> g r e", e=GW)[i * NJ + j]).then_inc(S(f"m{j}"), 16)
            for j in range(NJ):
                load(0, j)

            def turn(i, last):
                for j in range(NJ):
                    g = i * NJ + j
                    sp.wait_ge(S("z"), at(p, "z", (g + 1) * TG))
                    sp.nop(nofuse=True)
                    sp.dma_start(AGG[g], zT[0:D, j % 2]).then_inc(S(f"o{j}"), 16)
                    if not last:
                        load(i + 1, j)
            with sp.Fori(0, NI - 1) as i:
                turn(i, False)
            turn(NI - 1, True)
            for j in range(NJ):
                sp.wait_ge(S(f"o{j}"), at(p, f"o{j}", 16 * NI))

        def msg_pe(p):
            pe = nc.tensor
            pe.sem_inc(S("seg"), NJ)

            def turned(i, j):
                g = i * NJ + j
                pe.wait_ge(S(f"g{j}"), at(p, f"g{j}", (i + 1) * (16 * TG * 2)))
                pe.wait_ge(S(f"m{j}"), at(p, f"m{j}", (i + 1) * 16))
                pe.wait_ge(S("y"), at(p, "y", g))
                pe.wait_ge(S("th"), at(p, "th", g))
                for t in range(TG):
                    pe.transpose(ps[0:D, DB, t * P:(t + 1) * P], ringG[:, j, t], ident[:])
                for t in range(TG):
                    pe.transpose(ps[0:D, DB + 1, t * P:(t + 1) * P], ringS[:, j, t], ident[:])
                pe.matmul(ps[0:D + 2, DB + 2, 0:GW], WE[:], aux[:, j], start=True, stop=True).then_inc(S("D"), 1)

            def message(i, j):
                g = i * NJ + j
                pe.wait_ge(S("y"), at(p, "y", g + 1))
                pe.wait_ge(S("th"), at(p, "th", g + 1))
                pe.wait_ge(S("u"), at(p, "u", before(i, j)))
                for t in range(TG):
                    o = ps[:, OB + j % 2, t * P:(t + 1) * P]
                    e = slice(t * P, (t + 1) * P)
                    pe.matmul(o, xsT[:, e], WM[:, 0], start=True, stop=False)
                    pe.matmul(o, xdT[:, e], WM[:, 1], start=False, stop=False)
                    ins = pe.matmul(o, heT[:, e], WM3[:], start=False, stop=True)
                ins.then_inc(S("cv"), 1)

            def seg(i, j):
                g, b = i * NJ + j, j % 2
                pe.wait_ge(S("S"), at(p, "S", g + 1))
                pe.wait_ge(S("u"), at(p, "u", g + 1))
                pe.wait_ge(S("z"), at(p, "z", before(i, j) * TG))
                for t in range(TG):
                    ins = pe.matmul(ps[0:D, ZB + b, t * P:(t + 1) * P], ringO[:, j, t], Sm[:, b, t],
                                    start=True, stop=True)
                ins.then_inc(S("seg"), 1)

            with pe.Fori(0, NI) as i:
                turned(i, 0)
                for j in range(NJ):
                    message(i, j)
                    if j + 1 < NJ:
                        turned(i, j + 1)
                    seg(i, j)

        def msg_act(p):
            act = nc.scalar

            def evict(i, j):
                g = i * NJ + j
                act.wait_ge(S("D"), at(p, "D", g + 1))
                act.wait_ge(S("cv"), at(p, "cv", g))
                act.activation(xdT, ps[0:D, DB + 1, 0:GW], ACT.Copy)
                act.activation(heT, ps[0:D + 2, DB + 2, 0:GW], ACT.Relu).then_inc(S("th"), 1)

            with act.Fori(0, NI) as i:
                evict(i, 0)
                for j in range(NJ):
                    g = i * NJ + j
                    act.wait_ge(S("cv"), at(p, "cv", g + 1))
                    act.wait_ge(S("seg"), at(p, "seg", g + 1))
                    act.wait_ge(S("out"), at(p, "out", g))
                    act.activation(ringO[:, j], rows_bank(j), ACT.Relu).then_inc(S("u"), 1)
                    act.wait_ge(S("u"), at(p, "u", g + 1))
                    act.activation(yb[:, 0].rearrange("p t f -> p (t f)"),
                                   ringO[:, j].rearrange("p t f -> p (t f)"), ACT.Square).then_inc(S("sq"), 1)
                    if j + 1 < NJ:
                        evict(i, j + 1)

        def msg_dve(p):
            dve = nc.vector
            link(dve, "dve", dve.memset(zT[0:D], 0.0))
            link(dve, "dve", dve.memset(acc[:], 0.0))
            stage(p, 0, 0)
            stage(p, 0, 1)

            def evict(i, j):
                g = i * NJ + j
                dve.wait_ge(S("D"), at(p, "D", g + 1))
                dve.wait_ge(S("cv"), at(p, "cv", g))
                dve.tensor_copy(xsT, ps[0:D, DB, 0:GW]).then_inc(S("y"), 1)

            with dve.Fori(0, NI) as i:
                evict(i, 0)
                for j in range(NJ):
                    g = i * NJ + j
                    build_S(p, i, j, one)
                    dve.wait_ge(S("u"), at(p, "u", g + 1))
                    dve.wait_ge(S("out"), at(p, "out", g))
                    dve.tensor_tensor(acc[:, 0], acc[:, 0], ringO[:, j], ALU.add)
                    dve.wait_ge(S("sq"), at(p, "sq", g + 1))
                    dve.tensor_tensor(acc[:, 1], acc[:, 1], yb[:, 0], ALU.add).then_inc(S("out"), 1)
                    if j + 1 < NJ:
                        evict(i, j + 1)
                    if j > 1:
                        dve.wait_ge(S(f"o{j - 2}"), at(p, f"o{j - 2}", (i + 1) * 16))
                    else:
                        dve.wait_ge(S(f"o{NJ - 1 - j}"), at(p, f"o{NJ - 1 - j}", i * 16))
                        if j:
                            dve.wait_ge(S(f"o{NJ - 1}"), at(p, f"o{NJ - 1}", i * 16))
                    add_carry(p, i, j)
                    if j == HALF:
                        stage_after(p, i, 0)
                stage_after(p, i, 1)

        def join_buf(b):
            return (wc, wq)[b][0:D, 0:3 * GW].rearrange("p (k e) -> p k e", k=3)

        def join_sp(p):
            sp = nc.sync

            def load(i, j):
                g = i * NJ + j
                sp.wait_ge(S("cv"), at(p, "cv", before(i, j)))
                sp.nop(nofuse=True)
                sp.dma_start(join_buf(j % 2)[:, 0:2], NDT[g]).then_inc(S(f"m{j}"), 16)
                sp.dma_start(join_buf(j % 2)[:, 2], AGG[g]).then_inc(S(f"r{j}"), 16)
                sp.dma_start((wc, wq)[j % 2][D:D + 2, 2 * GW:3 * GW],
                             LINE[0:2].rearrange("r (g e) -> g r e", e=GW)[g]).then_inc(S(f"s{j}"), 16)

            def store(i, j):
                sp.wait_ge(S("out"), at(p, "out", i * NJ + j + 1))
                sp.nop(nofuse=True)
                sp.dma_start(table_rows(T[5], i * NJ + j), ringO[:, j]).then_inc(S(f"o{j}"), 16)

            with sp.Fori(0, NI) as i:
                load(i, 0)
                for j in range(NJ):
                    if j + 1 < NJ:
                        load(i, j + 1)
                    if j:
                        store(i, j - 1)
                store(i, NJ - 1)
            for j in range(NJ):
                sp.wait_ge(S(f"o{j}"), at(p, f"o{j}", 16 * NI))

        def join_pe(p):
            pe = nc.tensor
            with pe.Fori(0, NI) as i:
                for j in range(NJ):
                    g = i * NJ + j
                    for r in "mrs":
                        pe.wait_ge(S(f"{r}{j}"), at(p, f"{r}{j}", (i + 1) * 16))
                    pe.wait_ge(S("y"), at(p, "y", before(i, j)))
                    for t in range(TG):
                        o = ps[:, OB + j % 2, t * P:(t + 1) * P]
                        e = slice(t * P, (t + 1) * P)
                        pe.matmul(o, join_buf(j % 2)[:, 0, e], cent[:], start=True, stop=False)
                        pe.matmul(o, join_buf(j % 2)[:, 1, e], AN[0:D], start=False, stop=False)
                        ins = pe.matmul(o, (wc, wq)[j % 2][0:D + 2, 2 * GW + t * P:2 * GW + (t + 1) * P], AM[:],
                                        start=False, stop=True)
                    ins.then_inc(S("cv"), 1)

        def join_dve(p):
            with nc.vector.Fori(0, NI) as i:
                for j in range(NJ):
                    ln_sum(p, i, j)
                    if j:
                        ln_scale(p, i, j - 1)
                ln_scale(p, i, NJ - 1)

        def hop2_pool(p):
            pool = nc.gpsimd

            def gather(i, j):
                pool.wait_ge(S("staged"), at(p, "staged", 2 * i + (1 if j < HALF else 2)))
                pool.nop(nofuse=True)
                pool.wait_ge(S("seg"), at(p, "seg", i * NJ + j + 1))
                pool.nop(nofuse=True)
                for t in range(TG):
                    pool.indirect_dma_start(
                        ringG[:, j, t, :], None, p["table"],
                        bass.IndirectOffsetOnAxis(ap=stg[:, 0, TG * j + t:TG * j + t + 1], axis=0)).then_inc(S(f"g{j}"), 16)

            def scatter(i, j):
                pool.wait_ge(S("staged"), at(p, "staged", 2 * i + (1 if j < HALF else 2)))
                pool.nop(nofuse=True)
                pool.wait_ge(S("out"), at(p, "out", (i - 1) * NJ + j + 1))
                pool.nop(nofuse=True)
                for t in range(TG):
                    pool.indirect_dma_start(
                        a["out"], bass.IndirectOffsetOnAxis(ap=stg[:, 1, TG * j + t:TG * j + t + 1], axis=0),
                        ringO[:, j, t, :], None, bounds_check=N - 1, oob_is_err=False).then_inc(S(f"w{j}"), 16)

            def scattered(i, j):
                pool.wait_ge(S(f"w{j}"), at(p, f"w{j}", i * (16 * TG)))
                pool.nop(nofuse=True)
                pool.sem_inc(S(f"o{j}"), 16)

            for j in range(NJ):
                gather(0, j)
            with pool.Fori(1, NI) as i:
                for j in range(NJ):
                    gather(i, j)
                    scatter(i, j)
                    if j > 1:
                        scattered(i, j - 2)
                scattered(i, NJ - 2)
                scattered(i, NJ - 1)
            for j in range(NJ):
                scatter(NI, j)
            for j in range(NJ):
                pool.wait_ge(S(f"w{j}"), at(p, f"w{j}", NI * (16 * TG)))

        def tab_put_dve(p):
            dve = nc.vector
            dve.tensor_copy(tabg[:], tabs[:, 0:TI, :])
            dve.tensor_copy(stg[:, 0], go_i[:, 0:TI]).then_inc(S("staged"), 1)
            with dve.Fori(0, NI - 1) as i:
                for j in range(NJ):
                    dve.wait_ge(S(f"g{j}"), at(p, f"g{j}", (i + 1) * (16 * TG)))
                dve.tensor_copy(tabg[:], tabs[:, ds((i + 1) * TI, TI), :])
                dve.tensor_copy(stg[:, 0], go_i[:, ds((i + 1) * TI, TI)]).then_inc(S("staged"), 1)

        def tab_put_pool(p):
            pool = nc.gpsimd
            with pool.Fori(0, NI) as i:
                pool.wait_ge(S("staged"), at(p, "staged", i + 1))
                pool.nop(nofuse=True)
                for j in range(NJ):
                    for t in range(j * TG, (j + 1) * TG):
                        pool.indirect_dma_start(
                            TAB, bass.IndirectOffsetOnAxis(ap=stg[:, 0, t:t + 1], axis=0), tabg[:, t, :], None,
                            bounds_check=N - 1, oob_is_err=False).then_inc(S(f"g{j}"), 16)
            for j in range(NJ):
                pool.wait_ge(S(f"g{j}"), at(p, f"g{j}", 16 * TG * NI))

        def tab_get_dve(p):
            dve = nc.vector

            def take(i, js):
                lo, hi = js[0] * TG, (js[-1] + 1) * TG
                for j in js:
                    dve.wait_ge(S(f"g{j}"), at(p, f"g{j}", (i + 1) * (16 * TG)))
                dve.tensor_copy(tabs[:, ds(i * TI + lo, hi - lo), :], tabg[:, lo:hi])
                stage(p, i + 1, 0 if lo == 0 else 1)

            with dve.Fori(0, NI) as i:
                def group(j):
                    if j == HALF:
                        take(i, range(HALF))
                spread(p["beside"], i, p["dense_dve"], group)
                take(i, range(HALF, NJ))
            link(dve, "dve", dve.drain())

        def tab_get_pool(p):
            pool = nc.gpsimd
            with pool.Fori(0, NI) as i:
                for j in range(NJ):
                    pool.wait_ge(S("staged"), at(p, "staged", 2 * i + (1 if j < HALF else 2)))
                    pool.nop(nofuse=True)
                    for t in range(j * TG, (j + 1) * TG):
                        pool.indirect_dma_start(
                            tabg[:, t, :], None, TAB,
                            bass.IndirectOffsetOnAxis(ap=stg[:, 0, t:t + 1], axis=0)).then_inc(S(f"g{j}"), 16)

        def tab_get_sp(p):
            with nc.sync.Fori(0, NI) as i:
                spread(p["beside"], i, p["dense_sp"], nothing)

        DENSE, dorder = {}, []

        def add_dense(name, signals, **k):
            n = CH * k["turns"]
            uses = {w: n for w in signals.split()}
            for w in ("tp", "ev"):
                if w in uses:
                    uses[w] = 2 * n
            uses[k["last"]] += CH
            for c in range(CH):
                for w, m in k["slots"].items():
                    uses[f"{w}{c}"] = 16 * m * k["turns"]
            k.setdefault("t0", 0)
            names = sorted(set(uses) | {f"{w}{c}" for w in DENSE_DMA.split() for c in range(CH)} | set(CHAIN.split()))
            k["uses"] = uses
            k["base"] = {w: START + sum(DENSE[q]["uses"].get(w, 0) for q in dorder) for w in names}
            DENSE[name] = k
            dorder.append(name)

        def R(name):
            return sem("d_" + name)

        def dat(p, name, v):
            return v + p["base"][name] + (CH if name == p["last"] else 0)

        def block_rows(t, p, i, c, row0=0):
            n = p["all"] * p["turn"]
            return t[row0:row0 + n].rearrange("(i c q r) f -> i c q (r f)", c=CH, q=p["sub"], r=CR)[i + p["t0"], c]

        def cols(buf, p, c, rows_=D):
            w = p["turn"] // CH
            return buf[0:rows_, c * w:(c + 1) * w]

        def part(buf, p, c, q, rows_=D):
            if p["natural"]:
                w = p["turn"] // CH
                return buf[0:rows_, c * w + q:(c + 1) * w:CR]
            return buf[0:rows_, c * p["turn"] // CH + q * p["sub"]:c * p["turn"] // CH + (q + 1) * p["sub"]]

        def rowbuf(buf, p, c):
            return buf[0:p["sub"], c * GW:c * GW + CR * D].rearrange("p (q f) -> p q f", q=CR)

        def flat(buf, p, c):
            return buf[0:p["sub"], c * GW:c * GW + CR * D]

        def bank(p, c):
            return ps[0:D, DB + c, 0:CR * p["sub"]]

        def bank_rows(p, c):
            return ps[0:p["sub"], DB + c].rearrange("p (q f) -> p q f", q=CR)[:, :, 0:D]

        def small(buf, p, c):
            return buf[0:p["sub"], c]

        def nothing(step):
            pass

        def is_last(p, i):
            return isinstance(i, int) and i == p["turns"] - 1

        def columns(t, p, i, c):
            w = p["turn"] // CH
            return t[:, ds((i + p["t0"]) * p["turn"] + c * w, w)]

        def load_chain(p, i, c):
            if p["rows_in"]:
                nc.sync.dma_start(flat(xin, p, c), block_rows(p["x"], p, i, c)).then_inc(R(f"ld{c}"), 16)
            else:
                nc.sync.dma_start(cols(wx, p, c), columns(p["x"], p, i, c)).then_inc(R(f"ld{c}"), 16)

        def load_mask(p, i, c):
            w = p["turn"] // CH
            nc.sync.dma_start(w2[D:D + 1, c * w:(c + 1) * w],
                              ACTV[ds(i + p["t0"], 1), c * w:(c + 1) * w]).then_inc(R(f"mk{c}"), 16)

        FIRST, SECOND = (0, 1), (2, 3)

        def chain_turn(step_of, p, i, between, opening=False):
            half = CHAIN_GAPS // 2 + 1
            for step in range(CHAIN_GAPS):
                step_of(p, i, step, FIRST)
                if step + half < CHAIN_GAPS:
                    if not opening:
                        step_of(p, i - 1, step + half, SECOND)
                else:
                    step_of(p, i, step + half - CHAIN_GAPS, SECOND)
                between(step)

        def chain_close(step_of, p):
            for step in range(CHAIN_GAPS // 2 + 1, CHAIN_GAPS):
                step_of(p, p["turns"] - 1, step, SECOND)

        def chain_sp_step(p, i, step, cs):
            sp = nc.sync
            last, side = is_last(p, i), p["rows_in"]
            for c in cs:
                g = i * CH + c + 1
                if side and step == 1:
                    sp.wait_ge(R("tr"), dat(p, "tr", g))
                    sp.nop(nofuse=True)
                    if not last:
                        load_chain(p, i + 1, c)
                if not side and step == 3 and not last:
                    sp.wait_ge(R("p3"), dat(p, "p3", g))
                    sp.nop(nofuse=True)
                    load_chain(p, i + 1, c)
                if side and step in (2, 3):
                    sp.wait_ge(R("ev"), dat(p, "ev", event(i, step - 2, c) + 1))
                    sp.nop(nofuse=True)
                    sp.dma_start(block_rows(T[step - 1], p, i, c, EP), flat(rows, p, c)).then_inc(R(f"ro{c}"), 16)
                if side and step == 4:
                    sp.wait_ge(R("x1"), dat(p, "x1", g))
                    sp.nop(nofuse=True)
                    sp.dma_start(block_rows(T[3], p, i, c, EP), flat(wc, p, c)).then_inc(R(f"rp{c}"), 16)
                if side and step == 8:
                    sp.wait_ge(R("x2"), dat(p, "x2", g))
                    sp.nop(nofuse=True)
                    sp.dma_start(block_rows(T[4], p, i, c, EP), flat(wq, p, c)).then_inc(R(f"rq{c}"), 16)
                if step == 10:
                    sp.wait_ge(R("c2"), dat(p, "c2", g))
                    sp.nop(nofuse=True)
                    sp.dma_start(columns(p["to"], p, i, c), cols(w2, p, c)).then_inc(R(f"o{c}"), 16)
                    if not side and not last:
                        sp.wait_ge(R("pn"), dat(p, "pn", g))
                        sp.nop(nofuse=True)
                        load_mask(p, i + 1, c)

        def event(i, s, c):
            return i * (2 * CH) + (c // 2) * CH + s * 2 + c % 2

        def chain_pe_step(p, i, step, cs):
            pe = nc.tensor
            n = p["sub"]
            for c in cs:
                g = i * CH + c + 1
                if step == 0:
                    pe.wait_ge(R(f"ld{c}"), dat(p, f"ld{c}", (i + 1) * 16))
                    pe.wait_ge(R(p["last"]), dat(p, p["last"], g - CH))
                    if p["rows_in"]:
                        for q in range(CR):
                            ins = pe.transpose(ps[0:D, DB + c, q * n:(q + 1) * n],
                                               rowbuf(xin, p, c)[:, q], ident[0:n, 0:n])
                        ins.then_inc(R("tr"), 1)
                        pe.wait_ge(R("x0"), dat(p, "x0", g))
                    pe.matmul(bank(p, c), W["1"][0:D, 0:D], cols(wx, p, c), start=True, stop=True).then_inc(R("p1"), 1)
                if step in (1, 2):
                    pe.wait_ge(R("h1" if step == 1 else "h2"), dat(p, "h1" if step == 1 else "h2", g))
                    if p["rows_in"]:
                        e = event(i, step - 1, c)
                        pe.wait_ge(R("ev"), dat(p, "ev", i * (2 * CH) if (step, c) == (1, 0) else e - 1))
                        for q in range(CR):
                            ins = pe.transpose(ps[0:n, ZB + c % 2, q * D:(q + 1) * D], part(wh, p, c, q),
                                               ident[0:D, 0:D])
                        ins.then_inc(R("tp"), 1)
                if step == 1:
                    pe.matmul(bank(p, c), W["2"][0:D, 0:D], cols(wh, p, c), start=True, stop=True).then_inc(R("p2"), 1)
                if step == 2:
                    for q in range(CR):
                        o = ps[0:n, DB + c, q * P:(q + 1) * P]
                        pe.matmul(o, part(wx, p, c, q), cent[:], start=True, stop=False)
                        ins = pe.matmul(o, part(wh, p, c, q, D + 1), W3C[:], start=False, stop=True)
                    ins.then_inc(R("p3"), 1)
                if step == 4:
                    pe.wait_ge(R("x1"), dat(p, "x1", g))
                    for q in range(CR):
                        ins = pe.transpose(ps[0:D, DB + c, q * n:(q + 1) * n], rowbuf(wc, p, c)[:, q], ident[0:n, 0:n])
                    ins.then_inc(R("t1"), 1)
                if step == 5:
                    pe.wait_ge(R("e1"), dat(p, "e1", g))
                    for q in range(CR):
                        ins = pe.matmul(ps[0:n, DB + c, q * P:(q + 1) * P], part(w1, p, c, q, D + 1), W["G"][:],
                                        start=True, stop=True)
                    ins.then_inc(R("pg"), 1)
                if step == 8:
                    pe.wait_ge(R("x2"), dat(p, "x2", g))
                    for q in range(CR):
                        ins = pe.transpose(ps[0:D, DB + c, q * n:(q + 1) * n], rowbuf(wq, p, c)[:, q], ident[0:n, 0:n])
                    ins.then_inc(R("t2"), 1)
                if step == 9 and not p["rows_in"]:
                    pe.wait_ge(R("c2"), dat(p, "c2", g))
                    pe.wait_ge(R(f"mk{c}"), dat(p, f"mk{c}", (i + 1) * 16))
                    pe.matmul(bank(p, c), WN[:], cols(w2, p, c, D + 1), start=True, stop=True).then_inc(R("pn"), 1)

        def chain_act_step(p, i, step, cs):
            act = nc.scalar
            n = p["sub"]
            for c in cs:
                g = i * CH + c + 1
                if step == 0:
                    act.wait_ge(R("p1"), dat(p, "p1", g))
                    act.activation(cols(wh, p, c), bank(p, c), ACT.Relu, bias=col[:, B_1:B_1 + 1]).then_inc(R("h1"), 1)
                if step in (1, 2) and p["rows_in"]:
                    act.wait_ge(R("tp"), dat(p, "tp", event(i, step - 1, c) + 1))
                    act.wait_ge(R(f"ro{c}"), dat(p, f"ro{c}", i * 32 + 16 * (step - 1)))
                    act.activation(flat(rows, p, c), ps[0:n, ZB + c % 2, 0:CR * D], ACT.Copy).then_inc(R("ev"), 1)
                if step == 2:
                    act.wait_ge(R("p3"), dat(p, "p3", g))
                    if p["rows_in"]:
                        act.wait_ge(R(f"rq{c}"), dat(p, f"rq{c}", i * 16))
                    act.activation(rowbuf(wq, p, c), bank_rows(p, c), ACT.Square).then_inc(R("q1"), 1)
                if step == 3:
                    act.wait_ge(R("s1"), dat(p, "s1", g))
                    act.activation(small(dsd, p, c), small(dss, p, c), ACT.Sqrt, bias=epsc[0:n, 0:1],
                                   scale=1.0 / D).then_inc(R("d1"), 1)
                if step == 4:
                    act.wait_ge(R("t1"), dat(p, "t1", g))
                    act.activation(cols(w1, p, c), bank(p, c), ACT.Copy).then_inc(R("e1"), 1)
                if step == 5:
                    act.wait_ge(R("pg"), dat(p, "pg", g))
                    act.activation(rowbuf(wq, p, c), bank_rows(p, c), ACT.Tanh).then_inc(R("th"), 1)
                if step == 7:
                    act.wait_ge(R("mv"), dat(p, "mv", g))
                    act.activation(small(dsd, p, c), dmv[0:n, c, :, 1], ACT.Sqrt, bias=epsc[0:n, 0:1]).then_inc(R("d2"), 1)
                if step == 9 and not p["rows_in"]:
                    k = (i + p["t0"]) * CH + c
                    act.wait_ge(R("pn"), dat(p, "pn", g))
                    act.activation(cols(wh, p, c), bank(p, c), ACT.Relu, bias=col[:, B_N:B_N + 1],
                                   accum_out=stN[:, 0, ds(k, 1)]).then_inc(R("rn"), 1)
                if step == 10 and not p["rows_in"]:
                    k = (i + p["t0"]) * CH + c
                    act.wait_ge(R("rn"), dat(p, "rn", g))
                    act.activation(cols(wh, p, c), cols(wh, p, c), ACT.Square,
                                   accum_out=stN[:, 1, ds(k, 1)]).then_inc(R("qn"), 1)

        def over_row(ap, p):
            return ap.unsqueeze(2).to_broadcast([p["sub"], CR, D])

        def chain_dve_step(p, i, step, cs):
            dve = nc.vector
            n = p["sub"]
            for c in cs:
                g = i * CH + c + 1
                if step == 0 and p["rows_in"]:
                    dve.wait_ge(R("tr"), dat(p, "tr", g))
                    dve.tensor_copy(cols(wx, p, c), bank(p, c)).then_inc(R("x0"), 1)
                if step == 1:
                    dve.wait_ge(R("p2"), dat(p, "p2", g))
                    dve.tensor_scalar(cols(wh, p, c), bank(p, c), col[:, B_2:B_2 + 1], 0.0, ALU.add, ALU.max).then_inc(R("h2"), 1)
                if step == 2:
                    dve.wait_ge(R("q1"), dat(p, "q1", g))
                    dve.tensor_reduce(small(dss, p, c), rowbuf(wq, p, c), AX_X, ALU.add).then_inc(R("s1"), 1)
                if step == 3:
                    dve.wait_ge(R("d1"), dat(p, "d1", g))
                    dve.reciprocal(small(drs, p, c), small(dsd, p, c)).then_inc(R("r1"), 1)
                if step == 5:
                    dve.wait_ge(R("th"), dat(p, "th", g))
                    dve.tensor_tensor(rowbuf(wq, p, c), rowbuf(wq, p, c), rowbuf(wc, p, c), ALU.add).then_inc(R("y"), 1)
                if step == 7:
                    dve.wait_ge(R("d2"), dat(p, "d2", g))
                    dve.reciprocal(small(drs, p, c), small(dsd, p, c)).then_inc(R("r2"), 1)
                if step == 8:
                    dve.wait_ge(R("t2"), dat(p, "t2", g))
                    dve.wait_ge(R(f"o{c}"), dat(p, f"o{c}", i * 16))
                    dve.tensor_copy(cols(w2, p, c), bank(p, c)).then_inc(R("c2"), 1)
            for c in cs:
                g = i * CH + c + 1
                if step == 3:
                    dve.wait_ge(R("r1"), dat(p, "r1", g))
                    if p["rows_in"]:
                        dve.wait_ge(R(f"rp{c}"), dat(p, f"rp{c}", i * 16))
                    dve.tensor_tensor(rowbuf(wc, p, c), bank_rows(p, c), over_row(small(drs, p, c), p),
                                      ALU.mult).then_inc(R("x1"), 1)
                if step == 6:
                    dve.wait_ge(R("y"), dat(p, "y", g))
                    for q in range(CR):
                        ins = dve.bn_stats(dst6[0:n, c, q], rowbuf(wq, p, c)[:, q])
                    ins.then_inc(R("st"), 1)
                if step == 7:
                    dve.wait_ge(R("r2"), dat(p, "r2", g))
                    for q in range(CR):
                        ins = dve.tensor_scalar(rowbuf(wq, p, c)[:, q], rowbuf(wq, p, c)[:, q],
                                                dmv[0:n, c, q, 0:1], drs[0:n, c, q:q + 1],
                                                ALU.subtract, ALU.mult)
                    ins.then_inc(R("x2"), 1)
            if step == 6:
                for c in cs:
                    dve.wait_ge(R("st"), dat(p, "st", i * CH + c + 1))
                    dve.nop(nofuse=True)
                    for q in range(CR):
                        ins = dve.bn_aggr(dmv[0:n, c, q], dst6[0:n, c, q])
                    ins.then_inc(R("mv"), 1)

        def chain_sp_turn(p, i, between):
            chain_turn(chain_sp_step, p, i, between)

        def chain_pe_turn(p, i, between):
            chain_turn(chain_pe_step, p, i, between)

        def chain_act_turn(p, i, between):
            chain_turn(chain_act_step, p, i, between)

        def chain_dve_turn(p, i, between):
            chain_turn(chain_dve_step, p, i, between)

        def chain_sp_start(p):
            for c in range(CH):
                load_chain(p, 0, c)
                if not p["rows_in"]:
                    load_mask(p, 0, c)
            chain_turn(chain_sp_step, p, 0, nothing, opening=True)

        def dense_pe_start(p):
            nc.tensor.sem_inc(R(p["last"]), CH)

        def chain_pe_start(p):
            dense_pe_start(p)
            chain_turn(chain_pe_step, p, 0, nothing, opening=True)

        def chain_act_start(p):
            chain_turn(chain_act_step, p, 0, nothing, opening=True)

        def chain_dve_start(p):
            chain_turn(chain_dve_step, p, 0, nothing, opening=True)

        def chain_sp(p, first):
            sp = nc.sync
            if first < p["turns"] - 1:
                with sp.Fori(first, p["turns"] - 1) as i:
                    chain_sp_turn(p, i, nothing)
            if first < p["turns"]:
                chain_sp_turn(p, p["turns"] - 1, nothing)
            chain_close(chain_sp_step, p)
            for c in range(CH):
                sp.wait_ge(R(f"o{c}"), dat(p, f"o{c}", 16 * p["turns"]))
                if p["rows_in"]:
                    sp.wait_ge(R(f"ro{c}"), dat(p, f"ro{c}", 32 * p["turns"]))
                    sp.wait_ge(R(f"rp{c}"), dat(p, f"rp{c}", 16 * p["turns"]))
                    sp.wait_ge(R(f"rq{c}"), dat(p, f"rq{c}", 16 * p["turns"]))

        def chain_rest(eng, step_of, p, first):
            if first < p["turns"]:
                with eng.Fori(first, p["turns"]) as i:
                    chain_turn(step_of, p, i, nothing)
            chain_close(step_of, p)

        def chain_pe(p, first):
            chain_rest(nc.tensor, chain_pe_step, p, first)

        def chain_act(p, first):
            chain_rest(nc.scalar, chain_act_step, p, first)

        def chain_dve(p, first):
            chain_rest(nc.vector, chain_dve_step, p, first)

        def load_end(p, i, c):
            nc.sync.dma_start(cols(w2, p, c), columns(p["x"], p, i, c)).then_inc(R(f"ld{c}"), 16)

        def end_sp_start(p):
            for c in range(CH):
                load_end(p, 0, c)

        def end_sp_turn(p, i, between):
            sp = nc.sync
            between(0)
            for c in range(CH):
                sp.wait_ge(R("p3"), dat(p, "p3", i * CH + c + 1))
                sp.nop(nofuse=True)
                if not is_last(p, i):
                    load_end(p, i + 1, c)
            for c in range(CH):
                sp.wait_ge(R("y"), dat(p, "y", i * CH + c + 1))
                sp.nop(nofuse=True)
                sp.dma_start(block_rows(p["to"], p, i, c, p["row0"]), flat(wc, p, c)).then_inc(R(f"ro{c}"), 16)
            between(1)

        def end_sp(p, first=0):
            sp = nc.sync
            if first == 0:
                end_sp_start(p)
            if p["turns"] - 1 > first:
                with sp.Fori(first, p["turns"] - 1) as i:
                    end_sp_turn(p, i, nothing)
            end_sp_turn(p, p["turns"] - 1, nothing)
            for c in range(CH):
                sp.wait_ge(R(f"ro{c}"), dat(p, f"ro{c}", 16 * p["turns"]))

        def end_pe_turn(p, i, between):
            pe = nc.tensor
            for c in range(CH):
                pe.wait_ge(R(f"ld{c}"), dat(p, f"ld{c}", (i + 1) * 16))
                pe.wait_ge(R("y"), dat(p, "y", i * CH + c + 1 - CH))
                pe.matmul(bank(p, c), WN[0:D], cols(w2, p, c), start=True, stop=True).then_inc(R("pn"), 1)
            between(0)
            for c in range(CH):
                pe.wait_ge(R("rn"), dat(p, "rn", i * CH + c + 1))
                for q in range(CR):
                    o = ps[0:p["sub"], DB + c, q * P:(q + 1) * P]
                    pe.matmul(o, part(w2, p, c, q), cent[:], start=True, stop=False)
                    ins = pe.matmul(o, part(wh, p, c, q, D + 1), AN[:], start=False, stop=True)
                ins.then_inc(R("p3"), 1)
            between(1)

        def end_pe(p, first=0):
            if first == 0:
                dense_pe_start(p)
            with nc.tensor.Fori(first, p["turns"]) as i:
                end_pe_turn(p, i, nothing)

        def end_act_turn(p, i, between):
            act = nc.scalar
            sc, bi = (1.0, 0) if p["row0"] else (1.0 + EPS, 1)
            for c in range(CH):
                act.wait_ge(R("pn"), dat(p, "pn", i * CH + c + 1))
                act.activation(cols(wh, p, c), bank(p, c), ACT.Relu, bias=col[:, B_N:B_N + 1]).then_inc(R("rn"), 1)
            between(0)
            for c in range(CH + 1):
                if c < CH:
                    act.wait_ge(R("p3"), dat(p, "p3", i * CH + c + 1))
                    act.activation(rowbuf(wq, p, c), bank_rows(p, c), ACT.Square).then_inc(R("q1"), 1)
                if c:
                    act.wait_ge(R("s1"), dat(p, "s1", i * CH + c))
                    act.activation(small(dsd, p, c - 1), small(dss, p, c - 1), ACT.Sqrt,
                                   bias=epsc[0:p["sub"], bi:bi + 1], scale=sc / D).then_inc(R("d1"), 1)
            between(1)

        def end_act(p, first=0):
            with nc.scalar.Fori(first, p["turns"]) as i:
                end_act_turn(p, i, nothing)

        def end_dve_turn(p, i, between):
            dve = nc.vector
            between(0)
            for c in range(CH + 1):
                if c < CH:
                    dve.wait_ge(R("q1"), dat(p, "q1", i * CH + c + 1))
                    dve.tensor_reduce(small(dss, p, c), rowbuf(wq, p, c), AX_X, ALU.add).then_inc(R("s1"), 1)
                if c:
                    k = c - 1
                    dve.wait_ge(R("d1"), dat(p, "d1", i * CH + k + 1))
                    dve.reciprocal(small(drs, p, k), small(dsd, p, k)).then_inc(R("r1"), 1)
                    dve.wait_ge(R("r1"), dat(p, "r1", i * CH + k + 1))
                    dve.wait_ge(R(f"ro{k}"), dat(p, f"ro{k}", i * 16))
                    dve.tensor_tensor(rowbuf(wc, p, k), bank_rows(p, k), over_row(small(drs, p, k), p),
                                      ALU.mult).then_inc(R("y"), 1)
            between(1)

        def end_dve(p, first=0):
            with nc.vector.Fori(first, p["turns"]) as i:
                end_dve_turn(p, i, nothing)

        def norm_dve(k, s, q, count, g, b, ac, sc):
            dve = nc.vector
            t = tmp[0][0:D]
            link(dve, "dve", dve.tensor_scalar(t[:, 0:1], s, 1.0 / count, None, ALU.mult))
            link(dve, "dve", dve.tensor_scalar(t[:, 1:2], q, 1.0 / count, None, ALU.mult))
            link(dve, "dve", dve.tensor_tensor(t[:, 2:3], t[:, 0:1], t[:, 0:1], ALU.mult))
            dve.tensor_tensor(t[:, 3:4], t[:, 1:2], t[:, 2:3], ALU.subtract).then_inc(sem("norm_var"), 1)
            dve.wait_ge(sem("norm_root"), k)
            link(dve, "dve", dve.reciprocal(t[:, 5:6], t[:, 4:5]))
            link(dve, "dve", dve.tensor_tensor(col[:, ac:ac + 1], col[:, g:g + 1], t[:, 5:6], ALU.mult))
            link(dve, "dve", dve.tensor_tensor(t[:, 6:7], t[:, 0:1], col[:, ac:ac + 1], ALU.mult))
            link(dve, "dve", dve.tensor_tensor(col[:, sc:sc + 1], col[:, b:b + 1], t[:, 6:7], ALU.subtract))

        def norm_act(k):
            act = nc.scalar
            act.wait_ge(sem("norm_var"), k)
            act.activation(tmp[0][0:D, 4:5], tmp[0][0:D, 3:4], ACT.Sqrt, bias=epsc[0:D, 0:1]).then_inc(sem("norm_root"), 1)

        CHAIN = "tr x0 p1 h1 p2 h2 p3 q1 s1 d1 r1 x1 t1 e1 pg th y st mv d2 r2 x2 t2 c2 pn rn qn tp ev"
        DENSE_DMA = "ld mk o ro rp rq"
        chain_sig = "p1 h1 p2 h2 p3 q1 s1 d1 r1 x1 t1 e1 pg th y st mv d2 r2 x2 t2 c2"
        end_sig = "pn rn p3 q1 s1 d1 r1 y"
        side = dict(turns=NL, all=NL, turn=STURN, sub=P, natural=False)
        nodes = dict(all=ND, turn=TURN, sub=NSUB, natural=False, x=a["xT"], to=X2T, rows_in=False, last="qn",
                     slots=dict(ld=1, o=1, mk=1), gaps=CHAIN_GAPS)
        add_dense("dense1", chain_sig + " pn rn qn", turns=DENSE1, **nodes)
        add_dense("source", chain_sig + " tr x0 tp ev", x=XS, to=X2L, rows_in=True, last="c2",
                  slots=dict(ld=1, o=1, ro=2, rp=1, rq=1), gaps=CHAIN_GAPS, **side)
        add_dense("dense2", chain_sig + " pn rn qn", turns=ND - DENSE1, t0=DENSE1, **nodes)
        add_dense("source3", end_sig, x=X2L, to=T[5], row0=EP, last="y", slots=dict(ld=1, ro=1), gaps=END_GAPS,
                  **side)
        add_dense("final", end_sig, x=X2T, to=a["out"], row0=0, last="y", slots=dict(ld=1, ro=1), gaps=END_GAPS,
                  turns=ND, all=ND, turn=TURN, sub=NSUB, natural=True)
        PQ, DQ = PASSES, DENSE

        def beside(name, first, m):
            return dict(dense=DQ[name], first=first, turns=m)
        ln_sig = "S seg mask z cv out y st mv sq rc "
        GS = 2 + 2 * NI
        add_pass("tab_put", kind="tab", staged=NI, slots=(TG, 0, 0, 0, 0))
        add_pass("emlp", "cv th out", slots=(0, 1, 0, 0, 0), kind="emlp")
        add_pass("tab_get", kind="tab", gather=(gs_i,), staged=GS, slots=(TG, 0, 0, 0, 0), beside=beside("dense1", 1, 1))
        add_pass("copy", kind="copy", gather=(gs_i, gd_i), ngather=2, to=(XS, XD), staged=GS,
                 slots=(2 * TG, 0, 0, 0, 2), beside=beside("dense1", NI + 1, 2))
        add_pass("conv1", "S D seg mask z cv out", NJ, slots=(0, 1, 1, 0, 1), kind="conv", m=XS, s=XD, own=True,
                 w=wE, W=W["1"], tail="relu", out=T[1])
        add_pass("conv2", "S D seg mask z cv out", NJ, GS, slots=(TG, 0, 1, 0, 1), kind="conv", gather=(gi_i,),
                 table=T[1], s=T[1], own=True, w=wE, W=W["2"], tail="relu", out=T[2], beside=beside("dense2", 1, 1))
        add_pass("conv3", ln_sig + "D", NJ, GS, slots=(TG, 0, 1, 1, 1), kind="conv", gather=(gi_i,),
                 table=T[2], s=T[2], r=XD, own=True, w=wE, W=W["3"], tail="ln", out=T[3], beside=beside("dense2", NI + 1, 1))
        add_pass("att", "y out", 0, GS, slots=(TG, 0, 1, 0, 1), kind="att", gather=(gi_i,), s=T[3], beside=beside("dense2", 2 * NI + 1, 1))
        add_pass("gat", ln_sig + "D th", NJ, slots=(0, 1, 1, 0, 1), kind="conv", m=GX, s=T[3], own=True,
                 w=wE, W=W["G"], tail="tanh", out=T[4])
        add_pass("mlp", "seg y cv th out", slots=(0, 1, 1, 0, 1), kind="mlp", s=T[4])
        add_pass("msg", "S D seg mask z cv y th u sq out", NJ, GS, slots=(2 * TG, 1, 0, 0, 1), kind="msg",
                 gather=(gi_i, gr_i), ngather=2)
        add_pass("join", "cv y st mv sq rc out", slots=(0, 1, 1, 1, 1), kind="join", tail="copy")
        add_pass("hop1", "S seg mask z cv out", NJ, GS, slots=(TG, 0, 0, 0, 1), kind="conv", gather=(gi_i,),
                 table=T[5], w=wE, W=W["I"], tail="plain", out=TN, beside=beside("final", 0, 4))
        add_pass("hop2", ln_sig + "u", NJ, GS, slots=(TG, 0, 1, 1, 1, TG), kind="conv", gather=(gn_i,),
                 table=TN, s=T[5], r=TN, w=wE, W=W["I"], tail="half", scatter=go_i)
        loaded = sem("loaded")
        n_loads = [0]

        def prepare_sp():
            sp = nc.sync
            sp.wait_ge(sem("cleared"), 1)

            def ld(dst, src):
                n_loads[0] += 1
                sp.dma_start(dst, src).then_inc(loaded, 16)
            r = lambda v: a[v].rearrange("(o f) -> o f", o=1)
            c = lambda v: a[v].rearrange("(f o) -> f o", o=1)
            ld(ident[:], a["ident"])
            ld(cent[:], a["cent"])
            for k, wn, bn in (("1", "L0_gnn_W1", "L0_gnn_b1"), ("2", "L0_gnn_W2", "L0_gnn_b2"),
                              ("3", "L0_gnn_W3", "L0_gnn_b3"), ("G", "L1_gnn_W", "L1_gnn_bias")):
                ld(W[k][0:D, 0:D], a[wn])
                ld(W[k][D:D + 1, 0:D], r(bn))
            ld(W["I"][:, 0:D], a["eye_row"])
            ld(WN[0:D], a["L2_gnn_W_node"])
            ld(WE[2:2 + DE, 0:D], a["L2_gnn_W_edge"])
            ld(WE[0:1, 0:D], r("L2_gnn_b_edge"))
            ld(WE[0:2, D:D + 2], a["ident"][0:2, 0:2])
            ld(WM[:, :, 0:D], a["L2_gnn_W_msg"].rearrange("(k f) n -> f k n", k=3))
            ld(mb2[D:D + 1, 0:D], r("L2_gnn_b_msg"))
            for k, v in ((B_1, "L0_gnn_b1"), (B_2, "L0_gnn_b2"), 
                         (B_N, "L2_gnn_b_node"), (G_N, "L2_gnn_g_node"),
                         (BE_N, "L2_gnn_beta_node"), (G_E, "L2_gnn_g_edge"), (BE_E, "L2_gnn_beta_edge"),
                         (G_M, "L2_gnn_g_msg"), (BE_M, "L2_gnn_beta_msg")):
                ld(col[:, k:k + 1], c(v))
            ld(att[:, 0:1], c("L1_gnn_att_src"))
            ld(att[:, 1:2], c("L1_gnn_att_dst"))
            ld(src_i[:], a["src_cols"])
            ld(dst_i[:], a["dst_cols"])
            ld(own[:], a["own_cols"])
            ld(ownr[:], a["own_rows"])
            for b, (t0, n) in enumerate(RB):
                for k in range(3):
                    ld(dl_i[0:n, b, k], a["dst_line"][k + t0 * P:k + (t0 + n) * P].rearrange("(t e) -> t e", e=P))
            for h in (0, 1):
                r0, nr = EP + h * (LR - EP) // 2, (LR - EP) // 2
                ld(XS[r0:r0 + nr].rearrange("(p a) f -> p (a f)", p=P), zero[:, 0:nr // P * D])
            for h in range(2):
                ld(TAB[h * N // 2:(h + 1) * N // 2].rearrange("(p a) f -> p (a f)", p=125), zero[0:125, 0:800])
            ld(TN[EP:EP + P], zero[:, 0:D])
            sp.wait_ge(loaded, 16 * n_loads[0])
            sp.sem_inc(sem("ready"), 1)
            sp.wait_ge(sem("lines"), 1)
            m = 0
            for b, (t0, n) in enumerate(RB):
                v = lambda t: t[t0 * P:(t0 + n) * P].rearrange("(t e) -> t e", e=P)
                for dst, src in ((v(LID), lid_b[0:n, b]), (v(LINE[0]), rv[5][0:n, b]), (v(LINE[1]), onesr[0:n, b]),
                                 (v(LINE[2]), rv[2][0:n, b]),
                                 (CONT[t0:t0 + n].rearrange("(t o) -> t o", o=1), rcol[0:n, b, 6:7])):
                    sp.dma_start(dst, src).then_inc(sem("lined"), 16)
                    m += 16
            sp.wait_ge(sem("lined"), m)
            sp.dma_start(lidB[:], LID.rearrange("(o e) -> o e", o=1).to_broadcast([P, EP])).then_inc(sem("lined"), 16)
            sp.dma_start(contB[:], CONT.rearrange("(o e) -> o e", o=1).to_broadcast([P, ET])).then_inc(sem("lined"), 16)
            sp.wait_ge(sem("lined"), m + 32)

        def prepare_dve():
            dve = nc.vector
            for t, v in ((ones, 1.0), (onesr, 1.0), (one, 1.0), (zero, 0.0), (WE, 0.0), (mb2, 0.0),
                         (zT, 1.0), (gs_i, 0), (gd_i, 0), (gi_i, 0), (gr_i, 0), (gn_i, 0), (go_i, N), (tabs, 0.0)):
                link(dve, "dve", dve.memset(t[:], v))
            link(dve, "dve", dve.memset(WN[D:D + 1], -BIG))
            link(dve, "dve", dve.memset(mb2[D:D + 2], -BIG))
            for t in list(W.values()) + [W3C, AN, AM, WM, WM3]:
                link(dve, "dve", dve.memset(t[:], 0.0))
            link(dve, "dve", dve.memset(wh[D:D + 1], 1.0))
            link(dve, "dve", dve.memset(w1[D:D + 1], 1.0))
            link(dve, "dve", dve.memset(epsc[:, 0:1], EPS))
            link(dve, "dve", dve.memset(epsc[:, 1:2], EPS * EPS))
            dve.sem_inc(sem("cleared"), 1)
            dve.wait_ge(sem("ready"), 1)
            L = lambda ins: link(dve, "dve", ins)
            dve.wait_ge(sem("w_pe"), 1)
            L(dve.tensor_copy(wt[:, 0, 0:D + 1], ps[0:D, DB, 0:D + 1]))
            L(dve.tensor_copy(wt[:, 1, 0:D], ps[0:D, DB, P:P + D]))
            L(dve.tensor_scalar(attB[:, 0], ones[0:D], att[:, 0:1], None, ALU.mult))
            dve.tensor_scalar(attB[:, 1], ones[0:D], att[:, 1:2], None, ALU.mult).then_inc(sem("w_dve"), 1)
            dve.wait_ge(sem("w_pe"), 2)
            L(dve.tensor_copy(W3C[:, 0:D], ps[0:D + 1, DB + 1, 0:D]))
            for k in range(2):
                L(dve.tensor_copy(uv[:, k], ps[:, DB + 2, k * P:k * P + D]))
            L(dve.tensor_copy(gs_i[:, 0:ET], src_i[:]))
            L(dve.tensor_copy(tmp[1][:], dst_i[:]))
            L(dve.tensor_scalar(gd_i[:, 0:ET], tmp[1][:], float(N - 1), None, ALU.min))
            blocks(lambda n, b: dve.tensor_copy(dl[0:n, b], dl_i[0:n, b]))
            blocks(lambda n, b: dve.tensor_tensor(keepF[0:n, b], dl[0:n, b, 1], dl[0:n, b, 0], ALU.is_equal))
            blocks(lambda n, b: dve.tensor_tensor(keepB[0:n, b], dl[0:n, b, 1], dl[0:n, b, 2], ALU.is_equal))
            blocks(lambda n, b: dve.tensor_scalar(penF[0:n, b], keepF[0:n, b], 1.0, BIG, ALU.subtract, ALU.mult))
            blocks(lambda n, b: dve.tensor_scalar(penB[0:n, b], keepB[0:n, b], 1.0, BIG, ALU.subtract, ALU.mult))
            for k, v in enumerate((keepF, keepB, penF, penB)):
                blocks(lambda n, b: dve.tensor_reduce(rcol[0:n, b, 1 + k:2 + k], v[0:n, b], AX_X, ALU.min))
            dve.sem_inc(sem("keep_cols"), 1)
            dve.wait_ge(sem("keep_rows"), 1)
            for k in range(4):
                L(dve.tensor_copy(krow[0:1, k], ps[0:1, DB + k, 0:ET]))
            blocks(lambda n, b: dve.tensor_scalar(rv[0][0:n, b], keepF[0:n, b], -1.0, 1.0, ALU.mult, ALU.add))
            blocks(lambda n, b: dve.memset(rv[0][0:n, b, 0:1], 0.0))
            blocks(lambda n, b: dve.tensor_tensor_scan(rv[1][0:n, b], onesr[0:n, b], rv[0][0:n, b], 0.0, ALU.mult, ALU.add))
            blocks(lambda n, b: dve.tensor_copy(lid_b[0:n, b], rv[1][0:n, b]))
            blocks(lambda n, b: dve.tensor_scalar(rcol[0:n, b, 6:7], keepF[0:n, b, 0:1], 1.0, None, ALU.subtract))
            to_cols_dve(lid)
            scan_dve(rv[3], onesr, keepF, krow[0:1, 0], True)
            scan_dve(rv[4], onesr, keepB, krow[0:1, 1], False)
            blocks(lambda n, b: dve.scalar_tensor_tensor(out=rv[5][0:n, b], in0=rv[3][0:n, b], scalar=-1.0,
                                                         in1=rv[4][0:n, b], op0=ALU.add, op1=ALU.add))
            blocks(lambda n, b: dve.scalar_tensor_tensor(out=rv[6][0:n, b], in0=rv[4][0:n, b], scalar=-1.0,
                                                         in1=ownr[0:n, b], op0=ALU.add, op1=ALU.add))
            blocks(lambda n, b: dve.tensor_scalar(rv[0][0:n, b], keepB[0:n, b], -1.0, 1.0, ALU.mult, ALU.add))
            blocks(lambda n, b: dve.scalar_tensor_tensor(out=rv[7][0:n, b], in0=dl[0:n, b, 1], scalar=float(N),
                                                         in1=rv[0][0:n, b], op0=ALU.is_lt, op1=ALU.mult))
            blocks(lambda n, b: dve.tensor_scalar(rv[2][0:n, b], rv[7][0:n, b], -1.0, 1.0, ALU.mult, ALU.add))
            dve.sem_inc(sem("lines"), 1)
            to_cols_dve(deg)
            to_cols_dve(repf)
            to_cols_dve(isrep)
            L(dve.tensor_copy(gr_i[:, 0:ET], repf[:]))
            L(dve.tensor_scalar(tmp[1][:], tmp[1][:], float(N), None, ALU.subtract))
            L(dve.tensor_tensor(tmp[1][:], tmp[1][:], isrep[:], ALU.mult))
            L(dve.tensor_scalar(go_i[:, 0:ET], tmp[1][:], float(N), None, ALU.add))
            L(dve.tensor_copy(tabs[:, 0:ET, 0], repf[:]))
            L(dve.tensor_copy(tabs[:, 0:ET, 1], deg[:]))

        def prepare_pe():
            pe = nc.tensor
            pe.wait_ge(sem("ready"), 1)
            pe.transpose(ps[0:D, DB, 0:D + 1], W["3"][:, 0:D], ident[0:D + 1, 0:D + 1])
            pe.transpose(ps[0:D, DB, P:P + D], W["G"][0:D, 0:D], ident[0:D, 0:D]).then_inc(sem("w_pe"), 1)
            pe.wait_ge(sem("w_dve"), 1)
            pe.matmul(ps[0:D + 1, DB + 1, 0:P], wt[:, 0, 0:D + 1], cent[:], start=True, stop=True)
            for k in range(2):
                ins = pe.matmul(ps[:, DB + 2, k * P:k * P + D], attB[:, k], wt[:, 1, 0:D], start=True, stop=True)
            ins.then_inc(sem("w_pe"), 1)
            pe.wait_ge(sem("keep_cols"), 1)
            for k in range(4):
                for b, (t0, n) in enumerate(RB):
                    ins = pe.transpose(ps[0:1, DB + k, t0:t0 + n], rcol[0:n, b, 1 + k:2 + k], ident[0:n, 0:n])
            ins.then_inc(sem("keep_rows"), 1)
            to_cols_pe(rv[1])
            scan_pe(rv[3], True)
            scan_pe(rv[4], False)
            to_cols_pe(rv[5])
            to_cols_pe(rv[6])
            to_cols_pe(rv[7])

        def index_dve():
            dve = nc.vector
            L = lambda ins: link(dve, "dve", ins)
            s_, d_, A, B = tabs[:, 0:ET, 0], tabs[:, 0:ET, 1], tmp[2][:], tmp[3][:]
            L(dve.tensor_scalar(A, d_, 0.0, None, ALU.is_gt))
            L(dve.tensor_tensor(B, s_, own[:], ALU.subtract))
            L(dve.tensor_scalar(B, B, float(EP), None, ALU.subtract))
            L(dve.tensor_tensor(B, B, A, ALU.mult))
            L(dve.tensor_tensor(B, B, own[:], ALU.add))
            L(dve.tensor_scalar(gi_i[:, 0:ET], B, float(EP), None, ALU.add))
            L(dve.tensor_scalar(B, s_, float(EP), None, ALU.subtract))
            L(dve.tensor_tensor(B, B, A, ALU.mult))
            L(dve.tensor_scalar(gn_i[:, 0:ET], B, float(EP), None, ALU.add))
            L(dve.tensor_scalar(A, d_, 1.0, None, ALU.add))
            dve.tensor_scalar(B, deg[:], 1.0, None, ALU.add).then_inc(sem("deg1"), 1)
            dve.wait_ge(sem("deg_root"), 1)
            L(dve.reciprocal(A, A))
            L(dve.reciprocal(B, B))
            L(dve.tensor_tensor(wE[:], A, B, ALU.mult))
            L(dve.tensor_tensor(B, B, B, ALU.mult))
            L(dve.tensor_tensor(wS[:], B, isrep[:], ALU.mult))

        def active_dve():
            dve = nc.vector
            L = lambda ins: link(dve, "dve", ins)
            half = TURN // 2
            dve.wait_ge(sem("tab_in"), 32)
            for h, t in enumerate((wx, wh)):
                src = t[0:ND, 0:2 * half].rearrange("i (n two) -> i n two", two=2)[:, :, 1]
                dst = wc[0:ND, h * half:(h + 1) * half]
                L(dve.tensor_scalar(dst, src, 0.0, None, ALU.is_gt))
            dve.sem_inc(sem("active"), 1)

        def index_act():
            act = nc.scalar
            act.wait_ge(sem("deg1"), 1)
            act.activation(tmp[2][:], tmp[2][:], ACT.Sqrt)
            act.activation(tmp[3][:], tmp[3][:], ACT.Sqrt).then_inc(sem("deg_root"), 1)

        def active_sp():
            sp = nc.sync
            half = TURN // 2
            for h, t in enumerate((wx, wh)):
                sp.dma_start(t[0:ND, 0:2 * half],
                             TAB.rearrange("(i h n) two -> i h (n two)", h=2, n=half)[:, h]).then_inc(sem("tab_in"), 16)
            sp.wait_ge(sem("active"), 1)
            sp.dma_start(ACTV, wc[0:ND, 0:TURN]).then_inc(sem("active_out"), 16)
            sp.wait_ge(sem("active_out"), 16)

        def soft_dve():
            dve = nc.vector
            asr, adr, aor = rv[0], rv[1], rv[2]
            to_rows_dve(asr)
            to_rows_dve(adr)
            to_rows_dve(aor)
            blocks(lambda n, b: dve.tensor_scalar(rv[7][0:n, b], keepB[0:n, b], -1.0, 1.0, ALU.mult, ALU.add))
            blocks(lambda n, b: dve.tensor_tensor(adr[0:n, b], adr[0:n, b], rv[7][0:n, b], ALU.mult))
            blocks(lambda n, b: dve.tensor_tensor(aor[0:n, b], aor[0:n, b], rv[7][0:n, b], ALU.mult))
            scan_dve(rv[3], adr, keepB, krow[0:1, 1], False)
            scan_dve(rv[4], aor, keepB, krow[0:1, 1], False)
            for x in (asr, rv[4]):
                blocks(lambda n, b: dve.tensor_tensor(x[0:n, b], x[0:n, b], rv[3][0:n, b], ALU.add))
                blocks(lambda n, b: dve.scalar_tensor_tensor(out=x[0:n, b], in0=x[0:n, b], scalar=SLOPE, in1=x[0:n, b],
                                                             op0=ALU.mult, op1=ALU.max))
            scan_dve(rv[1], asr, penF, krow[0:1, 2], True, summed=False)
            scan_dve(rv[2], asr, penB, krow[0:1, 3], False, summed=False)
            blocks(lambda n, b: dve.tensor_tensor(rv[1][0:n, b], rv[1][0:n, b], rv[2][0:n, b], ALU.max))
            blocks(lambda n, b: dve.tensor_tensor(rv[1][0:n, b], rv[1][0:n, b], rv[4][0:n, b], ALU.max))
            blocks(lambda n, b: dve.tensor_tensor(rv[5][0:n, b], asr[0:n, b], rv[1][0:n, b], ALU.subtract))
            blocks(lambda n, b: dve.tensor_tensor(rv[6][0:n, b], rv[4][0:n, b], rv[1][0:n, b], ALU.subtract))
            dve.sem_inc(sem("logits"), 1)
            dve.wait_ge(sem("exps"), 1)
            scan_dve(rv[1], rv[5], keepF, krow[0:1, 0], True)
            scan_dve(rv[2], rv[5], keepB, krow[0:1, 1], False)
            blocks(lambda n, b: dve.tensor_tensor(rv[1][0:n, b], rv[1][0:n, b], rv[5][0:n, b], ALU.subtract))
            blocks(lambda n, b: dve.tensor_tensor(rv[1][0:n, b], rv[1][0:n, b], rv[2][0:n, b], ALU.add))
            blocks(lambda n, b: dve.tensor_tensor(rv[1][0:n, b], rv[1][0:n, b], rv[6][0:n, b], ALU.add))
            blocks(lambda n, b: dve.tensor_scalar(rv[1][0:n, b], rv[1][0:n, b], 1e-16, None, ALU.add))
            blocks(lambda n, b: dve.reciprocal(rv[1][0:n, b], rv[1][0:n, b]))
            blocks(lambda n, b: dve.tensor_tensor(rv[5][0:n, b], rv[5][0:n, b], rv[1][0:n, b], ALU.mult))
            blocks(lambda n, b: dve.tensor_tensor(rv[6][0:n, b], rv[6][0:n, b], rv[1][0:n, b], ALU.mult))
            to_cols_dve(wE)
            to_cols_dve(wS)
            link(dve, "dve", dve.tensor_tensor(wS[:], wS[:], isrep[:], ALU.mult))

        def soft_pe():
            to_rows_pe(a_s)
            to_rows_pe(a_d)
            to_rows_pe(a_o)
            scan_pe(rv[3], False)
            scan_pe(rv[4], False)
            scan_pe(rv[1], True)
            scan_pe(rv[2], False)
            scan_pe(rv[1], True)
            scan_pe(rv[2], False)
            to_cols_pe(rv[5])
            to_cols_pe(rv[6])

        def soft_act():
            act = nc.scalar
            act.wait_ge(sem("logits"), 1)
            for v in (rv[5], rv[6]):
                for b, (_, n) in enumerate(RB):
                    ins = act.activation(v[0:n, b], v[0:n, b], ACT.Exp)
            ins.then_inc(sem("exps"), 1)

        def norm1_dve():
            dve = nc.vector
            L = lambda ins: link(dve, "dve", ins)
            t = tmp[1][0:D]
            for k, st in enumerate((stN, stE)):
                for m in range(2):
                    L(dve.tensor_reduce(t[:, 2 * k + m:2 * k + m + 1], st[:, m], AX_X, ALU.add))
            norm_dve(1, t[:, 0:1], t[:, 1:2], N, G_N, BE_N, A_N, S_N)
            norm_dve(2, t[:, 2:3], t[:, 3:4], E, G_E, BE_E, A_E, S_E)
            L(dve.tensor_scalar(wt[:, 1, 0:D], ident[0:D, 0:D], col[:, A_E:A_E + 1], None, ALU.mult))
            L(dve.tensor_copy(wt[:, 1, D:D + 1], col[:, S_E:S_E + 1]))
            L(dve.tensor_scalar(wt[:, 0, 0:D], ident[0:D, 0:D], col[:, A_N:A_N + 1], None, ALU.mult))
            dve.tensor_copy(wt[:, 0, D:D + 1], col[:, S_N:S_N + 1]).then_inc(sem("norm1"), 1)
            dve.wait_ge(sem("norm1_pe"), 1)
            L(dve.tensor_copy(AN[:, 0:D], ps[0:D + 1, DB, 0:D]))
            L(dve.tensor_copy(WM3[D:D + 2], mb2[D:D + 2]))
            L(dve.tensor_tensor(WM3[0:D + 1], mb2[0:D + 1], ps[0:D + 1, DB + 1, 0:P], ALU.add))

        def norm1_pe():
            pe = nc.tensor
            pe.wait_ge(sem("norm1"), 1)
            pe.matmul(ps[0:D + 1, DB, 0:P], wt[:, 0, 0:D + 1], cent[:], start=True, stop=True)
            pe.matmul(ps[0:D + 1, DB + 1, 0:P], wt[:, 1, 0:D + 1], WM[:, 2], start=True, stop=True).then_inc(sem("norm1_pe"), 1)

        def norm2_dve():
            dve = nc.vector
            L = lambda ins: link(dve, "dve", ins)
            t = tmp[1][0:D]
            dve.wait_ge(sem("msum"), 1)
            L(dve.tensor_copy(t[:, 0:2], ps[0:D, DB, 0:2]))
            norm_dve(3, t[:, 0:1], t[:, 1:2], E, G_M, BE_M, A_M, S_M)
            L(dve.tensor_scalar(wt[:, 0, 0:D], ident[0:D, 0:D], col[:, A_M:A_M + 1], None, ALU.mult))
            L(dve.tensor_copy(wt[:, 0, D:D + 1], col[:, S_M:S_M + 1]))
            dve.tensor_copy(wt[:, 0, D + 1:D + 2], col[:, S_N:S_N + 1]).then_inc(sem("norm2"), 1)
            dve.wait_ge(sem("norm2_pe"), 1)
            L(dve.tensor_copy(AM[:, 0:D], ps[0:D + 2, DB + 1, 0:D]))
            L(dve.reciprocal(tmp[2][:], deg[:]))
            L(dve.tensor_copy(wE[:], tmp[2][:]))

        def norm2_pe():
            pe = nc.tensor
            for m in range(2):
                for t in range(TG):
                    ins = pe.matmul(ps[0:D, DB, m:m + 1], acc[:, m, t], ones[:, 0:1], start=(t == 0), stop=(t == TG - 1))
            ins.then_inc(sem("msum"), 1)
            pe.wait_ge(sem("norm2"), 1)
            pe.matmul(ps[0:D + 2, DB + 1, 0:P], wt[:, 0], cent[:], start=True, stop=True).then_inc(sem("norm2_pe"), 1)

        block = ctx.enter_context(nc.Block())

        @block.sync
        def _(sp):
            prepare_sp()
            barrier(sp, "sp")
            emlp_sp(PQ["emlp"])
            barrier(sp, "sp")
            active_sp()
            chain_sp_start(DQ["dense1"])
            tab_get_sp(PQ["tab_get"])
            copy_sp(PQ["copy"])
            chain_sp(DQ["dense1"], 3 * NI + 1)
            barrier(sp, "sp")
            chain_sp_start(DQ["source"])
            chain_sp(DQ["source"], 1)
            barrier(sp, "sp")
            chain_sp_start(DQ["dense2"])
            for name in ("conv1", "conv2", "conv3"):
                conv_sp(PQ[name])
                barrier(sp, "sp")
            att_sp(PQ["att"])
            chain_sp(DQ["dense2"], 3 * NI + 1)
            barrier(sp, "sp")
            barrier(sp, "sp")
            conv_sp(PQ["gat"])
            barrier(sp, "sp")
            mlp_sp(PQ["mlp"])
            barrier(sp, "sp")
            barrier(sp, "sp")
            msg_sp(PQ["msg"])
            barrier(sp, "sp")
            barrier(sp, "sp")
            join_sp(PQ["join"])
            barrier(sp, "sp")
            end_sp(DQ["source3"])
            barrier(sp, "sp")
            end_sp_start(DQ["final"])
            conv_sp(PQ["hop1"])
            end_sp(DQ["final"], 4 * NI)
            barrier(sp, "sp")
            conv_sp(PQ["hop2"])

        @block.gpsimd
        def _(pool):
            for name in list(PQ["hop2"]["base"]):
                if start_of(name):
                    pool.sem_inc(S(name), START)
            for name in list(DQ["final"]["base"]):
                pool.sem_inc(R(name), START)
            barrier(pool, "pool")
            tab_put_pool(PQ["tab_put"])
            barrier(pool, "pool")
            tab_get_pool(PQ["tab_get"])
            gather_pool(PQ["copy"], (ringG, ringS), (a["x"], a["x"]))
            barrier(pool, "pool")
            barrier(pool, "pool")
            barrier(pool, "pool")
            for name in ("conv2", "conv3"):
                gather_pool(PQ[name], (ringG,), (PQ[name]["table"],))
                barrier(pool, "pool")
            gather_pool(PQ["att"], (ringG,), (T[3],))
            for _ in range(5):
                barrier(pool, "pool")
            gather_pool(PQ["msg"], (ringG, ringS), (T[4], T[4]))
            for _ in range(4):
                barrier(pool, "pool")
            gather_pool(PQ["hop1"], (ringG,), (PQ["hop1"]["table"],))
            barrier(pool, "pool")
            hop2_pool(PQ["hop2"])

        @block.scalar
        def _(act):
            barrier(act, "act")
            emlp_act(PQ["emlp"])
            barrier(act, "act")
            chain_act_start(DQ["dense1"])
            copy_act(PQ["tab_get"])
            index_act()
            copy_act(PQ["copy"])
            chain_act(DQ["dense1"], 3 * NI + 1)
            barrier(act, "act")
            chain_act_start(DQ["source"])
            chain_act(DQ["source"], 1)
            barrier(act, "act")
            chain_act_start(DQ["dense2"])
            for name in ("conv1", "conv2", "conv3"):
                conv_act(PQ[name])
                barrier(act, "act")
            copy_act(PQ["att"])
            chain_act(DQ["dense2"], 3 * NI + 1)
            barrier(act, "act")
            soft_act()
            barrier(act, "act")
            conv_act(PQ["gat"])
            barrier(act, "act")
            mlp_act(PQ["mlp"])
            barrier(act, "act")
            norm_act(1)
            norm_act(2)
            barrier(act, "act")
            msg_act(PQ["msg"])
            barrier(act, "act")
            norm_act(3)
            barrier(act, "act")
            conv_act(PQ["join"])
            barrier(act, "act")
            end_act(DQ["source3"])
            barrier(act, "act")
            conv_act(PQ["hop1"])
            end_act(DQ["final"], 4 * NI)
            barrier(act, "act")
            conv_act(PQ["hop2"])

        @block.vector
        def _(dve):
            prepare_dve()
            barrier(dve, "dve_")
            tab_put_dve(PQ["tab_put"])
            barrier(dve, "dve_")
            stage(PQ["tab_get"], 0, 0)
            stage(PQ["tab_get"], 0, 1)
            active_dve()
            chain_dve_start(DQ["dense1"])
            tab_get_dve(PQ["tab_get"])
            index_dve()
            copy_dve(PQ["copy"])
            chain_dve(DQ["dense1"], 3 * NI + 1)
            barrier(dve, "dve_")
            chain_dve_start(DQ["source"])
            chain_dve(DQ["source"], 1)
            barrier(dve, "dve_")
            chain_dve_start(DQ["dense2"])
            for name in ("conv1", "conv2", "conv3"):
                conv_dve(PQ[name])
                barrier(dve, "dve_")
            att_dve(PQ["att"])
            chain_dve(DQ["dense2"], 3 * NI + 1)
            barrier(dve, "dve_")
            soft_dve()
            barrier(dve, "dve_")
            conv_dve(PQ["gat"])
            barrier(dve, "dve_")
            mlp_dve(PQ["mlp"])
            barrier(dve, "dve_")
            norm1_dve()
            barrier(dve, "dve_")
            msg_dve(PQ["msg"])
            barrier(dve, "dve_")
            norm2_dve()
            barrier(dve, "dve_")
            join_dve(PQ["join"])
            barrier(dve, "dve_")
            end_dve(DQ["source3"])
            barrier(dve, "dve_")
            conv_dve(PQ["hop1"])
            end_dve(DQ["final"], 4 * NI)
            barrier(dve, "dve_")
            conv_dve(PQ["hop2"])

        @block.tensor
        def _(pe):
            prepare_pe()
            barrier(pe, "pe")
            emlp_pe(PQ["emlp"])
            barrier(pe, "pe")
            chain_pe_start(DQ["dense1"])
            copy_pe(PQ["tab_get"])
            copy_pe(PQ["copy"])
            chain_pe(DQ["dense1"], 3 * NI + 1)
            barrier(pe, "pe")
            chain_pe_start(DQ["source"])
            chain_pe(DQ["source"], 1)
            barrier(pe, "pe")
            chain_pe_start(DQ["dense2"])
            for name in ("conv1", "conv2", "conv3"):
                conv_pe(PQ[name])
                barrier(pe, "pe")
            copy_pe(PQ["att"])
            chain_pe(DQ["dense2"], 3 * NI + 1)
            barrier(pe, "pe")
            soft_pe()
            barrier(pe, "pe")
            conv_pe(PQ["gat"])
            barrier(pe, "pe")
            mlp_pe(PQ["mlp"])
            barrier(pe, "pe")
            norm1_pe()
            barrier(pe, "pe")
            msg_pe(PQ["msg"])
            barrier(pe, "pe")
            norm2_pe()
            barrier(pe, "pe")
            join_pe(PQ["join"])
            barrier(pe, "pe")
            end_pe(DQ["source3"])
            barrier(pe, "pe")
            dense_pe_start(DQ["final"])
            conv_pe(PQ["hop1"])
            end_pe(DQ["final"], 4 * NI)
            barrier(pe, "pe")
            conv_pe(PQ["hop2"])


def kernel(**inputs):
    import numpy as np
    import concourse.bacc as bacc
    from concourse.bass_utils import run_bass_kernel_spmd

    arrays = {k: np.ascontiguousarray(v) for k, v in inputs.items() if k not in ("src", "dst", "edge_attr_4")}
    src, dst, attr = (np.asarray(inputs[k]) for k in ("src", "dst", "edge_attr_4"))
    pad = EP - E
    lines = np.concatenate([np.full(1, -1, dst.dtype), dst, np.full(pad, N, dst.dtype), np.full(1, -1, dst.dtype)])
    arrays["dst_line"] = lines
    arrays["dst_cols"] = np.ascontiguousarray(lines[1:1 + EP].reshape(ET, P).T)
    arrays["src_cols"] = np.ascontiguousarray(np.concatenate([src, np.zeros(pad, src.dtype)]).reshape(ET, P).T)
    auxe = np.zeros((2 + DE, EP), attr.dtype)
    auxe[0, :E] = 1
    auxe[1, E:] = 1
    auxe[2:, :E] = attr.T
    arrays["auxe"] = auxe
    eye = np.eye(P, dtype=np.float32)
    arrays["ident"] = eye
    arrays["eye_row"] = np.ascontiguousarray(np.eye(D + 1, D, dtype=np.float32))
    arrays["cent"] = np.zeros((D, P), np.float32)
    arrays["cent"][:, :D] = np.eye(D) - 1.0 / D
    arrays["xT"] = np.ascontiguousarray(arrays["x"].T)
    slots = np.arange(EP, dtype=np.float32)
    arrays["own_cols"] = np.ascontiguousarray(slots.reshape(ET, P).T)
    own_rows = np.zeros((P, 2, P), np.float32)
    own_rows[:, 0] = slots.reshape(ET, P)[:P]
    own_rows[:ET - P, 1] = slots.reshape(ET, P)[P:]
    arrays["own_rows"] = own_rows
    nc = bacc.Bacc("TRN2", target_bir_lowering=False, num_devices=1)
    args = {}
    feed = {}
    for name, v in arrays.items():
        feed[f"in_{name}"] = v
        args[name] = nc.dram_tensor(f"in_{name}", v.shape, mybir.dt.from_np(v.dtype), kind="ExternalInput").ap()
    args["out"] = nc.dram_tensor("out_x", (N, D), F32, kind="ExternalOutput").ap()
    build(nc, args)
    r = run_bass_kernel_spmd(nc, [feed], core_ids=[0])
    return r.results[0]["out_x"]
```
